# Optimizing a Trainium2 kernel written in Bass

```python
import numpy as np
import jax
import jax.numpy as jnp

def _softmax(x, axis=-1):
    return jax.nn.softmax(x, axis=axis)

def _gelu(x):
    return jax.nn.gelu(x, approximate=True)

def _silu(x):
    return jax.nn.silu(x)

def _sigmoid(x):
    return jax.nn.sigmoid(x)

def _layernorm(x, axis=-1, eps=1e-05):
    m = jnp.mean(x, axis=axis, keepdims=True)
    v = jnp.var(x, axis=axis, keepdims=True)
    return (x - m) / jnp.sqrt(v + eps)

def _scatter_add(tgt, idx, src, axis=0):
    return tgt.at[idx].add(src)

def _segment_sum(src, seg, n):
    return jax.ops.segment_sum(src, seg, n)
kernel_name = 'mk_flamingo_gated_d4_seqx_r8_c29ca9'

def setup_inputs(seed: int=0):
    np.random.seed(seed)
    _w = jnp.asarray

    def _rec_inputs():
        import jax
        import jax.numpy as jnp
        _rk = jax.random.key(seed)
        x = 7.22e-05 + 1 * jax.random.normal(jax.random.fold_in(_rk, 1), (16, 56, 256), jnp.float32)
        _lenS = 56 - jax.random.randint(jax.random.fold_in(_rk, 7), (16,), 0, max(1, 56 // 4) + 1, jnp.int32)
        _lenS2 = 1500 - jax.random.randint(jax.random.fold_in(_rk, 8), (16,), 0, max(1, 1500 // 4) + 1, jnp.int32)
        _ctx_512P = jax.random.normal(jax.random.fold_in(_rk, 11), (16, 16, 64), jnp.float32)
        _ctx_512c = jax.random.dirichlet(jax.random.fold_in(_rk, 511), 0.3 * jnp.ones((16,), jnp.float32), (16, 1500))
        _ctx_512t = jnp.einsum('bsk,bkd->bsd', _ctx_512c, _ctx_512P)
        _ctx_512t = _ctx_512t * jax.lax.rsqrt(jnp.mean(jnp.square(_ctx_512t)) + 1e-12) * 0.953939
        ctx_512 = -0.000514642 + 1.00011 * (_ctx_512t + 0.3 * jax.random.normal(jax.random.fold_in(_rk, 611), (16, 1500, 64), jnp.float32))
        _g = jax.random.normal(jax.random.fold_in(_rk, 9001), (2, 4), jnp.float32)
        _g = jnp.sign(_g) * jnp.maximum(jnp.abs(_g), 1.0) + (_g == 0) * 1.0
        g_xattn = _g[0]
        g_ffn = _g[1]
        return (x, ctx_512, g_xattn, g_ffn)
    x, ctx_512, g_xattn, g_ffn = _rec_inputs()

    def _L0_xattn_setup():
        import jax, jax.numpy as jnp
        import numpy as np
        B, S, H, NH, L = (2, 256, 256, 16, 64)
        HD = H // NH
        key = jax.random.key(seed)
        k1, k2, k3, k4, k5 = jax.random.split(key, 5)
        scale = 0.02
        return {'q': jax.random.normal(k1, (B, S, H), dtype=jnp.float32), 'latent_kv': jax.random.normal(k2, (B, S, L), dtype=jnp.float32), 'Wq': jax.random.normal(k3, (H, H), dtype=jnp.float32) * scale, 'Wkv_expand': jax.random.normal(k4, (2 * H, L), dtype=jnp.float32) * scale, 'Wout': jax.random.normal(k5, (H, H), dtype=jnp.float32) * scale}
    _L0_xattn_all = _L0_xattn_setup()
    _L0_xattn_in = {k: v for k, v in _L0_xattn_all.items() if k in ('Wq', 'Wkv_expand', 'Wout')}
    del _L0_xattn_all

    def _L0_ffn_setup():
        import jax, jax.numpy as jnp
        import numpy as np
        HIDDEN = 256
        EXPERT_FF = 176
        NUM_EXPERTS = 16
        NUM_SHARED = 2
        SHARED_FF = EXPERT_FF * NUM_SHARED
        TOP_K = 4
        SCALE = 1.0
        BATCH, SEQ = (1, 256)

        def _moe_forward(hidden_states, Wg, W1, W2, W3, W1s, W2s, W3s):
            B, S, D = hidden_states.shape
            x = hidden_states.reshape(-1, D)
            T = x.shape[0]
            E = Wg.shape[0]
            shared = jax.nn.silu(x @ W1s.T) * (x @ W3s.T) @ W2s.T
            logits = x @ Wg.T
            probs = jax.nn.softmax(logits.astype(jnp.float32), axis=-1)
            topk_w, sel = jax.lax.top_k(probs, TOP_K)
            topk_w = topk_w.astype(x.dtype) * SCALE
            combine = jnp.zeros((T, E), x.dtype).at[jnp.arange(T)[:, None], sel].add(topk_w)
            h = jax.nn.silu(jnp.einsum('td,efd->etf', x, W1)) * jnp.einsum('td,efd->etf', x, W3)
            routed = jnp.einsum('etf,edf->td', h * combine.T[:, :, None], W2)
            return (shared + routed).reshape(B, S, D)
        key = jax.random.key(seed)
        ks = jax.random.split(key, 8)
        std = 0.02
        return {'hidden_states': jax.random.normal(ks[0], (BATCH, SEQ, HIDDEN), dtype=jnp.float32), 'Wg': jax.random.normal(ks[1], (NUM_EXPERTS, HIDDEN), dtype=jnp.float32) * std, 'W1': jax.random.normal(ks[2], (NUM_EXPERTS, EXPERT_FF, HIDDEN), dtype=jnp.float32) * std, 'W2': jax.random.normal(ks[3], (NUM_EXPERTS, HIDDEN, EXPERT_FF), dtype=jnp.float32) * std, 'W3': jax.random.normal(ks[4], (NUM_EXPERTS, EXPERT_FF, HIDDEN), dtype=jnp.float32) * std, 'W1s': jax.random.normal(ks[5], (SHARED_FF, HIDDEN), dtype=jnp.float32) * std, 'W2s': jax.random.normal(ks[6], (HIDDEN, SHARED_FF), dtype=jnp.float32) * std, 'W3s': jax.random.normal(ks[7], (SHARED_FF, HIDDEN), dtype=jnp.float32) * std}
    _L0_ffn_all = _L0_ffn_setup()
    _L0_ffn_in = {k: v for k, v in _L0_ffn_all.items() if k in ('Wg', 'W1', 'W2', 'W3', 'W1s', 'W2s', 'W3s')}
    del _L0_ffn_all

    def _L1_xattn_setup():
        import jax, jax.numpy as jnp
        import numpy as np
        B, S, L = (2, 128, 128)
        DIM_Q, H, K, D_C, D_CQ, R = (256, 16, 128, 64, 192, 64)

        def _rope_tables(seq_len, dim, dtype):
            inv_freq = 1.0 / 10000.0 ** (jnp.arange(0, dim, 2, dtype=dtype) / dim)
            t = jnp.arange(seq_len, dtype=dtype)
            freqs = t[:, None] * inv_freq[None, :]
            sin = jnp.repeat(jnp.sin(freqs), 2, axis=-1)
            cos = jnp.repeat(jnp.cos(freqs), 2, axis=-1)
            return (sin, cos)

        def _rotate_half(x):
            h = x.shape[-1] // 2
            return jnp.concatenate([-x[..., h:], x[..., :h]], axis=-1)
        key = jax.random.key(seed)
        ks = jax.random.split(key, 8)
        s_in = 1.0 / np.sqrt(DIM_Q)
        s_k = 1.0 / np.sqrt(K)
        s_cq = 1.0 / np.sqrt(D_CQ)
        s_c = 1.0 / np.sqrt(D_C)
        return {'hidden_q': jax.random.normal(ks[0], (B, S, DIM_Q), jnp.float32), 'kv_c': jax.random.normal(ks[1], (B, L, D_C), jnp.float32), 'Wq': jax.random.normal(ks[2], (H * K, DIM_Q), jnp.float32) * s_in, 'w_kc_q': jax.random.normal(ks[3], (H, K, D_CQ), jnp.float32) * s_k, 'w_kc_kv': jax.random.normal(ks[4], (H, K, D_C), jnp.float32) * s_k, 'W_qr': jax.random.normal(ks[5], (H, D_CQ, R), jnp.float32) * s_cq / np.sqrt(R), 'W_kr': jax.random.normal(ks[6], (H, D_C, R), jnp.float32) * s_c, 'Wo': jax.random.normal(ks[7], (DIM_Q, H * K), jnp.float32) * s_k}
    _L1_xattn_all = _L1_xattn_setup()
    _L1_xattn_in = {k: v for k, v in _L1_xattn_all.items() if k in ('Wq', 'w_kc_q', 'w_kc_kv', 'W_qr', 'W_kr', 'Wo')}
    del _L1_xattn_all

    def _L1_ffn_setup():
        import jax, jax.numpy as jnp
        import numpy as np
        _FP8_DTYPE = jnp.float8_e4m3fn
        _FP8_MAX = 448.0
        key = jax.random.key(seed)
        k_x, k_w = jax.random.split(key)
        B, S, IN, OUT = (2, 1024, 256, 256)
        x = jax.random.normal(k_x, (B, S, IN), dtype=jnp.float32)
        w_f32 = jax.random.normal(k_w, (OUT, IN), dtype=jnp.float32) * 0.02
        weight = w_f32.astype(_FP8_DTYPE)
        weight_scale = jnp.asarray(1.5, dtype=jnp.float32)
        input_scale = jnp.asarray(0.75, dtype=jnp.bfloat16)
        return {'x': x, 'weight': weight, 'weight_scale': weight_scale, 'input_scale': input_scale}
    _L1_ffn_all = _L1_ffn_setup()
    _L1_ffn_in = {k: v for k, v in _L1_ffn_all.items() if k in ('weight', 'weight_scale', 'input_scale')}
    del _L1_ffn_all

    def _L2_xattn_setup():
        import jax, jax.numpy as jnp
        import numpy as np
        B, S, L = (2, 128, 128)
        DIM_Q, H, K, D_C, D_CQ, R = (256, 16, 128, 64, 192, 64)

        def _rope_tables(length, dim):
            inv = 1.0 / 10000.0 ** (jnp.arange(0, dim, 2, dtype=jnp.float32) / dim)
            f = jnp.arange(length, dtype=jnp.float32)[:, None] * inv[None, :]
            sin = jnp.repeat(jnp.sin(f), 2, axis=-1)
            cos = jnp.repeat(jnp.cos(f), 2, axis=-1)
            return (sin, cos)

        def _rotate_half(x):
            half = x.shape[-1] // 2
            return jnp.concatenate([-x[..., half:], x[..., :half]], axis=-1)

        def _apply_rope(x, sin, cos):
            return x * cos + _rotate_half(x) * sin
        key = jax.random.key(seed)
        ks = jax.random.split(key, 8)
        return {'hidden_q': jax.random.normal(ks[0], (B, S, DIM_Q), jnp.float32), 'kv_c': jax.random.normal(ks[1], (B, L, D_C), jnp.float32), 'Wq': jax.random.normal(ks[2], (H * K, DIM_Q), jnp.float32) / np.sqrt(DIM_Q).astype(np.float32), 'w_kc_q': jax.random.normal(ks[3], (H, K, D_CQ), jnp.float32) / np.sqrt(K).astype(np.float32), 'w_kc_kv': jax.random.normal(ks[4], (H, K, D_C), jnp.float32) / np.sqrt(K).astype(np.float32), 'W_qr': jax.random.normal(ks[5], (H, D_CQ, R), jnp.float32) / np.float32(np.sqrt(D_CQ) * np.sqrt(R)), 'W_kr': jax.random.normal(ks[6], (H, D_C, R), jnp.float32) / np.sqrt(D_C).astype(np.float32), 'Wo': jax.random.normal(ks[7], (DIM_Q, H * K), jnp.float32) / np.sqrt(H * K).astype(np.float32)}
    _L2_xattn_all = _L2_xattn_setup()
    _L2_xattn_in = {k: v for k, v in _L2_xattn_all.items() if k in ('Wq', 'w_kc_q', 'w_kc_kv', 'W_qr', 'W_kr', 'Wo')}
    del _L2_xattn_all

    def _L2_ffn_setup():
        import jax, jax.numpy as jnp
        import numpy as np
        H, I, E = (256, 512, 8)
        B, S = (2, 256)
        key = jax.random.key(seed)
        ks = jax.random.split(key, 5)
        scale = 0.02
        return {'hidden_states': jax.random.normal(ks[0], (B, S, H), dtype=jnp.float32), 'router_w': jax.random.normal(ks[1], (H, E), dtype=jnp.float32) * scale, 'gate_w': jax.random.normal(ks[2], (E, H, I), dtype=jnp.float32) * scale, 'up_w': jax.random.normal(ks[3], (E, H, I), dtype=jnp.float32) * scale, 'down_w': jax.random.normal(ks[4], (E, I, H), dtype=jnp.float32) * scale}
    _L2_ffn_all = _L2_ffn_setup()
    _L2_ffn_in = {k: v for k, v in _L2_ffn_all.items() if k in ('router_w', 'gate_w', 'up_w', 'down_w')}
    del _L2_ffn_all

    def _L3_xattn_setup():
        import jax, jax.numpy as jnp
        import numpy as np
        B, S, L = (2, 128, 128)
        DIM_Q, H, K, D_C, D_CQ, R = (256, 16, 128, 64, 192, 64)

        def _rope_tables(seq_len, dim, dtype):
            inv_freq = 1.0 / 10000.0 ** (jnp.arange(0, dim, 2, dtype=dtype) / dim)
            t = jnp.arange(seq_len, dtype=dtype)
            freqs = t[:, None] * inv_freq[None, :]
            sin = jnp.repeat(jnp.sin(freqs), 2, axis=-1)
            cos = jnp.repeat(jnp.cos(freqs), 2, axis=-1)
            return (sin, cos)

        def _rotate_half(x):
            h = x.shape[-1] // 2
            return jnp.concatenate([-x[..., h:], x[..., :h]], axis=-1)
        key = jax.random.key(seed)
        ks = jax.random.split(key, 8)
        s_in = 1.0 / np.sqrt(DIM_Q)
        s_k = 1.0 / np.sqrt(K)
        s_cq = 1.0 / np.sqrt(D_CQ)
        s_c = 1.0 / np.sqrt(D_C)
        return {'hidden_q': jax.random.normal(ks[0], (B, S, DIM_Q), jnp.float32), 'kv_c': jax.random.normal(ks[1], (B, L, D_C), jnp.float32), 'Wq': jax.random.normal(ks[2], (H * K, DIM_Q), jnp.float32) * s_in, 'w_kc_q': jax.random.normal(ks[3], (H, K, D_CQ), jnp.float32) * s_k, 'w_kc_kv': jax.random.normal(ks[4], (H, K, D_C), jnp.float32) * s_k, 'W_qr': jax.random.normal(ks[5], (H, D_CQ, R), jnp.float32) * s_cq / np.sqrt(R), 'W_kr': jax.random.normal(ks[6], (H, D_C, R), jnp.float32) * s_c, 'Wo': jax.random.normal(ks[7], (DIM_Q, H * K), jnp.float32) * s_k}
    _L3_xattn_all = _L3_xattn_setup()
    _L3_xattn_in = {k: v for k, v in _L3_xattn_all.items() if k in ('Wq', 'w_kc_q', 'w_kc_kv', 'W_qr', 'W_kr', 'Wo')}
    del _L3_xattn_all

    def _L3_ffn_setup():
        import jax, jax.numpy as jnp
        import numpy as np
        TOP_K = 4
        NUM_EXPERTS = 16
        key = jax.random.key(seed)
        ks = jax.random.split(key, 6)
        B, S, H, I, E = (2, 128, 256, 224, NUM_EXPERTS)
        return {'x': jax.random.normal(ks[0], (B, S, H), dtype=jnp.float32), 'router_w': jax.random.normal(ks[1], (E, H), dtype=jnp.float32) * 0.02, 'expert_bias': jnp.zeros((E,), dtype=jnp.float32), 'gate_proj': jax.random.normal(ks[2], (E, H, I), dtype=jnp.float32) * 0.02, 'up_proj': jax.random.normal(ks[3], (E, H, I), dtype=jnp.float32) * 0.02, 'down_proj': jax.random.normal(ks[4], (E, I, H), dtype=jnp.float32) * 0.02}
    _L3_ffn_all = _L3_ffn_setup()
    _L3_ffn_in = {k: v for k, v in _L3_ffn_all.items() if k in ('router_w', 'expert_bias', 'gate_proj', 'up_proj', 'down_proj')}
    del _L3_ffn_all
    return {'x': x, 'ctx_512': ctx_512, 'g_xattn': g_xattn, 'g_ffn': g_ffn, 'L0_xattn_Wq': _L0_xattn_in['Wq'], 'L0_xattn_Wkv_expand': _L0_xattn_in['Wkv_expand'], 'L0_xattn_Wout': _L0_xattn_in['Wout'], 'L0_ffn_Wg': _L0_ffn_in['Wg'], 'L0_ffn_W1': _L0_ffn_in['W1'], 'L0_ffn_W2': _L0_ffn_in['W2'], 'L0_ffn_W3': _L0_ffn_in['W3'], 'L0_ffn_W1s': _L0_ffn_in['W1s'], 'L0_ffn_W2s': _L0_ffn_in['W2s'], 'L0_ffn_W3s': _L0_ffn_in['W3s'], 'L1_xattn_Wq': _L1_xattn_in['Wq'], 'L1_xattn_w_kc_q': _L1_xattn_in['w_kc_q'], 'L1_xattn_w_kc_kv': _L1_xattn_in['w_kc_kv'], 'L1_xattn_W_qr': _L1_xattn_in['W_qr'], 'L1_xattn_W_kr': _L1_xattn_in['W_kr'], 'L1_xattn_Wo': _L1_xattn_in['Wo'], 'L1_ffn_weight': _L1_ffn_in['weight'], 'L1_ffn_weight_scale': _L1_ffn_in['weight_scale'], 'L1_ffn_input_scale': _L1_ffn_in['input_scale'], 'L2_xattn_Wq': _L2_xattn_in['Wq'], 'L2_xattn_w_kc_q': _L2_xattn_in['w_kc_q'], 'L2_xattn_w_kc_kv': _L2_xattn_in['w_kc_kv'], 'L2_xattn_W_qr': _L2_xattn_in['W_qr'], 'L2_xattn_W_kr': _L2_xattn_in['W_kr'], 'L2_xattn_Wo': _L2_xattn_in['Wo'], 'L2_ffn_router_w': _L2_ffn_in['router_w'], 'L2_ffn_gate_w': _L2_ffn_in['gate_w'], 'L2_ffn_up_w': _L2_ffn_in['up_w'], 'L2_ffn_down_w': _L2_ffn_in['down_w'], 'L3_xattn_Wq': _L3_xattn_in['Wq'], 'L3_xattn_w_kc_q': _L3_xattn_in['w_kc_q'], 'L3_xattn_w_kc_kv': _L3_xattn_in['w_kc_kv'], 'L3_xattn_W_qr': _L3_xattn_in['W_qr'], 'L3_xattn_W_kr': _L3_xattn_in['W_kr'], 'L3_xattn_Wo': _L3_xattn_in['Wo'], 'L3_ffn_router_w': _L3_ffn_in['router_w'], 'L3_ffn_expert_bias': _L3_ffn_in['expert_bias'], 'L3_ffn_gate_proj': _L3_ffn_in['gate_proj'], 'L3_ffn_up_proj': _L3_ffn_in['up_proj'], 'L3_ffn_down_proj': _L3_ffn_in['down_proj']}

def reference(x, ctx_512, g_xattn, g_ffn, L0_xattn_Wq, L0_xattn_Wkv_expand, L0_xattn_Wout, L0_ffn_Wg, L0_ffn_W1, L0_ffn_W2, L0_ffn_W3, L0_ffn_W1s, L0_ffn_W2s, L0_ffn_W3s, L1_xattn_Wq, L1_xattn_w_kc_q, L1_xattn_w_kc_kv, L1_xattn_W_qr, L1_xattn_W_kr, L1_xattn_Wo, L1_ffn_weight, L1_ffn_weight_scale, L1_ffn_input_scale, L2_xattn_Wq, L2_xattn_w_kc_q, L2_xattn_w_kc_kv, L2_xattn_W_qr, L2_xattn_W_kr, L2_xattn_Wo, L2_ffn_router_w, L2_ffn_gate_w, L2_ffn_up_w, L2_ffn_down_w, L3_xattn_Wq, L3_xattn_w_kc_q, L3_xattn_w_kc_kv, L3_xattn_W_qr, L3_xattn_W_kr, L3_xattn_Wo, L3_ffn_router_w, L3_ffn_expert_bias, L3_ffn_gate_proj, L3_ffn_up_proj, L3_ffn_down_proj):
    import jax
    import jax.numpy as jnp

    def _L0_xattn_ref(q, latent_kv, Wq, Wkv_expand, Wout):
        import jax, jax.numpy as jnp
        import numpy as np
        B, S, H, NH, L = (2, 256, 256, 16, 64)
        HD = H // NH
        b, sq, _ = q.shape
        sk = latent_kv.shape[1]
        qp = q @ Wq.T
        kv = latent_kv @ Wkv_expand.T
        k, v = jnp.split(kv, 2, axis=-1)
        qh = qp.reshape(b, sq, NH, HD).transpose(0, 2, 1, 3)
        kh = k.reshape(b, sk, NH, HD).transpose(0, 2, 1, 3)
        vh = v.reshape(b, sk, NH, HD).transpose(0, 2, 1, 3)
        inv_sqrt_d = 1.0 / jnp.sqrt(jnp.float32(HD))
        scores = jnp.einsum('bhqd,bhkd->bhqk', qh, kh) * inv_sqrt_d
        causal = jnp.tril(jnp.ones((sq, sk), dtype=bool))
        scores = jnp.where(causal, scores, jnp.finfo(scores.dtype).min)
        attn = jax.nn.softmax(scores, axis=-1)
        out = jnp.einsum('bhqk,bhkd->bhqd', attn, vh)
        out = out.transpose(0, 2, 1, 3).reshape(b, sq, H)
        return out @ Wout.T

    def _L0_ffn_ref(hidden_states, Wg, W1, W2, W3, W1s, W2s, W3s):
        import jax, jax.numpy as jnp
        import numpy as np
        HIDDEN = 256
        EXPERT_FF = 176
        NUM_EXPERTS = 16
        NUM_SHARED = 2
        SHARED_FF = EXPERT_FF * NUM_SHARED
        TOP_K = 4
        SCALE = 1.0
        BATCH, SEQ = (1, 256)

        def _moe_forward(hidden_states, Wg, W1, W2, W3, W1s, W2s, W3s):
            B, S, D = hidden_states.shape
            x = hidden_states.reshape(-1, D)
            T = x.shape[0]
            E = Wg.shape[0]
            shared = jax.nn.silu(x @ W1s.T) * (x @ W3s.T) @ W2s.T
            logits = x @ Wg.T
            probs = jax.nn.softmax(logits.astype(jnp.float32), axis=-1)
            topk_w, sel = jax.lax.top_k(probs, TOP_K)
            topk_w = topk_w.astype(x.dtype) * SCALE
            combine = jnp.zeros((T, E), x.dtype).at[jnp.arange(T)[:, None], sel].add(topk_w)
            h = jax.nn.silu(jnp.einsum('td,efd->etf', x, W1)) * jnp.einsum('td,efd->etf', x, W3)
            routed = jnp.einsum('etf,edf->td', h * combine.T[:, :, None], W2)
            return (shared + routed).reshape(B, S, D)
        return _moe_forward(hidden_states, Wg, W1, W2, W3, W1s, W2s, W3s)

    def _L1_xattn_ref(hidden_q, kv_c, Wq, w_kc_q, w_kc_kv, W_qr, W_kr, Wo):
        import jax, jax.numpy as jnp
        import numpy as np
        B, S, L = (2, 128, 128)
        DIM_Q, H, K, D_C, D_CQ, R = (256, 16, 128, 64, 192, 64)

        def _rope_tables(seq_len, dim, dtype):
            inv_freq = 1.0 / 10000.0 ** (jnp.arange(0, dim, 2, dtype=dtype) / dim)
            t = jnp.arange(seq_len, dtype=dtype)
            freqs = t[:, None] * inv_freq[None, :]
            sin = jnp.repeat(jnp.sin(freqs), 2, axis=-1)
            cos = jnp.repeat(jnp.cos(freqs), 2, axis=-1)
            return (sin, cos)

        def _rotate_half(x):
            h = x.shape[-1] // 2
            return jnp.concatenate([-x[..., h:], x[..., :h]], axis=-1)
        b, s, _ = hidden_q.shape
        l = kv_c.shape[1]
        q_hk = (hidden_q @ Wq.T).reshape(b, s, H, K)
        q_big = jnp.einsum('bshk,hkq->bshq', q_hk, w_kc_q)
        sin, cos = _rope_tables(l, D_C, kv_c.dtype)
        kv_rope = kv_c * cos[None] + _rotate_half(kv_c) * sin[None]
        q_r = jnp.einsum('bshq,hqr->bhsr', q_big, W_qr)
        k_r = jnp.einsum('bld,hdr->bhlr', kv_rope, W_kr)
        scores = jnp.einsum('bhsr,bhlr->bhsl', q_r, k_r)
        attn = jax.nn.softmax(scores, axis=-1)
        ctx_c = jnp.einsum('bhsl,bld->bhsd', attn, kv_rope)
        ctx_lat = jnp.einsum('bhsd,hkd->bshk', ctx_c, w_kc_kv)
        out = ctx_lat.reshape(b, s, H * K) @ Wo.T
        return out

    def _L1_ffn_ref(x, weight, weight_scale, input_scale):
        import jax, jax.numpy as jnp
        import numpy as np
        _FP8_DTYPE = jnp.float8_e4m3fn
        _FP8_MAX = 448.0
        orig_dtype = x.dtype
        w = weight.astype(orig_dtype) * weight_scale.astype(orig_dtype)
        s_f32 = input_scale.astype(jnp.float32)
        x_scaled = x.astype(jnp.float32) / s_f32
        x_fp8 = jnp.clip(x_scaled, -_FP8_MAX, _FP8_MAX).astype(_FP8_DTYPE)
        x_qdq = x_fp8.astype(orig_dtype) * s_f32.astype(orig_dtype)
        return jnp.einsum('bsi,oi->bso', x_qdq, w)

    def _L2_xattn_ref(hidden_q, kv_c, Wq, w_kc_q, w_kc_kv, W_qr, W_kr, Wo):
        import jax, jax.numpy as jnp
        import numpy as np
        B, S, L = (2, 128, 128)
        DIM_Q, H, K, D_C, D_CQ, R = (256, 16, 128, 64, 192, 64)

        def _rope_tables(length, dim):
            inv = 1.0 / 10000.0 ** (jnp.arange(0, dim, 2, dtype=jnp.float32) / dim)
            f = jnp.arange(length, dtype=jnp.float32)[:, None] * inv[None, :]
            sin = jnp.repeat(jnp.sin(f), 2, axis=-1)
            cos = jnp.repeat(jnp.cos(f), 2, axis=-1)
            return (sin, cos)

        def _rotate_half(x):
            half = x.shape[-1] // 2
            return jnp.concatenate([-x[..., half:], x[..., :half]], axis=-1)

        def _apply_rope(x, sin, cos):
            return x * cos + _rotate_half(x) * sin
        Bv, Sv, _ = hidden_q.shape
        _, Lv, _ = kv_c.shape
        q_hk = (hidden_q @ Wq.T).reshape(Bv, Sv, H, K)
        q_big = jnp.einsum('bshk,hkq->bshq', q_hk, w_kc_q)
        sin_q, cos_q = _rope_tables(Sv, D_CQ)
        q_big = _apply_rope(q_big, sin_q[None, :, None, :], cos_q[None, :, None, :])
        sin_k, cos_k = _rope_tables(Lv, D_C)
        kv_r = _apply_rope(kv_c, sin_k[None], cos_k[None])
        q_r = jnp.einsum('bshq,hqr->bhsr', q_big, W_qr)
        k_r = jnp.einsum('bld,hdr->bhlr', kv_r, W_kr)
        scores = jnp.einsum('bhsr,bhlr->bhsl', q_r, k_r)
        attn = jax.nn.softmax(scores, axis=-1)
        ctx_c = jnp.einsum('bhsl,bld->bhsd', attn, kv_r)
        ctx_lat = jnp.einsum('bhsd,hkd->bhsk', ctx_c, w_kc_kv)
        ctx = ctx_lat.transpose(0, 2, 1, 3).reshape(Bv, Sv, H * K)
        return ctx @ Wo.T

    def _L2_ffn_ref(hidden_states, router_w, gate_w, up_w, down_w):
        import jax, jax.numpy as jnp
        import numpy as np
        H, I, E = (256, 512, 8)
        B, S = (2, 256)
        hidden_shape = hidden_states.shape
        x = hidden_states.reshape(-1, hidden_shape[-1])
        route = jax.nn.sigmoid(x @ router_w)
        max_ind = jnp.argmax(route, axis=1)
        max_prob = jnp.take_along_axis(route, max_ind[:, None], axis=1)
        out = jnp.zeros_like(x)
        num_experts = gate_w.shape[0]
        for e in range(num_experts):
            mask = (max_ind == e)[:, None]
            h = jax.nn.silu(x @ gate_w[e]) * (x @ up_w[e])
            out = out + jnp.where(mask, h @ down_w[e], 0.0)
        out = out * max_prob
        return out.reshape(hidden_shape)

    def _L3_xattn_ref(hidden_q, kv_c, Wq, w_kc_q, w_kc_kv, W_qr, W_kr, Wo):
        import jax, jax.numpy as jnp
        import numpy as np
        B, S, L = (2, 128, 128)
        DIM_Q, H, K, D_C, D_CQ, R = (256, 16, 128, 64, 192, 64)

        def _rope_tables(seq_len, dim, dtype):
            inv_freq = 1.0 / 10000.0 ** (jnp.arange(0, dim, 2, dtype=dtype) / dim)
            t = jnp.arange(seq_len, dtype=dtype)
            freqs = t[:, None] * inv_freq[None, :]
            sin = jnp.repeat(jnp.sin(freqs), 2, axis=-1)
            cos = jnp.repeat(jnp.cos(freqs), 2, axis=-1)
            return (sin, cos)

        def _rotate_half(x):
            h = x.shape[-1] // 2
            return jnp.concatenate([-x[..., h:], x[..., :h]], axis=-1)
        b, s, _ = hidden_q.shape
        l = kv_c.shape[1]
        q_hk = (hidden_q @ Wq.T).reshape(b, s, H, K)
        q_big = jnp.einsum('bshk,hkq->bshq', q_hk, w_kc_q)
        sin, cos = _rope_tables(l, D_C, kv_c.dtype)
        kv_rope = kv_c * cos[None] + _rotate_half(kv_c) * sin[None]
        q_r = jnp.einsum('bshq,hqr->bhsr', q_big, W_qr)
        k_r = jnp.einsum('bld,hdr->bhlr', kv_rope, W_kr)
        scores = jnp.einsum('bhsr,bhlr->bhsl', q_r, k_r)
        attn = jax.nn.softmax(scores, axis=-1)
        ctx_c = jnp.einsum('bhsl,bld->bhsd', attn, kv_rope)
        ctx_lat = jnp.einsum('bhsd,hkd->bshk', ctx_c, w_kc_kv)
        out = ctx_lat.reshape(b, s, H * K) @ Wo.T
        return out

    def _L3_ffn_ref(x, router_w, expert_bias, gate_proj, up_proj, down_proj):
        import jax, jax.numpy as jnp
        import numpy as np
        TOP_K = 4
        NUM_EXPERTS = 16
        logits = jnp.einsum('bsh,eh->bse', x, router_w) + expert_bias
        scores = jax.nn.softmax(logits, axis=-1)
        top_w, top_idx = jax.lax.top_k(scores, TOP_K)
        top_w = top_w / jnp.sum(top_w, axis=-1, keepdims=True)
        g = jnp.einsum('bsh,khe->bske', x, gate_proj)
        u = jnp.einsum('bsh,khe->bske', x, up_proj)
        act = jax.nn.silu(g) * u
        out = jnp.einsum('bske,keh->bskh', act, down_proj)
        sel = jnp.take_along_axis(out, top_idx[..., None], axis=2)
        return jnp.sum(sel * top_w[..., None], axis=2)
    x = x + jnp.tanh(g_xattn[0]) * _L0_xattn_ref(_layernorm(x, axis=-1), ctx_512, L0_xattn_Wq, L0_xattn_Wkv_expand, L0_xattn_Wout)
    x = x + jnp.tanh(g_ffn[0]) * _L0_ffn_ref(_layernorm(x, axis=-1), L0_ffn_Wg, L0_ffn_W1, L0_ffn_W2, L0_ffn_W3, L0_ffn_W1s, L0_ffn_W2s, L0_ffn_W3s)
    x = x + jnp.tanh(g_xattn[1]) * _L1_xattn_ref(_layernorm(x, axis=-1), ctx_512, L1_xattn_Wq, L1_xattn_w_kc_q, L1_xattn_w_kc_kv, L1_xattn_W_qr, L1_xattn_W_kr, L1_xattn_Wo)
    x = x + jnp.tanh(g_ffn[1]) * _L1_ffn_ref(_layernorm(x, axis=-1), L1_ffn_weight, L1_ffn_weight_scale, L1_ffn_input_scale)
    x = x + jnp.tanh(g_xattn[2]) * _L2_xattn_ref(_layernorm(x, axis=-1), ctx_512, L2_xattn_Wq, L2_xattn_w_kc_q, L2_xattn_w_kc_kv, L2_xattn_W_qr, L2_xattn_W_kr, L2_xattn_Wo)
    x = x + jnp.tanh(g_ffn[2]) * _L2_ffn_ref(_layernorm(x, axis=-1), L2_ffn_router_w, L2_ffn_gate_w, L2_ffn_up_w, L2_ffn_down_w)
    x = x + jnp.tanh(g_xattn[3]) * _L3_xattn_ref(_layernorm(x, axis=-1), ctx_512, L3_xattn_Wq, L3_xattn_w_kc_q, L3_xattn_w_kc_kv, L3_xattn_W_qr, L3_xattn_W_kr, L3_xattn_Wo)
    x = x + jnp.tanh(g_ffn[3]) * _L3_ffn_ref(_layernorm(x, axis=-1), L3_ffn_router_w, L3_ffn_expert_bias, L3_ffn_gate_proj, L3_ffn_up_proj, L3_ffn_down_proj)
    return x

_drawn_inputs = setup_inputs


def setup_inputs(seed=0):
    import zlib

    import numpy as np

    out = dict(_drawn_inputs(seed))
    spreads = {'L3_ffn_expert_bias': (0.0, 0.8)}
    factors = {'g_ffn': 45.264,
     'L0_xattn_Wq': 8.0,
     'L0_xattn_Wkv_expand': 3.755,
     'L0_xattn_Wout': 3.795,
     'L0_ffn_Wg': 8.0,
     'L0_ffn_W1': 8.0,
     'L0_ffn_W2': 8.0,
     'L0_ffn_W3': 8.0,
     'L0_ffn_W1s': 5.232,
     'L0_ffn_W2s': 5.202,
     'L0_ffn_W3s': 5.191,
     'L2_ffn_router_w': 8.0,
     'L2_ffn_gate_w': 8.0,
     'L2_ffn_up_w': 8.0,
     'L2_ffn_down_w': 8.0,
     'L3_ffn_router_w': 8.0,
     'L3_ffn_gate_proj': 8.0,
     'L3_ffn_up_proj': 8.0,
     'L3_ffn_down_proj': 8.0}
    for name, (base, spread) in spreads.items():
        noise = np.random.default_rng([zlib.crc32(name.encode()), seed]).standard_normal(out[name].shape)
        drawn = base * np.exp(spread * noise) if base else spread * noise
        out[name] = jnp.asarray(drawn.astype(out[name].dtype))
    for name, factor in factors.items():
        out[name] = (out[name] * factor).astype(out[name].dtype)
    return out
```

```python
from contextlib import ExitStack

import numpy as np
import concourse.bass as bass
from concourse import mybir

FP32 = mybir.dt.float32
F32R = mybir.dt.float32r
BF16 = mybir.dt.bfloat16
U8 = mybir.dt.uint8
I32 = mybir.dt.int32
ALU = mybir.AluOpType
ACT = mybir.ActivationFunctionType
AX = mybir.AxisListType

B, S, H, L, D = 16, 56, 256, 1500, 64
NH, K, CQ = 16, 128, 192
T = B * S
NT = T // 128
KC = H // 128
HALF = T // 2
NP = NH // 2
KP = 125
NC = L // KP
SB = 500
NS = L // SB
CG = NC // NS
CQH = CQ // 2
EPS = 1e-5
FP8_MAX = 448.0


class Count:

    def __init__(self, eng, sem):
        self.eng, self.sem, self.n = eng, sem, 0

    def mark(self, ins):
        self.n += 1
        ins.then_inc(self.sem, 1)

    def link(self, ins):
        self.mark(ins)
        self.eng.wait_ge(self.sem, self.n)


class Semaphores:

    EACH = 26

    def __init__(self, nc, stack):
        self.sets = [[stack.enter_context(nc.semaphore(f"set{i}_{n}")) for n in range(self.EACH)] for i in range(2)]
        self.used, self.turn = [0, 0], 0

    def start(self):
        self.turn = 1 - self.turn
        self.used[self.turn] = 0

    def take(self):
        n = self.used[self.turn]
        self.used[self.turn] = n + 1
        return self.sets[self.turn][n]

    def clear_earlier(self, sp):
        for sem in self.sets[1 - self.turn][:self.used[1 - self.turn]]:
            sp.sem_clear(sem)


class Stage:

    semaphores = None

    def __init__(self, nc, name):
        self.nc, self.name, self.stack, self.started = nc, name, ExitStack(), False

    def __enter__(self):
        self.stack.__enter__()
        return self

    def __exit__(self, *a):
        return self.stack.__exit__(*a)

    def sb(self, name, shape, dt=FP32):
        return self.stack.enter_context(self.nc.sbuf_tensor(f"{self.name}_{name}", shape, dt))

    def sem(self, name):
        if not self.started:
            self.started = True
            self.semaphores.start()
        return self.semaphores.take()


def from_first(eng, steps, step):
    step(0, True)
    with eng.Fori(1, steps) as i:
        step(i, False)


def rotate_context(nc, G):
    with Stage(nc, "rot") as st:
        cosT, sinT = st.sb("cosT", [128, L]), st.sb("sinT", [128, L])
        cosN, sinN = st.sb("cosN", [KP, NC * D]), st.sb("sinN", [KP, NC * D])
        ct, cs = st.sb("ct", [128, 2, L]), st.sb("cs", [128, 2, L])
        hi, lo = st.sb("hi", [128, 2, L], F32R), st.sb("lo", [128, 2, L], F32R)
        cn, cm = st.sb("cn", [KP, 2, 2, NC * D]), st.sb("cm", [KP, 2, 2, NC * D])
        tables = st.sem("tables")
        gates_in = st.sem("gates_in")
        in_t = [st.sem(f"in_t{s}") for s in range(2)]
        in_n = [st.sem(f"in_n{s}") for s in range(2)]
        sin_done, mul_done, sum_t, hi_done, lo_done, sum_n = (
            st.sem(n) for n in ("sin_done", "mul_done", "sum_t", "hi_done", "lo_done", "sum_n"))
        out_t = [st.sem(f"out_t{s}") for s in range(2)]
        out_n = [st.sem(f"out_n{s}") for s in range(2)]
        gates_done = st.sem("gates_done")
        k0_in, k0_done = st.sem("k0_in"), st.sem("k0_done")
        k0 = st.sb("k0", [128, T])
        with nc.Block() as block:

            @block.sync
            def _(sp):
                Stage.semaphores.clear_earlier(sp)
                for dst, src in ((cosT, "cosT"), (sinT, "sinT"), (cosN, "cosN"), (sinN, "sinN")):
                    sp.dma_start(dst[:, :], G[src]).then_inc(tables, 16)

                def step(i, first):
                    for s in range(2):
                        if not first:
                            sp.wait_ge(lo_done, i * 2 + s - 1)
                        rows = bass.ds(i * 256 + s * 128, 128)
                        sp.dma_start(ct[:, s, :], G["ctxT"][rows, :]).then_inc(in_t[s], 16)
                        sp.dma_start(cs[:, s, :], G["ctxTs"][rows, :]).then_inc(in_t[s], 16)
                        if not first:
                            sp.wait_ge(out_n[s], i * 16)
                        pair = bass.ds(i * 4 + 2 * s, 2)
                        sp.dma_start(cn[:, s], G["ctxN"][pair].rearrange("b p n -> p b n")).then_inc(in_n[s], 16)
                        sp.dma_start(cm[:, s], G["ctxNs"][pair].rearrange("b p n -> p b n")).then_inc(in_n[s], 16)

                from_first(sp, B // 4, step)

            @block.gpsimd
            def _(pool):
                pool.wait_ge(tables, 64)
                with pool.Fori(0, B // 4) as i:
                    for s in range(2):
                        pool.wait_ge(in_t[s], i * 32 + 32)
                        pool.tensor_tensor(cs[:, s, :], cs[:, s, :], sinT[:, :], ALU.mult).then_inc(sin_done, 1)
                        pool.wait_ge(in_n[s], i * 32 + 32)
                        pool.tensor_tensor(cm[:, s], cm[:, s], sinN[:, :].unsqueeze(1).broadcast_to([KP, 2, NC * D]),
                                           ALU.mult).then_inc(sin_done, 1)

            @block.vector
            def _(dve):
                dve.wait_ge(tables, 64)

                def step(i, first):
                    for s in range(2):
                        n = i * 2 + s
                        dve.wait_ge(in_t[s], i * 32 + 32)
                        dve.tensor_tensor(ct[:, s, :], ct[:, s, :], cosT[:, :], ALU.mult).then_inc(mul_done, 1)
                        dve.wait_ge(in_n[s], i * 32 + 32)
                        dve.tensor_tensor(cn[:, s], cn[:, s], cosN[:, :].unsqueeze(1).broadcast_to([KP, 2, NC * D]),
                                          ALU.mult).then_inc(mul_done, 1)
                        dve.wait_ge(mul_done, n * 2 + 2)
                        dve.wait_ge(sin_done, n * 2 + 2)
                        dve.tensor_tensor(ct[:, s, :], ct[:, s, :], cs[:, s, :], ALU.add).then_inc(sum_t, 1)
                        dve.tensor_tensor(cn[:, s], cn[:, s], cm[:, s], ALU.add).then_inc(sum_n, 1)
                        dve.wait_ge(hi_done, n + 1)
                        if not first:
                            dve.wait_ge(out_t[s], i * 32)
                        dve.tensor_tensor(lo[:, s, :], ct[:, s, :], hi[:, s, :].bitcast(FP32),
                                          ALU.subtract).then_inc(lo_done, 1)

                from_first(dve, B // 4, step)
                dve.wait_ge(k0_in, 48)
                dve.tensor_copy(G["k0"][:, 0, :], k0[:, :]).then_inc(k0_done, 1)
                dve.wait_ge(k0_done, 1)
                dve.tensor_tensor(G["k0"][:, 1, :], k0[:, :], G["k0"][:, 0, :].bitcast(FP32),
                                  ALU.subtract).then_inc(k0_done, 1)

            @block.scalar
            def _(act):
                act.dma_start(k0[0:64, :], G["ctx0T"]).then_inc(k0_in, 16)
                act.dma_start(k0[64:128, :], G["ctx0T"]).then_inc(k0_in, 16)
                act.dma_start(G["v0"][:, :, :], G["ctx0N"]).then_inc(k0_in, 16)
                act.dma_start(G["x"][:, :, :], G["x_in"]).then_inc(gates_in, 16)
                act.dma_start(G["ident"][:, :], G["ident_in"]).then_inc(gates_in, 16)
                act.dma_start(G["gate"][:, 0:4], G["g_xattn"].broadcast_to([128, 4])).then_inc(gates_in, 16)
                act.dma_start(G["gate"][:, 4:8], G["g_ffn"].broadcast_to([128, 4])).then_inc(gates_in, 16)
                act.wait_ge(gates_in, 64)
                act.activation(G["tanh"][:, :], G["gate"][:, :], ACT.Tanh).then_inc(gates_done, 1)

                def step(i, first):
                    for s in range(2):
                        n = i * 2 + s
                        if not first:
                            act.wait_ge(out_t[s], i * 32)
                        act.wait_ge(sum_t, n + 1)
                        act.activation(hi[:, s, :], ct[:, s, :], ACT.Copy).then_inc(hi_done, 1)
                        act.wait_ge(sum_n, n + 1)
                        act.dma_start(G["kvn"][bass.ds(i * 4 + 2 * s, 2)].rearrange("b p n -> p b n"),
                                      cn[:, s]).then_inc(out_n[s], 16)
                        act.wait_ge(lo_done, n + 1)
                        rows = bass.ds(i * 256 + s * 128, 128)
                        act.dma_start(G["kvt_hi"][rows, :], hi[:, s, :].bitcast(FP32)).then_inc(out_t[s], 16)
                        act.dma_start(G["kvt_lo"][rows, :], lo[:, s, :].bitcast(FP32)).then_inc(out_t[s], 16)

                from_first(act, B // 4, step)
                for s in range(2):
                    act.wait_ge(out_t[s], B // 4 * 32)
                    act.wait_ge(out_n[s], B // 4 * 16)


def normalise(nc, G, name):
    x, xT, PS, ident = G["x"], G["xT"], G["PS"], G["ident"]
    with Stage(nc, name) as st:
        stats, mv = st.sb("stats", [128, NT, 6]), st.sb("mv", [128, NT, 2])
        ve, sd, r, t = (st.sb(n, [128, NT]) for n in ("ve", "sd", "r", "t"))
        xn = st.sb("xn", [128, NT, H])
        chain, var_ready, sqrt_done, xn_ready, tr_done, copied = (
            st.sem(n) for n in ("chain", "var_ready", "sqrt_done", "xn_ready", "tr_done", "copied"))
        with nc.Block() as block:

            @block.sync
            def _(sp):
                Stage.semaphores.clear_earlier(sp)

            @block.vector
            def _(dve):
                c = Count(dve, chain)
                for i in range(NT):
                    c.mark(dve.bn_stats(stats[:, i, :], x[:, i, :]))
                for i in range(NT):
                    dve.wait_ge(chain, i + 1)
                    c.mark(dve.bn_aggr(mv[:, i, :], stats[:, i, :]))
                dve.wait_ge(chain, c.n)
                dve.tensor_scalar(ve[:, :], mv[:, :, 1], EPS, None, ALU.add).then_inc(var_ready, 1)
                dve.wait_ge(sqrt_done, 1)
                c.link(dve.reciprocal(r[:, :], sd[:, :]))
                c.link(dve.tensor_tensor(t[:, :], r[:, :], r[:, :], ALU.mult))
                c.link(dve.tensor_tensor(t[:, :], t[:, :], ve[:, :], ALU.mult))
                c.link(dve.tensor_scalar(t[:, :], t[:, :], -0.5, 1.5, ALU.mult, ALU.add))
                c.link(dve.tensor_tensor(r[:, :], r[:, :], t[:, :], ALU.mult))
                for i in range(NT):
                    dve.tensor_scalar(xn[:, i, :], x[:, i, :], mv[:, i, 0:1], r[:, i:i + 1],
                                      ALU.subtract, ALU.mult).then_inc(xn_ready, 1)

            @block.scalar
            def _(act):
                act.wait_ge(var_ready, 1)
                act.activation(sd[:, :], ve[:, :], ACT.Sqrt).then_inc(sqrt_done, 1)
                for i in range(NT):
                    act.wait_ge(tr_done, i + 1)
                    act.activation(xT[:, :, 128 * i:128 * i + 128],
                                   PS[i][:, 0:256].rearrange("p (k n) -> p k n", k=KC), ACT.Copy).then_inc(copied, 1)

            @block.tensor
            def _(pe):
                for i in range(NT):
                    pe.wait_ge(xn_ready, i + 1)
                    for k in range(KC):
                        last = pe.transpose(PS[i][:, 128 * k:128 * k + 128], xn[:, i, 128 * k:128 * k + 128],
                                            ident[:, :])
                    last.then_inc(tr_done, 1)


def fold_small(nc, G, A, Bm):
    PS = G["PS"]
    HD = H // NH
    with Stage(nc, "fold0") as st:
        wq, wk = st.sb("wq", [HD, NH, H]), st.sb("wk", [HD, NH, D])
        wv, wo = st.sb("wv", [HD, NH, D]), st.sb("wo", [HD, NH, H])
        w_in, a_ready, b_ready, a_done, b_done = (
            st.sem(n) for n in ("w_in", "a_ready", "b_ready", "a_done", "b_done"))
        with nc.Block() as block:

            @block.sync
            def _(sp):
                Stage.semaphores.clear_earlier(sp)
                for dst, src in ((wq, "L0_wq"), (wk, "L0_wk"), (wv, "L0_wv"), (wo, "L0_wo")):
                    sp.dma_start(dst[:, :, :], G[src]).then_inc(w_in, 16)

            @block.tensor
            def _(pe):
                pe.wait_ge(w_in, 64)
                for g in range(4):
                    for h in range(4 * g, 4 * g + 4):
                        for k in range(KC):
                            o = (k * 4 + h % 4) * D
                            last = pe.matmul(PS[g][:, o:o + D], wq[:, h, 128 * k:128 * k + 128], wk[:, h, :],
                                             start=True, stop=True)
                    last.then_inc(a_ready, 1)
                for g in range(4):
                    for h in range(4 * g, 4 * g + 4):
                        o = h % 4 // 2 * H
                        last = pe.matmul(PS[4 + g][h % 2 * 64:h % 2 * 64 + 64, o:o + H], wv[:, h, :], wo[:, h, :],
                                         start=True, stop=True)
                    last.then_inc(b_ready, 1)

            @block.scalar
            def _(act):
                for g in range(4):
                    act.wait_ge(a_ready, g + 1)
                    act.activation(A[:, :, 4 * g:4 * g + 4, :],
                                   PS[g][:, :].rearrange("p (k h d) -> p k h d", k=KC, h=4),
                                   ACT.Copy).then_inc(a_done, 1)

            @block.vector
            def _(dve):
                for g in range(4):
                    dve.wait_ge(b_ready, g + 1)
                    dve.tensor_copy(Bm[:, 2 * g:2 * g + 2, :],
                                    PS[4 + g][:, :].rearrange("p (h n) -> p h n", h=2)).then_inc(b_done, 1)


def fold_latent(nc, G, l, A, Bm, Q=None, N=None):
    PS = G["PS"]
    rotated = Q is not None
    with Stage(nc, f"fold{l}") as st:
        wq = st.sb("wq", [K, NH, H])
        wqr, wkr = st.sb("wqr", [D, NH, CQ]), st.sb("wkr", [D, NH, D])
        wv, wo = st.sb("wv", [K, NH, D]), st.sb("wo", [K, NH, H])
        wc = st.sb("wc", [K, NH, CQ]) if rotated else st.sb("wc", [CQH, 2, NH, K])
        M = None if rotated else st.sb("M", [K, NH, D])
        Nn = N if rotated else st.sb("N", [CQH, 2, NH, D])
        in_n, in_b, in_q, n_ready, b_ready, m_ready, a_ready = (
            st.sem(n) for n in ("in_n", "in_b", "in_q", "n_ready", "b_ready", "m_ready", "a_ready"))
        n_done, b_done, m_done, a_done = (st.sem(n) for n in ("n_done", "b_done", "m_done", "a_done"))
        with nc.Block() as block:

            @block.sync
            def _(sp):
                Stage.semaphores.clear_earlier(sp)
                sp.dma_start(wqr[:, :, :], G[f"L{l}_wqr"]).then_inc(in_n, 16)
                sp.dma_start(wkr[:, :, :], G[f"L{l}_wkr"]).then_inc(in_n, 16)
                sp.dma_start(wc[:], G[f"L{l}_wc"]).then_inc(in_q, 16)
                sp.dma_start(wq[:, :, :], G[f"L{l}_wq"]).then_inc(in_q, 16)

            @block.tensor
            def _(pe):
                pe.wait_ge(in_n, 32)
                for g in range(4):
                    for h in range(4 * g, 4 * g + 4):
                        for c in range(2):
                            o = (c * 4 + h % 4) * D
                            last = pe.matmul(PS[g][0:CQH, o:o + D], wqr[:, h, CQH * c:CQH * c + CQH], wkr[:, h, :],
                                             start=True, stop=True)
                    last.then_inc(n_ready, 1)
                pe.wait_ge(in_b, 32)
                for g in range(4):
                    for h in range(4 * g, 4 * g + 4):
                        o = h % 4 // 2 * H
                        last = pe.matmul(PS[4 + g][h % 2 * 64:h % 2 * 64 + 64, o:o + H], wv[:, h, :], wo[:, h, :],
                                         start=True, stop=True)
                    last.then_inc(b_ready, 1)
                pe.wait_ge(in_q, 32)
                if rotated:
                    for h in range(NH):
                        if h < 4:
                            pe.wait_ge(n_done, h + 1)
                        else:
                            pe.wait_ge(a_done, h - 3)
                        for k in range(KC):
                            last = pe.matmul(PS[h % 4][:, k * CQ:k * CQ + CQ], wq[:, h, 128 * k:128 * k + 128],
                                             wc[:, h, :], start=True, stop=True)
                        last.then_inc(a_ready, 1)
                    return
                for g in range(2):
                    pe.wait_ge(n_done, 4)
                    for h in range(8 * g, 8 * g + 8):
                        for c in range(2):
                            last = pe.matmul(PS[g][:, h % 8 * D:h % 8 * D + D], wc[:, c, h, :], Nn[:, c, h, :],
                                             start=c == 0, stop=c == 1)
                    last.then_inc(m_ready, 1)
                for g in range(4):
                    pe.wait_ge(m_done, g // 2 + 1)
                    pe.wait_ge(b_done, g + 1)
                    for h in range(4 * g, 4 * g + 4):
                        for k in range(KC):
                            o = (k * 4 + h % 4) * D
                            last = pe.matmul(PS[4 + g][:, o:o + D], wq[:, h, 128 * k:128 * k + 128], M[:, h, :],
                                             start=True, stop=True)
                    last.then_inc(a_ready, 1)

            @block.scalar
            def _(act):
                act.dma_start(wv[:, :, :], G[f"L{l}_wv"]).then_inc(in_b, 16)
                act.dma_start(wo[:, :, :], G[f"L{l}_wo"]).then_inc(in_b, 16)
                for g in range(4):
                    act.wait_ge(n_ready, g + 1)
                    act.activation(Nn[:, :, 4 * g:4 * g + 4, :],
                                   PS[g][0:CQH, :].rearrange("p (c h d) -> p c h d", c=2, h=4),
                                   ACT.Copy).then_inc(n_done, 1)
                if rotated:
                    for h in range(NH):
                        act.wait_ge(a_ready, h + 1)
                        act.activation(Q[:, h, :, :], PS[h % 4][:, 0:KC * CQ].rearrange("p (k q) -> p k q", k=KC),
                                       ACT.Copy).then_inc(a_done, 1)
                    return
                for g in range(2):
                    act.wait_ge(m_ready, g + 1)
                    act.activation(M[:, 8 * g:8 * g + 8, :], PS[g][:, :].rearrange("p (h d) -> p h d", h=8),
                                   ACT.Copy).then_inc(m_done, 1)
                for g in range(4):
                    act.wait_ge(a_ready, g + 1)
                    act.activation(A[:, :, 4 * g:4 * g + 4, :],
                                   PS[4 + g][:, :].rearrange("p (k h d) -> p k h d", k=KC, h=4),
                                   ACT.Copy).then_inc(a_done, 1)

            @block.vector
            def _(dve):
                for g in range(4):
                    dve.wait_ge(b_ready, g + 1)
                    dve.tensor_copy(Bm[:, 2 * g:2 * g + 2, :],
                                    PS[4 + g][:, :].rearrange("p (h n) -> p h n", h=2)).then_inc(b_done, 1)


def queries(nc, G, l, A, q_all):
    PS, xT = G["PS"], G["xT"]
    with Stage(nc, f"q{l}") as st:
        q_ready, hi_done, lo_done = (st.sem(n) for n in ("q_ready", "hi_done", "lo_done"))
        groups = [(p, e) for p in range(NP) for e in range(2)]
        with nc.Block() as block:

            @block.sync
            def _(sp):
                Stage.semaphores.clear_earlier(sp)

            @block.tensor
            def _(pe):
                for n, (p, e) in enumerate(groups):
                    if n >= 4:
                        pe.wait_ge(lo_done, 2 * (n - 3))
                    for k in range(KC):
                        last = pe.matmul(PS[n % 4][:, 0:HALF],
                                         A[:, k, 2 * p:2 * p + 2, :].rearrange("p h d -> p (h d)"),
                                         xT[:, k, HALF * e:HALF * e + HALF], start=k == 0, stop=k == KC - 1)
                    last.then_inc(q_ready, 1)

            split_queries(block, PS, q_all, groups, q_ready, hi_done, lo_done)


def split_queries(block, PS, q_all, groups, q_ready, hi_done, lo_done):
    def places(n, p, e, odd):
        src = PS[n % 4][64 * odd:64 * odd + 64, 0:HALF].rearrange("p (b s) -> p b s", s=S)
        b0 = B // 2 * e
        return src, q_all[0:64, b0:b0 + B // 2, 2 * p + odd, :], q_all[64:128, b0:b0 + B // 2, 2 * p + odd, :]

    @block.scalar
    def _(act):
        for n, (p, e) in enumerate(groups):
            act.wait_ge(q_ready, n + 1)
            for odd in range(2):
                src, hi, _ = places(n, p, e, odd)
                act.activation(hi, src, ACT.Copy).then_inc(hi_done, 1)

    @block.vector
    def _(dve):
        for n, (p, e) in enumerate(groups):
            dve.wait_ge(hi_done, 2 * n + 2)
            for odd in range(2):
                src, hi, lo = places(n, p, e, odd)
                dve.tensor_tensor(lo, src, hi.bitcast(FP32), ALU.subtract).then_inc(lo_done, 1)


def rotated_queries(nc, G, Q, N, q_all):
    PS, xT = G["PS"], G["xT"]
    with Stage(nc, "q2") as st:
        cos, sin = st.sb("cos", [CQH, 2, S]), st.sb("sin", [CQH, 2, S])
        tc, ts = st.sb("tc", [CQH, 2, 2, HALF]), st.sb("ts", [CQH, 2, 2, HALF])
        tables, big_ready, mul_done, rot_done, q_ready, hi_done, lo_done = (
            st.sem(n) for n in ("tables", "big_ready", "mul_done", "rot_done", "q_ready", "hi_done", "lo_done"))
        units = [(p, e, odd) for p in range(NP) for e in range(2) for odd in range(2)]
        with nc.Block() as block:

            @block.sync
            def _(sp):
                Stage.semaphores.clear_earlier(sp)
                sp.dma_start(cos[:, :, :], G["cosQ"]).then_inc(tables, 16)
                sp.dma_start(sin[:, :, :], G["sinQ"]).then_inc(tables, 16)

            @block.tensor
            def _(pe):
                def big(u):
                    p, e, odd = units[u]
                    if u >= 2:
                        pe.wait_ge(mul_done, 4 * (u - 1))
                    for c in range(2):
                        for k in range(KC):
                            last = pe.matmul(PS[4 + u % 2 * 2 + c][0:CQH, 0:HALF],
                                             Q[:, 2 * p + odd, k, CQH * c:CQH * c + CQH],
                                             xT[:, k, HALF * e:HALF * e + HALF], start=k == 0, stop=k == KC - 1)
                    last.then_inc(big_ready, 1)

                def small(u):
                    p, e, odd = units[u]
                    g = u // 2
                    if g >= 4 and not odd:
                        pe.wait_ge(lo_done, 2 * (g - 3))
                    pe.wait_ge(rot_done, u + 1)
                    for c in range(2):
                        last = pe.matmul(PS[g % 4][64 * odd:64 * odd + 64, 0:HALF], N[:, c, 2 * p + odd, :],
                                         tc[:, u % 2, c, :], start=c == 0, stop=c == 1)
                    last.then_inc(q_ready, 1)

                for u in range(len(units) + 1):
                    if u < len(units):
                        big(u)
                    if u:
                        small(u - 1)

            def places(g, odd):
                p, e, _ = units[2 * g + odd]
                src = PS[g % 4][64 * odd:64 * odd + 64, 0:HALF].rearrange("p (b s) -> p b s", s=S)
                b0 = B // 2 * e
                return src, q_all[0:64, b0:b0 + B // 2, 2 * p + odd, :], q_all[64:128, b0:b0 + B // 2, 2 * p + odd, :]

            @block.scalar
            def _(act):
                for g in range(len(units) // 2):
                    act.wait_ge(q_ready, 2 * g + 2)
                    for odd in range(2):
                        src, hi, _ = places(g, odd)
                        act.activation(hi, src, ACT.Copy).then_inc(hi_done, 1)

            @block.vector
            def _(dve):
                def lows(g):
                    dve.wait_ge(hi_done, 2 * g + 2)
                    for odd in range(2):
                        src, hi, lo = places(g, odd)
                        dve.tensor_tensor(lo, src, hi.bitcast(FP32), ALU.subtract).then_inc(lo_done, 1)

                dve.wait_ge(tables, 32)
                for u in range(len(units)):
                    dve.wait_ge(big_ready, u + 1)
                    if u >= 2:
                        dve.wait_ge(q_ready, u - 1)
                    for c in range(2):
                        src = PS[4 + u % 2 * 2 + c][0:CQH, 0:HALF].rearrange("p (b s) -> p b s", s=S)
                        for dst, tab in ((tc[:, u % 2, c, :], cos[:, c, :]), (ts[:, u % 2, 1 - c, :], sin[:, 1 - c, :])):
                            dve.tensor_tensor(dst.rearrange("p (b s) -> p b s", s=S), src,
                                              tab.unsqueeze(1).broadcast_to([CQH, B // 2, S]),
                                              ALU.mult).then_inc(mul_done, 1)
                    if u >= 3 and u % 2:
                        lows((u - 3) // 2)
                lows(len(units) // 2 - 1)

            @block.gpsimd
            def _(pool):
                for u in range(len(units)):
                    pool.wait_ge(mul_done, 4 * u + 4)
                    pool.tensor_tensor(tc[:, u % 2], tc[:, u % 2], ts[:, u % 2], ALU.add).then_inc(rot_done, 1)


def attend_short(nc, G, q_all, ctxT):
    PS, ident, k0, v0 = G["PS"], G["ident"], G["k0"], G["v0"]
    SCALE = float(H // NH) ** -0.5
    W0 = 4 * 128
    with Stage(nc, "att0") as st:
        mask = st.sb("mask", [128, NT, S])
        qst = st.sb("qst", [128, 2, NH * S], F32R)
        pw = st.sb("p", [128, 2, (NT - 1) * S + 128])
        pT = st.sb("pT", [S, 2, T])
        mx, rs = st.sb("mx", [128, 2, NT]), st.sb("rs", [128, 2, NT])
        p = [pw[:, s, 0:NT * S].rearrange("p (t k) -> p t k", t=NT) for s in range(2)]
        oc = st.sb("oc", [128, 2, NT + 1, D])
        cT = st.sb("cT", [D, 2, NH, S])
        pad_done = st.sem("pad_done")
        mask_in, s_ready, masked, maxed, centred, exp_done, summed, inverted = (
            st.sem(n) for n in ("mask_in", "s_ready", "masked", "maxed", "centred", "exp_done", "summed", "inverted"))
        q_in = [st.sem(f"q_in{s}") for s in range(2)]
        t_ready, t_copied, o_ready, o_scaled, c_ready, c_copied, placed = (
            st.sem(n) for n in ("t_ready", "t_copied", "o_ready", "o_scaled", "c_ready", "c_copied", "placed"))
        with nc.Block() as block:

            @block.sync
            def _(sp):
                Stage.semaphores.clear_earlier(sp)
                sp.dma_start(mask[:, :, :], G["mask0"]).then_inc(mask_in, 16)

                def step(i, first):
                    for s in range(2):
                        if not first:
                            sp.wait_ge(s_ready, 2 * i + s - 1)
                        sp.dma_start(qst[:, s, :].bitcast(FP32),
                                     q_all[:, bass.ds(2 * i + s, 1)].bitcast(FP32)
                                     .rearrange("p b h s -> p (b h s)")).then_inc(q_in[s], 16)

                from_first(sp, B // 2, step)

            @block.tensor
            def _(pe):
                pe.wait_ge(pad_done, 2)

                def step(i, first):
                    for s in range(2):
                        pe.wait_ge(q_in[s], i * 16 + 16)
                        if not first:
                            pe.wait_ge(masked, 2 * i + s - 1)
                        for t in range(NT):
                            for part in range(2):
                                last = pe.matmul(PS[s][:, t * S:t * S + S], qst[:, s, 128 * t:128 * t + 128],
                                                 k0[:, part, bass.ds((2 * i + s) * S, S)],
                                                 start=part == 0, stop=part == 1)
                        last.then_inc(s_ready, 1)
                    for s in range(2):
                        pe.wait_ge(exp_done, 2 * i + s + 1)
                        if not (first and s == 0):
                            pe.wait_ge(t_copied, 2 * (2 * i + s))
                        for t in range(NT):
                            last = pe.transpose(PS[2 + t // 4][:, t % 4 * 128:t % 4 * 128 + 128],
                                                pw[:, s, t * S:t * S + 128], ident[:, :])
                            if t in (3, NT - 1):
                                last.then_inc(t_ready, 1)
                    for s in range(2):
                        pe.wait_ge(t_copied, 2 * (2 * i + s) + 2)
                        if not (first and s == 0):
                            pe.wait_ge(o_scaled, 2 * i + s)
                        for t in range(NT):
                            last = pe.matmul(PS[4][:, t * D:t * D + D], pT[:, s, 128 * t:128 * t + 128],
                                             v0[:, bass.ds(2 * i + s, 1), :].rearrange("p b d -> p (b d)"),
                                             start=True, stop=True)
                        last.then_inc(o_ready, 1)
                    for s in range(2):
                        pe.wait_ge(o_scaled, 2 * i + s + 1)
                        if not (first and s == 0):
                            pe.wait_ge(c_copied, 2 * (2 * i + s))
                        for t in range(0, NT, 2):
                            last = pe.transpose(PS[5][:, 64 * t:64 * t + 128],
                                                oc[:, s, t:t + 2, :].rearrange("p t d -> p (t d)"), ident[:, :])
                        last.then_inc(c_ready, 1)

                from_first(pe, B // 2, step)

            @block.vector
            def _(dve):
                dve.wait_ge(mask_in, 16)
                with dve.Fori(0, B // 2) as i:
                    for s in range(2):
                        n = 2 * i + s + 1
                        dve.wait_ge(s_ready, n)
                        dve.tensor_tensor(p[s], PS[s][:, 0:NT * S].rearrange("p (t k) -> p t k", t=NT),
                                          mask[:, :, :], ALU.add).then_inc(masked, 1)
                        dve.wait_ge(masked, n)
                        dve.tensor_reduce(mx[:, s, :], p[s], AX.X, ALU.max).then_inc(maxed, 1)
                        dve.wait_ge(maxed, n)
                        dve.tensor_tensor(p[s], p[s], mx[:, s, :].unsqueeze(2).broadcast_to([128, NT, S]),
                                          ALU.subtract).then_inc(centred, 1)
                    for s in range(2):
                        n = 2 * i + s + 1
                        dve.wait_ge(exp_done, n)
                        dve.tensor_reduce(rs[:, s, :], p[s], AX.X, ALU.add).then_inc(summed, 1)
                        dve.wait_ge(summed, n)
                        dve.reciprocal(rs[:, s, :], rs[:, s, :]).then_inc(inverted, 1)
                    for s in range(2):
                        n = 2 * i + s + 1
                        dve.wait_ge(inverted, n)
                        dve.wait_ge(o_ready, n)
                        dve.tensor_tensor(oc[:, s, 0:NT, :], PS[4][:, 0:NT * D].rearrange("p (t d) -> p t d", t=NT),
                                          rs[:, s, :].unsqueeze(2).broadcast_to([128, NT, D]),
                                          ALU.mult).then_inc(o_scaled, 1)

            @block.scalar
            def _(act):

                def step(i, first):
                    for s in range(2):
                        act.wait_ge(centred, 2 * i + s + 1)
                        act.activation(p[s], p[s], ACT.Exp, scale=SCALE).then_inc(exp_done, 1)
                    for s in range(2):
                        for g, (a, z) in enumerate(((0, W0), (W0, T))):
                            act.wait_ge(t_ready, 2 * (2 * i + s) + g + 1)
                            act.activation(pT[:, s, a:z], PS[2 + g][0:S, 0:z - a], ACT.Copy).then_inc(t_copied, 1)
                    for s in range(2):
                        if not first:
                            act.wait_ge(placed, 4 * i)
                        act.wait_ge(c_ready, 2 * i + s + 1)
                        for odd in range(2):
                            copy_context(act, PS[5], cT[:, s], odd, c_copied)

                from_first(act, B // 2, step)

            @block.gpsimd
            def _(pool):
                pool.memset(oc[:, :, NT, :], 0.0).then_inc(pad_done, 1)
                pool.memset(pw[:, :, NT * S:], 0.0).then_inc(pad_done, 1)
                with pool.Fori(0, B // 2) as i:
                    for s in range(2):
                        pool.wait_ge(c_copied, 2 * (2 * i + s) + 2)
                        place_context(pool, ctxT, cT[:, s], (2 * i + s) * S, placed)


def copy_context(act, bank, cT, odd, c_copied):
    n = (NT + 1 - odd) // 2
    tiles = cT.rearrange("p h s -> p (h s)").rearrange("p (t r) -> p t r", r=128)
    act.activation(tiles[:, odd:NT:2, :], bank[64 * odd:64 * odd + D, 0:128 * n].rearrange("p (t r) -> p t r", r=128),
                   ACT.Copy).then_inc(c_copied, 1)


def place_context(pool, ctxT, cT, at, placed):
    for odd in range(2):
        pool.tensor_copy(ctxT[64 * odd:64 * odd + 64, :, bass.ds(at, S)],
                         cT.rearrange("p (h two) s -> p two h s", two=2)[:, odd]).then_inc(placed, 1)


def attend_long(nc, G, l, q_all, ctxT):
    PS, ident = G["PS"], G["ident"]
    PST, PSO = PS[6], PS[7]
    N = B * NT
    with Stage(nc, f"att{l}") as st:
        qst = st.sb("qst", [128, 2, NH * S], F32R)
        kst = st.sb("kst", [128, 2, 2, L], F32R)
        vst = st.sb("vst", [KP, 2, NC, D])
        p = st.sb("p", [128, 2, L])
        pT = st.sb("pT", [KP, 2, NC, 128])
        nm = st.sb("nm", [128, 2])
        sums = st.sb("sums", [128, 2, NT])
        rs = st.sb("rs", [128, NT])
        oc = st.sb("oc", [128, NT + 1, D])
        cT = st.sb("cT", [D, NH, S])
        kv_in = [st.sem(f"kv_in{s}") for s in range(2)]
        s_ready, max_ready, exp_done, t_ready, act_copied, dve_copied = (
            st.sem(n) for n in ("s_ready", "max_ready", "exp_done", "t_ready", "act_copied", "dve_copied"))
        o_ready, inverted, o_scaled, c_ready, c_copied, placed, pad_done = (
            st.sem(n) for n in ("o_ready", "inverted", "o_scaled", "c_ready", "c_copied", "placed", "pad_done"))

        def emit(eng, steps):
            steps(0, True, False)
            with eng.Fori(1, B // 2 - 1) as i:
                steps(i, False, False)
            steps(B // 2 - 1, False, True)

        with nc.Block() as block:

            @block.sync
            def _(sp):
                Stage.semaphores.clear_earlier(sp)
                def load(i, s):
                    b = 2 * i + s
                    sp.dma_start(qst[:, s, :].bitcast(FP32),
                                 q_all[:, bass.ds(b, 1)].bitcast(FP32).rearrange("p b h s -> p (b h s)")
                                 ).then_inc(kv_in[s], 16)
                    for half in range(2):
                        for part, src in enumerate(("kvt_hi", "kvt_lo")):
                            sp.dma_start(kst[64 * half:64 * half + 64, s, part, :].bitcast(FP32),
                                         G[src][bass.ds(b * D, D), :]).then_inc(kv_in[s], 16)
                    sp.dma_start(vst[:, s].rearrange("p c d -> p (c d)"),
                                 G["kvn"][bass.ds(b, 1)].rearrange("b p n -> (b p) n")).then_inc(kv_in[s], 16)

                load(0, 0)
                load(0, 1)
                with sp.Fori(1, B // 2) as i:
                    for s in range(2):
                        sp.wait_ge(o_ready, 2 * i + s - 1)
                        load(i, s)

            @block.tensor
            def _(pe):
                def scores(i, j, banks):
                    s, t = j // NT % 2, j % NT
                    for c in banks:
                        for part in range(2):
                            last = pe.matmul(PS[3 * (j % 2) + c][:, 0:SB], qst[:, s, 128 * t:128 * t + 128],
                                             kst[:, s, part, SB * c:SB * c + SB], start=part == 0, stop=part == 1)
                    if banks[-1] == NS - 1:
                        last.then_inc(s_ready, 1)

                def sums_of(i, j, g):
                    s, t = j // NT % 2, j % NT
                    if t == 0 and g == 0 and not (isinstance(i, int) and i == j == 0):
                        pe.wait_ge(o_scaled, 2 * i + j // NT)
                    for c in range(CG * g, CG * g + CG):
                        last = pe.matmul(PSO[:, t * D:t * D + D], pT[:, j % 2, c, :], vst[:, s, c, :],
                                         start=c == 0, stop=c == NC - 1)
                    if t == NT - 1 and g == NS - 1:
                        last.then_inc(o_ready, 1)

                def steps(i, first, last_pair):
                    for j in range(2 * NT):
                        n = i * 2 * NT + j
                        ahead = not (last_pair and j >= 2 * NT - 2)
                        behind = not (first and j == 0)
                        for g in range(NS):
                            if g == 0:
                                pe.wait_ge(exp_done, n + 1)
                                if behind:
                                    pe.wait_ge(act_copied, 2 * n)
                                if j % NT == 2 and not (first and j == 2):
                                    pe.wait_ge(c_copied, 2 * (2 * i + j // NT))
                            elif g == 1:
                                pe.wait_ge(act_copied, 2 * n + 1)
                            else:
                                pe.wait_ge(dve_copied, n + 1)
                            for c in range(CG * g, CG * g + CG):
                                last = pe.transpose(PST[0:KP, c % CG * 128:c % CG * 128 + 128],
                                                    p[:, j % 2, KP * c:KP * c + KP], ident[:, :])
                            last.then_inc(t_ready, 1)
                            if g == 0 and ahead:
                                if (j + 2) % NT == 0:
                                    m = i + (j + 2) // (2 * NT)
                                    pe.wait_ge(kv_in[(j + 2) // NT % 2], m * 96 + 96)
                                scores(i, j + 2, (0, 1))
                            if g == 1:
                                if ahead:
                                    scores(i, j + 2, (2,))
                                if behind:
                                    previous(i, j, 0)
                            if g == 2 and behind:
                                previous(i, j, 1)
                                previous(i, j, 2)
                        t = j % NT
                        if t == 1 and not (first and j == 1):
                            pe.wait_ge(act_copied, 2 * n + 2)
                            context(2 * i + j // NT)

                def previous(i, j, g):
                    if j:
                        sums_of(i, j - 1, g)
                    else:
                        sums_of(i - 1, 2 * NT - 1, g)

                def context(done):
                    pe.wait_ge(o_scaled, done)
                    for t in range(0, NT, 2):
                        last = pe.transpose(PST[:, 64 * t:64 * t + 128],
                                            oc[:, t:t + 2, :].rearrange("p t d -> p (t d)"), ident[:, :])
                    last.then_inc(c_ready, 1)

                pe.wait_ge(pad_done, 1)
                pe.wait_ge(kv_in[0], 96)
                scores(0, 0, (0, 1, 2))
                scores(0, 1, (0, 1, 2))
                emit(pe, steps)
                pe.wait_ge(act_copied, 2 * N)
                for g in range(NS):
                    sums_of(B // 2 - 1, 2 * NT - 1, g)
                context(B)

            @block.vector
            def _(dve):
                def row_max(j, n):
                    dve.wait_ge(s_ready, n + 1)
                    dve.tensor_reduce(nm[:, j % 2:j % 2 + 1], banks(PS, 3 * (j % 2)), AX.XY, ALU.max,
                                      negate=True).then_inc(max_ready, 1)

                def scale(done):
                    dve.wait_ge(o_ready, done)
                    dve.reciprocal(rs[:, :], sums[:, (done - 1) % 2, :] if isinstance(done, int) else sums_of_slot[0]
                                   ).then_inc(inverted, 1)
                    dve.wait_ge(inverted, done)
                    dve.tensor_tensor(oc[:, 0:NT, :], PSO[:, 0:NT * D].rearrange("p (t d) -> p t d", t=NT),
                                      rs[:, :].unsqueeze(2).broadcast_to([128, NT, D]),
                                      ALU.mult).then_inc(o_scaled, 1)

                sums_of_slot = [None]

                def steps(i, first, last_pair):
                    for j in range(2 * NT):
                        n = i * 2 * NT + j
                        t = j % NT
                        if t == 1 and not (first and j == 1):
                            sums_of_slot[0] = sums[:, (j // NT + 1) % 2, :]
                            scale(2 * i + j // NT)
                        dve.wait_ge(t_ready, 3 * n + 2)
                        dve.tensor_copy(pT[:, j % 2, CG:2 * CG, :],
                                        PST[0:KP, :].rearrange("p (c r) -> p c r", c=CG)).then_inc(dve_copied, 1)
                        if not (last_pair and j >= 2 * NT - 2):
                            row_max(j, n + 2)

                row_max(0, 0)
                row_max(1, 1)
                emit(dve, steps)
                sums_of_slot[0] = sums[:, 1, :]
                scale(B)

            @block.scalar
            def _(act):
                def exps(i, j, n):
                    act.wait_ge(max_ready, n + 1)
                    act.activation(p[:, j % 2, :].rearrange("p (c k) -> p c k", c=NS), banks(PS, 3 * (j % 2)),
                                   ACT.Exp, bias=nm[:, j % 2:j % 2 + 1],
                                   accum_out=sums[:, j // NT % 2, j % NT:j % NT + 1]).then_inc(exp_done, 1)

                def copy(n, j, g):
                    act.wait_ge(t_ready, 3 * n + g + 1)
                    act.activation(pT[:, j % 2, CG * g:CG * g + CG, :],
                                   PST[0:KP, :].rearrange("p (c r) -> p c r", c=CG), ACT.Copy).then_inc(act_copied, 1)

                def context(done):
                    if not (isinstance(done, int) and done == 1):
                        act.wait_ge(placed, 2 * (done - 1))
                    act.wait_ge(c_ready, done)
                    for odd in range(2):
                        copy_context(act, PST, cT[:, :, :], odd, c_copied)

                def steps(i, first, last_pair):
                    for j in range(2 * NT):
                        n = i * 2 * NT + j
                        copy(n, j, 0)
                        if not (last_pair and j == 2 * NT - 1):
                            exps(i, j + 1, n + 1)
                        copy(n, j, 2)
                        if j % NT == 1 and not (first and j == 1):
                            context(2 * i + j // NT)

                exps(0, 0, 0)
                emit(act, steps)
                context(B)

            @block.gpsimd
            def _(pool):
                pool.memset(oc[:, NT, :], 0.0).then_inc(pad_done, 1)
                with pool.Fori(0, B) as b:
                    pool.wait_ge(c_copied, 2 * b + 2)
                    place_context(pool, ctxT, cT[:, :, :], b * S, placed)


def banks(PS, first):
    return PS.all[:, first * 512:(first + NS) * 512].rearrange("p (c k) -> p c k", c=NS)[:, :, 0:SB]


def project_out(nc, G, l, Bm, ctxT):
    PS, x = G["PS"], G["x"]
    with Stage(nc, f"out{l}") as st:
        o_ready, x_done = st.sem("o_ready"), st.sem("x_done")
        with nc.Block() as block:

            @block.sync
            def _(sp):
                Stage.semaphores.clear_earlier(sp)

            @block.tensor
            def _(pe):
                for t in range(NT):
                    for h in range(NP):
                        last = pe.matmul(PS[t][:, 0:H], ctxT[:, h, 128 * t:128 * t + 128], Bm[:, h, :],
                                         start=h == 0, stop=h == NP - 1)
                    last.then_inc(o_ready, 1)

            @block.vector
            def _(dve):
                for t in range(NT):
                    dve.wait_ge(o_ready, t + 1)
                    dve.scalar_tensor_tensor(x[:, t, :], PS[t][:, 0:H], G["tanh"][:, l:l + 1], x[:, t, :],
                                             ALU.mult, ALU.add).then_inc(x_done, 1)


def route(nc, G, l, E, top, kind, rows, groups_per_expert):
    PS, xT, ident = G["PS"], G["xT"], G["ident"]
    with Stage(nc, f"route{l}") as st:
        wr, tie = st.sb("wr", [128, KC, E]), st.sb("tie", [128, E * E])
        bias = st.sb("bias", [128, E])
        lg, e, key = st.sb("lg", [128, NT, E]), st.sb("e", [128, NT, E]), st.sb("key", [128, NT, E])
        gt, eq = st.sb("gt", [128, NT, E * E]), st.sb("eq", [128, NT, E * E])
        rank, z = st.sb("rank", [128, NT, E]), st.sb("z", [128, NT])
        comb, combT = st.sb("comb", [128, NT, rows]), st.sb("combT", [rows, T])
        in_w, lg_ready, to_exp, exp_done, chain, comb_ready, tr_ready, tr_copied, stored = (
            st.sem(n) for n in ("in_w", "lg_ready", "to_exp", "exp_done", "chain", "comb_ready", "tr_ready",
                                "tr_copied", "stored"))
        loads = [(wr[:, :, :], G[f"L{l}_router"]), (tie[:, :], G[f"tie{E}"])]
        if kind == "renormalised":
            loads.append((bias[:, :], G["L3_bias"].broadcast_to([128, E])))
        with nc.Block() as block:

            @block.sync
            def _(sp):
                Stage.semaphores.clear_earlier(sp)
                for dst, src in loads:
                    sp.dma_start(dst, src).then_inc(in_w, 16)
                sp.wait_ge(tr_copied, 2)
                sp.dma_start(G["comb"][0:rows * groups_per_expert, :].rearrange("(e g) n -> e g n", e=rows),
                             combT[:, :].unsqueeze(1).broadcast_to([rows, groups_per_expert, T])).then_inc(stored, 16)
                sp.wait_ge(stored, 16)

            @block.tensor
            def _(pe):
                pe.wait_ge(in_w, 16 * len(loads))
                for t in range(NT):
                    for k in range(KC):
                        last = pe.matmul(PS[0][:, t * E:t * E + E], xT[:, k, 128 * t:128 * t + 128], wr[:, k, :],
                                         start=k == 0, stop=k == KC - 1)
                last.then_inc(lg_ready, 1)
                pe.wait_ge(comb_ready, 1)
                for t in range(NT):
                    last = pe.transpose(PS[1 + t // 4][0:rows, t % 4 * 128:t % 4 * 128 + 128], comb[:, t, :],
                                        ident[:, :])
                    if t in (3, NT - 1):
                        last.then_inc(tr_ready, 1)

            @block.scalar
            def _(act):
                act.wait_ge(to_exp, 1)
                act.activation(e[:, :, :], (lg if kind == "sigmoid" else e)[:, :, :], ACT.Exp,
                               scale=-1.0 if kind == "sigmoid" else 1.0).then_inc(exp_done, 1)
                for g, (a, b) in enumerate(((0, 512), (512, T))):
                    act.wait_ge(tr_ready, g + 1)
                    act.activation(combT[:, a:b], PS[1 + g][0:rows, 0:b - a], ACT.Copy).then_inc(tr_copied, 1)

            @block.vector
            def _(dve):
                c = Count(dve, chain)
                dve.wait_ge(lg_ready, 1)
                dve.wait_ge(in_w, 16 * len(loads))
                logits = PS[0][:, 0:NT * E].rearrange("p (t e) -> p t e", t=NT)
                wide = [128, NT, E]
                if kind == "renormalised":
                    c.link(dve.tensor_tensor(lg[:, :, :], logits, bias[:, :].unsqueeze(1).broadcast_to(wide), ALU.add))
                else:
                    c.link(dve.tensor_copy(lg[:, :, :], logits))
                if kind == "sigmoid":
                    dve.engine_nop().then_inc(to_exp, 1)
                    dve.wait_ge(exp_done, 1)
                    c.link(dve.tensor_scalar(e[:, :, :], e[:, :, :], 1.0, None, ALU.add))
                    c.link(dve.reciprocal(e[:, :, :], e[:, :, :]))
                    values = e
                else:
                    c.link(dve.tensor_reduce(z[:, :], lg[:, :, :], AX.X, ALU.max))
                    dve.tensor_tensor(e[:, :, :], lg[:, :, :], z[:, :].unsqueeze(2).broadcast_to(wide),
                                      ALU.subtract).then_inc(to_exp, 1)
                    values = lg
                for t in range(NT):
                    other = values[:, t, :].unsqueeze(1).broadcast_to([128, E, E])
                    own = values[:, t, :].unsqueeze(2).broadcast_to([128, E, E])
                    c.mark(dve.tensor_tensor(gt[:, t, :].rearrange("p (a b) -> p a b", a=E), other, own, ALU.is_gt))
                    c.mark(dve.tensor_tensor(eq[:, t, :].rearrange("p (a b) -> p a b", a=E), other, own, ALU.is_equal))
                dve.wait_ge(chain, c.n)
                c.link(dve.tensor_tensor(eq[:, :, :], eq[:, :, :], tie[:, :].unsqueeze(1).broadcast_to([128, NT, E * E]),
                                         ALU.mult))
                c.link(dve.tensor_tensor(gt[:, :, :], gt[:, :, :], eq[:, :, :], ALU.add))
                c.link(dve.tensor_reduce(rank[:, :, :], gt[:, :, :].rearrange("p t (a b) -> p t a b", a=E), AX.X,
                                         ALU.add))
                c.link(dve.tensor_scalar(rank[:, :, :], rank[:, :, :], float(top), None, ALU.is_lt))
                if rows > E:
                    c.link(dve.memset(comb[:, :, E:E + 2], 1.0))
                    c.link(dve.memset(comb[:, :, E + 2:rows], 0.0))
                if kind != "sigmoid":
                    dve.wait_ge(exp_done, 1)
                if kind == "sigmoid":
                    dve.tensor_tensor(comb[:, :, 0:E], e[:, :, :], rank[:, :, :], ALU.mult).then_inc(comb_ready, 1)
                    return
                c.link(dve.tensor_tensor(key[:, :, :], e[:, :, :], rank[:, :, :], ALU.mult))
                over = e if kind == "softmax" else key
                c.link(dve.tensor_reduce(z[:, :], over[:, :, :], AX.X, ALU.add))
                c.link(dve.reciprocal(z[:, :], z[:, :]))
                dve.tensor_tensor(comb[:, :, 0:E], key[:, :, :], z[:, :].unsqueeze(2).broadcast_to(wide),
                                  ALU.mult).then_inc(comb_ready, 1)


def experts(nc, G, l, chunks, group_rows):
    PS, xT, x, ident = G["PS"], G["xT"], G["x"], G["ident"]
    GU = 2 * KC * 128
    groups = 128 // group_rows
    with Stage(nc, f"moe{l}") as st:
        raw = st.sb("raw", [128, 2, GU + H])
        w = st.sb("w", [128, 2, 2, GU + H], F32R)
        xs = st.sb("xs", [128, 2, KC, T], F32R)
        cb = st.sb("cb", [128, 2, T])
        sg, sc, hf = st.sb("sg", [128, 2, HALF]), st.sb("sc", [128, 2, HALF]), st.sb("hf", [128, 2, HALF])
        h = st.sb("h", [128, 2, 2, 2, HALF], F32R)
        oT = st.sb("oT", [128, KC, T])
        w_in = [st.sem(f"w_in{s}") for s in range(2)]
        cb_in = [st.sem(f"cb_in{s}") for s in range(2)]
        x_high, x_split, gu_high, gu_split, d_high, d_split = (
            st.sem(n) for n in ("x_high", "x_split", "gu_high", "gu_split", "d_high", "d_split"))
        gu_ready, silu_done, comb_done, h_made, h_high, h_split, d_done = (
            st.sem(n) for n in ("gu_ready", "silu_done", "comb_done", "h_made", "h_high", "h_split", "d_done"))
        o_copied, tr_ready, x_done = (st.sem(n) for n in ("o_copied", "tr_ready", "x_done"))
        w_dram = G[f"L{l}_experts"]

        def emit(eng, chunk):
            chunk(0, 0, True, True)
            chunk(0, 1, False, True)
            done = (chunks - 1) // 2
            with eng.Fori(1, done) as i:
                for s in range(2):
                    chunk(i, s, False, True)
            for c in range(2 * done, chunks):
                chunk(done, c % 2, False, c < chunks - 1)

        def following(i, s):
            return (i, 1) if s == 0 else (i + 1, 0)

        with nc.Block() as block:

            @block.sync
            def _(sp):
                Stage.semaphores.clear_earlier(sp)

                def chunk(i, s, first, more):
                    c = 2 * i + s
                    if not isinstance(i, int) or i:
                        sp.wait_ge(d_split, c - 1)
                    sp.dma_start(raw[:, s, :], w_dram[bass.ds(c * 128, 128), :]).then_inc(w_in[s], 16)
                    if not isinstance(i, int) or i:
                        sp.wait_ge(comb_done, 2 * c - 2)
                    sp.dma_start(cb[:, s, :], G["comb"][bass.ds(c * groups, groups), :].unsqueeze(1)
                                 .broadcast_to([groups, group_rows, T])).then_inc(cb_in[s], 16)

                emit(sp, chunk)

            @block.tensor
            def _(pe):
                PARTS = ((0, 0), (0, 1), (1, 0))

                def up(c, s, e):
                    for m in range(2):
                        n = 0
                        for k in range(KC):
                            o = (m * KC + k) * 128
                            for pw, px in PARTS:
                                last = pe.matmul(PS[2 * e + m][:, 0:HALF], w[:, s, pw, o:o + 128],
                                                 xs[:, px, k, HALF * e:HALF * e + HALF],
                                                 start=n == 0, stop=n == 3 * KC - 1)
                                n += 1
                    last.then_inc(gu_ready, 1)

                def down(c, s, e, start, stop):
                    if e == 0:
                        pe.wait_ge(d_split, c + 1)
                    pe.wait_ge(h_split, 2 * c + e + 1)
                    for d in range(KC):
                        o = GU + 128 * d
                        for n, (pw, ph) in enumerate(PARTS):
                            last = pe.matmul(PS[4 + 2 * d + e][:, 0:HALF], w[:, s, pw, o:o + 128], h[:, s, ph, e, :],
                                             start=start and n == 0, stop=stop and n == 2)
                    if e == 1:
                        last.then_inc(d_done, 1)

                def chunk(i, s, first, more):
                    c = 2 * i + s
                    pe.wait_ge(gu_split, c + 1)
                    for e in range(2):
                        if not first:
                            pe.wait_ge(h_made, 2 * (c - 1) + e + 1)
                        up(c, s, e)
                        if not first:
                            down(c - 1, 1 - s, e, isinstance(i, int) and c == 1, False)

                pe.wait_ge(x_split, 1)
                emit(pe, chunk)
                for e in range(2):
                    down(chunks - 1, (chunks - 1) % 2, e, False, True)
                for t in range(NT):
                    if t == 0:
                        pe.wait_ge(o_copied, 2 * KC)
                    if t >= 4:
                        pe.wait_ge(x_done, t - 3)
                    for d in range(KC):
                        last = pe.transpose(PS[t % 4][:, 128 * d:128 * d + 128], oT[:, d, 128 * t:128 * t + 128],
                                            ident[:, :])
                    last.then_inc(tr_ready, 1)

            @block.scalar
            def _(act):
                def gu_part(i, s):
                    act.wait_ge(w_in[s], i * 16 + 16)
                    act.activation(w[:, s, 0, 0:GU], raw[:, s, 0:GU], ACT.Copy).then_inc(gu_high, 1)

                def d_part(i, s):
                    act.activation(w[:, s, 0, GU:], raw[:, s, GU:], ACT.Copy).then_inc(d_high, 1)

                def chunk(i, s, first, more):
                    c = 2 * i + s
                    for e in range(2):
                        n = 2 * c + e
                        act.wait_ge(gu_ready, n + 1)
                        act.activation(sg[:, e, :], PS[2 * e][:, 0:HALF], ACT.Silu).then_inc(silu_done, 1)
                        if more and e == 0:
                            gu_part(*following(i, s))
                        if more and e == 1:
                            if not first:
                                act.wait_ge(d_done, c)
                            d_part(*following(i, s))
                        act.wait_ge(h_made, n + 1)
                        act.activation(h[:, s, 0, e, :], hf[:, e, :], ACT.Copy).then_inc(h_high, 1)

                gu_part(0, 0)
                act.activation(xs[:, 0], xT[:, :, :], ACT.Copy).then_inc(x_high, 1)
                d_part(0, 0)
                emit(act, chunk)
                act.wait_ge(d_done, chunks)
                for e in range(2):
                    act.activation(oT[:, 0, HALF * e:HALF * e + HALF], PS[4 + e][:, 0:HALF],
                                   ACT.Copy).then_inc(o_copied, 1)

            @block.gpsimd
            def _(pool):
                def chunk(i, s, first, more):
                    pool.wait_ge(cb_in[s], i * 16 + 16)
                    for e in range(2):
                        n = 2 * (2 * i + s) + e
                        pool.wait_ge(silu_done, n + 1)
                        pool.tensor_tensor(sc[:, e, :], sg[:, e, :], cb[:, s, HALF * e:HALF * e + HALF],
                                           ALU.mult).then_inc(comb_done, 1)

                emit(pool, chunk)

            @block.vector
            def _(dve):
                def gu_part(c, s):
                    dve.wait_ge(gu_high, c + 1)
                    dve.tensor_tensor(w[:, s, 1, 0:GU], raw[:, s, 0:GU], w[:, s, 0, 0:GU].bitcast(FP32),
                                      ALU.subtract).then_inc(gu_split, 1)

                def d_part(c, s):
                    dve.wait_ge(d_high, c + 1)
                    dve.tensor_tensor(w[:, s, 1, GU:], raw[:, s, GU:], w[:, s, 0, GU:].bitcast(FP32),
                                      ALU.subtract).then_inc(d_split, 1)

                def chunk(i, s, first, more):
                    c = 2 * i + s
                    for e in range(2):
                        n = 2 * c + e
                        dve.wait_ge(comb_done, n + 1)
                        dve.tensor_tensor(hf[:, e, :], PS[2 * e + 1][:, 0:HALF], sc[:, e, :],
                                          ALU.mult).then_inc(h_made, 1)
                        if more:
                            (gu_part if e == 0 else d_part)(c + 1, 1 - s)
                        dve.wait_ge(h_high, n + 1)
                        dve.tensor_tensor(h[:, s, 1, e, :], hf[:, e, :], h[:, s, 0, e, :].bitcast(FP32),
                                          ALU.subtract).then_inc(h_split, 1)

                gu_part(0, 0)
                dve.wait_ge(x_high, 1)
                dve.tensor_tensor(xs[:, 1], xT[:, :, :], xs[:, 0].bitcast(FP32), ALU.subtract).then_inc(x_split, 1)
                d_part(0, 0)
                emit(dve, chunk)
                dve.wait_ge(d_done, chunks)
                for e in range(2):
                    dve.tensor_copy(oT[:, 1, HALF * e:HALF * e + HALF], PS[6 + e][:, 0:HALF]).then_inc(o_copied, 1)
                for t in range(NT):
                    dve.wait_ge(tr_ready, t + 1)
                    dve.scalar_tensor_tensor(x[:, t, :], PS[t % 4][:, 0:H], G["tanh"][:, 4 + l:5 + l], x[:, t, :],
                                             ALU.mult, ALU.add).then_inc(x_done, 1)


def quantised_linear(nc, G):
    PS, xT, x = G["PS"], G["xT"], G["x"]
    with Stage(nc, "fp8") as st:
        w8, wi, wm = st.sb("w8", [128, KC, H], U8), st.sb("wi", [128, KC, H], I32), st.sb("wm", [128, KC, H], I32)
        wv, w2, wb = st.sb("wv", [128, KC, H]), st.sb("w2", [128, KC, H]), st.sb("wb", [128, KC, H], BF16)
        s16, sf, ws = st.sb("s16", [128, 1], BF16), st.sb("sf", [128, 1]), st.sb("ws", [128, 1])
        rs, sw = st.sb("rs", [128, 1]), st.sb("sw", [128, 1])
        y, step, q = st.sb("y", [128, KC, T]), st.sb("step", [128, KC, T]), st.sb("q", [128, KC, T], BF16)
        in_w, chain, w_ready, q_ready, o_ready, x_done = (
            st.sem(n) for n in ("in_w", "chain", "w_ready", "q_ready", "o_ready", "x_done"))
        with nc.Block() as block:

            @block.sync
            def _(sp):
                Stage.semaphores.clear_earlier(sp)
                sp.dma_start(w8[:, :, :], G["L1_w8"]).then_inc(in_w, 16)
                sp.dma_start(s16[:, :], G["L1_in_scale"].broadcast_to([128, 1])).then_inc(in_w, 16)
                sp.dma_start(ws[:, :], G["L1_w_scale"].broadcast_to([128, 1])).then_inc(in_w, 16)

            @block.vector
            def _(dve):
                c = Count(dve, chain)
                dve.wait_ge(in_w, 48)
                c.link(dve.tensor_copy(sf[:, :], s16[:, :]))
                c.link(dve.reciprocal(rs[:, :], sf[:, :]))
                c.link(dve.tensor_tensor(sw[:, :], sf[:, :], ws[:, :], ALU.mult))
                c.link(dve.tensor_tensor(sw[:, :], sw[:, :], G["tanh"][:, 5:6], ALU.mult))
                c.link(dve.tensor_scalar(y[:, :, :], xT[:, :, :], rs[:, :], FP8_MAX, ALU.mult, ALU.min))
                c.link(dve.tensor_scalar(y[:, :, :], y[:, :, :], -FP8_MAX, None, ALU.max))
                c.link(dve.tensor_scalar(step[:, :, :].bitcast(I32), y[:, :, :].bitcast(I32), 0x7F800000, None,
                                         ALU.bitwise_and))
                c.link(dve.tensor_scalar(step[:, :, :], step[:, :, :], 2.0 ** -6, 1.5 * 2.0 ** 20, ALU.max, ALU.mult))
                c.link(dve.tensor_tensor(y[:, :, :], y[:, :, :], step[:, :, :], ALU.add))
                dve.tensor_tensor(q[:, :, :], y[:, :, :], step[:, :, :], ALU.subtract).then_inc(q_ready, 1)
                c.link(dve.tensor_copy(wi[:, :, :], w8[:, :, :]))
                c.link(dve.tensor_scalar(wm[:, :, :], wi[:, :, :], 0x7F, 20, ALU.bitwise_and, ALU.logical_shift_left))
                c.link(dve.tensor_scalar(wm[:, :, :], wm[:, :, :], 0x40000000, None, ALU.bitwise_or))
                c.link(dve.tensor_scalar(wv[:, :, :], wm[:, :, :].bitcast(FP32), 2.0 ** -8, None, ALU.mult))
                c.link(dve.tensor_scalar(w2[:, :, :], wv[:, :, :], 2.0, -2.0 ** -6, ALU.mult, ALU.add))
                c.link(dve.tensor_tensor(wv[:, :, :], wv[:, :, :], w2[:, :, :], ALU.min))
                c.link(dve.tensor_scalar(wi[:, :, :], wi[:, :, :], 0x80, None, ALU.bitwise_and))
                c.link(dve.tensor_scalar(w2[:, :, :], wi[:, :, :], -1.0 / 64, 1.0, ALU.mult, ALU.add))
                dve.tensor_tensor(wb[:, :, :], wv[:, :, :], w2[:, :, :], ALU.mult).then_inc(w_ready, 1)
                for t in range(NT):
                    dve.wait_ge(o_ready, t + 1)
                    dve.scalar_tensor_tensor(x[:, t, :], PS[t][:, 0:H], sw[:, :], x[:, t, :],
                                             ALU.mult, ALU.add).then_inc(x_done, 1)

            @block.tensor
            def _(pe):
                pe.wait_ge(q_ready, 1)
                pe.wait_ge(w_ready, 1)
                for t in range(NT):
                    for k in range(KC):
                        last = pe.matmul(PS[t][:, 0:H], q[:, k, 128 * t:128 * t + 128], wb[:, k, :],
                                         start=k == 0, stop=k == KC - 1)
                    last.then_inc(o_ready, 1)


class Banks:

    def __init__(self, tensor):
        self.all = tensor[:, :]

    def __getitem__(self, i):
        return self.all[:, 512 * i:512 * i + 512]


MOE = {
    0: (16, 4, "softmax", 19, 176),
    2: (8, 1, "sigmoid", 8, 512),
    3: (16, 4, "renormalised", 16, 224),
}
CHUNKS = {0: 25, 2: 32, 3: 28}


def program(nc, G, out):
    with ExitStack() as stack:
        def sb(name, shape, dt=FP32):
            return stack.enter_context(nc.sbuf_tensor(name, shape, dt))

        G["comb"] = nc.dram_tensor("comb_rows", [19 * 11, T], FP32, kind="Internal").ap()
        G["kvt_hi"] = nc.dram_tensor("kvt_hi", [B * D, L], FP32, kind="Internal").ap()
        G["kvt_lo"] = nc.dram_tensor("kvt_lo", [B * D, L], FP32, kind="Internal").ap()
        G["kvn"] = nc.dram_tensor("kvn", [B, KP, NC * D], FP32, kind="Internal").ap()
        G["x"], G["xT"] = sb("x", [128, NT, H]), sb("xT", [128, KC, T])
        G["ident"], G["gate"], G["tanh"] = sb("ident", [128, 128]), sb("gate", [128, 8]), sb("tanh", [128, 8])
        G["PS"] = Banks(stack.enter_context(nc.psum_tensor("banks", [128, 8 * 512], FP32)))

        Stage.semaphores = Semaphores(nc, stack)
        with Stage(nc, "layer0") as st:
            G["k0"], G["v0"] = st.sb("k0", [128, 2, T], F32R), st.sb("v0", [S, B, D])
            rotate_context(nc, G)
            attention(nc, G, 0)
        for l in range(4):
            if l:
                attention(nc, G, l)
            normalise(nc, G, f"normf{l}")
            if l == 1:
                quantised_linear(nc, G)
            else:
                E, top, kind, rows, width = MOE[l]
                group_rows = np.gcd(width, 128).item()
                route(nc, G, l, E, top, kind, rows, width // group_rows)
                experts(nc, G, l, CHUNKS[l], group_rows)
        with Stage(nc, "store") as st:
            stored = st.sem("stored")
            with nc.Block() as block:

                @block.sync
                def _(sp):
                    Stage.semaphores.clear_earlier(sp)
                    sp.dma_start(out, G["x"][:, :, :]).then_inc(stored, 16)
                    sp.wait_ge(stored, 16)


def attention(nc, G, l):
    normalise(nc, G, f"norma{l}")
    with Stage(nc, f"keep{l}") as keep:
        Bm = keep.sb("B", [128, NP, H])
        q_all = keep.sb("q", [128, B, NH, S], F32R)
        with Stage(nc, f"mats{l}") as st:
            if l == 2:
                Q, N = st.sb("Q", [128, NH, KC, CQ]), st.sb("N", [CQH, 2, NH, D])
                fold_latent(nc, G, l, None, Bm, Q, N)
                rotated_queries(nc, G, Q, N, q_all)
            else:
                A = st.sb("A", [128, KC, NH, D])
                if l:
                    fold_latent(nc, G, l, A, Bm)
                else:
                    fold_small(nc, G, A, Bm)
                queries(nc, G, l, A, q_all)
        with Stage(nc, f"ctx{l}") as st:
            ctxT = st.sb("ctxT", [128, NP, T])
            if l:
                attend_long(nc, G, l, q_all, ctxT)
            else:
                attend_short(nc, G, q_all, ctxT)
            project_out(nc, G, l, Bm, ctxT)


def rope_tables(length, dim):
    inv = (1.0 / np.float32(10000.0) ** (np.arange(0, dim, 2, dtype=np.float32) / np.float32(dim))).astype(np.float32)
    f = np.arange(length, dtype=np.float32)[:, None] * inv[None, :]
    cos, sin = np.repeat(np.cos(f), 2, axis=-1), np.repeat(np.sin(f), 2, axis=-1)
    sign = np.where(np.arange(dim) < dim // 2, -1.0, 1.0).astype(np.float32)
    return cos, sin * sign


def laid_out(i):
    c = np.ascontiguousarray
    ctx = i["ctx_512"]
    swapped = np.concatenate([ctx[..., D // 2:], ctx[..., :D // 2]], axis=-1)

    def by_width(a):
        return c(a.transpose(0, 2, 1).reshape(B * D, L))

    def by_key(a):
        return c(a.reshape(B, NC, KP, D).transpose(0, 2, 1, 3).reshape(B, KP, NC * D))

    cos, sin = rope_tables(L, D)
    cosq, sinq = rope_tables(S, CQ)
    a = {
        "x_in": c(i["x"].reshape(NT, 128, H).transpose(1, 0, 2)),
        "ctxT": by_width(ctx), "ctxTs": by_width(swapped), "ctxN": by_key(ctx), "ctxNs": by_key(swapped),
        "cosT": c(np.tile(cos.T, (2, 1))), "sinT": c(np.tile(sin.T, (2, 1))),
        "cosN": by_key(np.broadcast_to(cos, (B, L, D)))[0], "sinN": by_key(np.broadcast_to(sin, (B, L, D)))[0],
        "cosQ": c(cosq.T.reshape(2, CQH, S).transpose(1, 0, 2)), "sinQ": c(sinq.T.reshape(2, CQH, S).transpose(1, 0, 2)),
        "ctx0T": c(ctx[:, :S].transpose(2, 0, 1).reshape(D, T)), "ctx0N": c(ctx[:, :S].transpose(1, 0, 2)),
        "ident_in": np.eye(128, dtype=np.float32),
        "g_xattn": c(i["g_xattn"].reshape(1, 4)), "g_ffn": c(i["g_ffn"].reshape(1, 4)),
    }
    row = np.arange(NH * S).reshape(NT, 128).T % S
    a["mask0"] = np.where(np.arange(S) <= row[:, :, None], 0.0, np.finfo(np.float32).min).astype(np.float32)
    for E in (8, 16):
        a[f"tie{E}"] = c(np.broadcast_to((np.arange(E)[None, :] < np.arange(E)[:, None]).astype(np.float32)
                                         .reshape(1, E * E), (128, E * E)))
    HD = H // NH
    wkv = i["L0_xattn_Wkv_expand"]
    a["L0_wq"] = c(i["L0_xattn_Wq"].reshape(NH, HD, H).transpose(1, 0, 2))
    a["L0_wk"] = c(wkv[:H].reshape(NH, HD, D).transpose(1, 0, 2))
    a["L0_wv"] = c(wkv[H:].reshape(NH, HD, D).transpose(1, 0, 2))
    a["L0_wo"] = c(i["L0_xattn_Wout"].T.reshape(NH, HD, H).transpose(1, 0, 2))
    for l in (1, 2, 3):
        w = {n: i[f"L{l}_xattn_{n}"] for n in ("Wq", "w_kc_q", "w_kc_kv", "W_qr", "W_kr", "Wo")}
        a[f"L{l}_wq"] = c(w["Wq"].reshape(NH, K, H).transpose(1, 0, 2))
        a[f"L{l}_wqr"] = c(w["W_qr"].transpose(2, 0, 1))
        a[f"L{l}_wkr"] = c(w["W_kr"].transpose(2, 0, 1))
        a[f"L{l}_wv"] = c(w["w_kc_kv"].transpose(1, 0, 2))
        a[f"L{l}_wo"] = c(w["Wo"].T.reshape(NH, K, H).transpose(1, 0, 2))
        if l == 2:
            a["L2_wc"] = c(w["w_kc_q"].transpose(1, 0, 2))
        else:
            a[f"L{l}_wc"] = c(w["w_kc_q"].reshape(NH, K, 2, CQH).transpose(3, 2, 0, 1))

    def expert_chunks(gate, up, down, chunks):
        pad = [(0, chunks * 128 - gate.shape[0]), (0, 0)]
        gate, up, down = (np.pad(m, pad) for m in (gate, up, down))
        def stationary(m):
            return m.reshape(chunks, 128, KC, 128).transpose(0, 3, 2, 1).reshape(chunks * 128, KC * 128)
        return c(np.concatenate([stationary(gate), stationary(up), down], axis=1))

    a["L0_experts"] = expert_chunks(
        np.concatenate([i["L0_ffn_W1"].reshape(-1, H), i["L0_ffn_W1s"]]),
        np.concatenate([i["L0_ffn_W3"].reshape(-1, H), i["L0_ffn_W3s"]]),
        np.concatenate([i["L0_ffn_W2"].transpose(0, 2, 1).reshape(-1, H), i["L0_ffn_W2s"].T]), CHUNKS[0])
    for l, (g, u, d) in {2: ("gate_w", "up_w", "down_w"), 3: ("gate_proj", "up_proj", "down_proj")}.items():
        a[f"L{l}_experts"] = expert_chunks(i[f"L{l}_ffn_{g}"].transpose(0, 2, 1).reshape(-1, H),
                                           i[f"L{l}_ffn_{u}"].transpose(0, 2, 1).reshape(-1, H),
                                           i[f"L{l}_ffn_{d}"].reshape(-1, H), CHUNKS[l])

    def router(w):
        return c(w.reshape(KC, 128, -1).transpose(1, 0, 2))

    a["L0_router"], a["L2_router"] = router(i["L0_ffn_Wg"].T), router(i["L2_ffn_router_w"])
    a["L3_router"], a["L3_bias"] = router(i["L3_ffn_router_w"].T), c(i["L3_ffn_expert_bias"].reshape(1, -1))
    a["L1_w8"] = c(i["L1_ffn_weight"].view(np.uint8).T.reshape(KC, 128, H).transpose(1, 0, 2))
    a["L1_in_scale"] = c(i["L1_ffn_input_scale"].reshape(1, 1))
    a["L1_w_scale"] = c(i["L1_ffn_weight_scale"].reshape(1, 1))
    return a


def kernel(**inputs):
    import concourse.bacc as bacc
    from concourse.bass_utils import run_bass_kernel_spmd

    nc = bacc.Bacc("TRN2", target_bir_lowering=False, num_devices=1)
    arrays, G = {}, {}
    for name, a in laid_out({k: np.asarray(v) for k, v in inputs.items()}).items():
        arrays[f"{name}_dram"] = a
        G[name] = nc.dram_tensor(f"{name}_dram", a.shape, mybir.dt.from_np(a.dtype), kind="ExternalInput").ap()
    out = nc.dram_tensor("out_dram", (128, NT, H), FP32, kind="ExternalOutput").ap()
    program(nc, G, out)
    r = run_bass_kernel_spmd(nc, [arrays], core_ids=[0])
    return np.ascontiguousarray(r.results[0]["out_dram"].transpose(1, 0, 2)).reshape(B, S, H)
```

```python
from contextlib import ExitStack

import numpy as np
import concourse.bass as bass
from concourse import mybir

FP32 = mybir.dt.float32
F32R = mybir.dt.float32r
BF16 = mybir.dt.bfloat16
U8 = mybir.dt.uint8
I32 = mybir.dt.int32
ALU = mybir.AluOpType
ACT = mybir.ActivationFunctionType
AX = mybir.AxisListType

B, S, H, L, D = 16, 56, 256, 1500, 64
NH, K, CQ = 16, 128, 192
T = B * S
NT = T // 128
KC = H // 128
HALF = T // 2
NP = NH // 2
KP = 125
NC = L // KP
SB = 500
NS = L // SB
CG = NC // NS
CQH = CQ // 2
EPS = 1e-5
FP8_MAX = 448.0


class Count:

    def __init__(self, eng, sem):
        self.eng, self.sem, self.n = eng, sem, 0

    def mark(self, ins):
        self.n += 1
        ins.then_inc(self.sem, 1)

    def link(self, ins):
        self.mark(ins)
        self.eng.wait_ge(self.sem, self.n)


class Semaphores:

    EACH = 26

    def __init__(self, nc, stack):
        self.sets = [[stack.enter_context(nc.semaphore(f"set{i}_{n}")) for n in range(self.EACH)] for i in range(2)]
        self.used, self.turn = [0, 0], 0

    def start(self):
        self.turn = 1 - self.turn
        self.used[self.turn] = 0

    def take(self):
        n = self.used[self.turn]
        self.used[self.turn] = n + 1
        return self.sets[self.turn][n]

    def clear_earlier(self, sp):
        for sem in self.sets[1 - self.turn][:self.used[1 - self.turn]]:
            sp.sem_clear(sem)


class Stage:

    semaphores = None

    def __init__(self, nc, name):
        self.nc, self.name, self.stack, self.started = nc, name, ExitStack(), False

    def __enter__(self):
        self.stack.__enter__()
        return self

    def __exit__(self, *a):
        return self.stack.__exit__(*a)

    def sb(self, name, shape, dt=FP32):
        return self.stack.enter_context(self.nc.sbuf_tensor(f"{self.name}_{name}", shape, dt))

    def sem(self, name):
        if not self.started:
            self.started = True
            self.semaphores.start()
        return self.semaphores.take()


def from_first(eng, steps, step):
    step(0, True)
    with eng.Fori(1, steps) as i:
        step(i, False)


def rotate_context(nc, G):
    with Stage(nc, "rot") as st:
        cosT, sinT = st.sb("cosT", [128, L]), st.sb("sinT", [128, L])
        cosN, sinN = st.sb("cosN", [KP, NC * D]), st.sb("sinN", [KP, NC * D])
        ct, cs = st.sb("ct", [128, 2, L]), st.sb("cs", [128, 2, L])
        hi, lo = st.sb("hi", [128, 2, L], F32R), st.sb("lo", [128, 2, L], F32R)
        cn, cm = st.sb("cn", [KP, 2, 2, NC * D]), st.sb("cm", [KP, 2, 2, NC * D])
        vs = st.sb("vs", [KP, 2, 2, NC, 2, D], F32R)
        tables = st.sem("tables")
        gates_in = st.sem("gates_in")
        in_t = [st.sem(f"in_t{s}") for s in range(2)]
        in_n = [st.sem(f"in_n{s}") for s in range(2)]
        sin_done, mul_done, sum_t, hi_done, lo_done, sum_n, high_n, low_n = (
            st.sem(n) for n in ("sin_done", "mul_done", "sum_t", "hi_done", "lo_done", "sum_n", "high_n", "low_n"))
        out_t = [st.sem(f"out_t{s}") for s in range(2)]
        out_n = [st.sem(f"out_n{s}") for s in range(2)]
        gates_done = st.sem("gates_done")
        k0_in, k0_done = st.sem("k0_in"), st.sem("k0_done")
        k0 = st.sb("k0", [128, T])
        with nc.Block() as block:

            @block.sync
            def _(sp):
                Stage.semaphores.clear_earlier(sp)
                for dst, src in ((cosT, "cosT"), (sinT, "sinT"), (cosN, "cosN"), (sinN, "sinN")):
                    sp.dma_start(dst[:, :], G[src]).then_inc(tables, 16)

                def step(i, first):
                    for s in range(2):
                        if not first:
                            sp.wait_ge(lo_done, i * 2 + s - 1)
                        rows = bass.ds(i * 256 + s * 128, 128)
                        sp.dma_start(ct[:, s, :], G["ctxT"][rows, :]).then_inc(in_t[s], 16)
                        sp.dma_start(cs[:, s, :], G["ctxTs"][rows, :]).then_inc(in_t[s], 16)
                        if not first:
                            sp.wait_ge(low_n, i * 2 + s - 1)
                        pair = bass.ds(i * 4 + 2 * s, 2)
                        sp.dma_start(cn[:, s], G["ctxN"][pair].rearrange("b p n -> p b n")).then_inc(in_n[s], 16)
                        sp.dma_start(cm[:, s], G["ctxNs"][pair].rearrange("b p n -> p b n")).then_inc(in_n[s], 16)

                from_first(sp, B // 4, step)

            @block.gpsimd
            def _(pool):
                pool.wait_ge(tables, 64)
                with pool.Fori(0, B // 4) as i:
                    for s in range(2):
                        pool.wait_ge(in_t[s], i * 32 + 32)
                        pool.tensor_tensor(cs[:, s, :], cs[:, s, :], sinT[:, :], ALU.mult).then_inc(sin_done, 1)
                        pool.wait_ge(in_n[s], i * 32 + 32)
                        pool.tensor_tensor(cm[:, s], cm[:, s], sinN[:, :].unsqueeze(1).broadcast_to([KP, 2, NC * D]),
                                           ALU.mult).then_inc(sin_done, 1)

            @block.vector
            def _(dve):
                dve.wait_ge(tables, 64)

                def step(i, first):
                    for s in range(2):
                        n = i * 2 + s
                        dve.wait_ge(in_t[s], i * 32 + 32)
                        dve.tensor_tensor(ct[:, s, :], ct[:, s, :], cosT[:, :], ALU.mult).then_inc(mul_done, 1)
                        dve.wait_ge(in_n[s], i * 32 + 32)
                        dve.tensor_tensor(cn[:, s], cn[:, s], cosN[:, :].unsqueeze(1).broadcast_to([KP, 2, NC * D]),
                                          ALU.mult).then_inc(mul_done, 1)
                        dve.wait_ge(mul_done, n * 2 + 2)
                        dve.wait_ge(sin_done, n * 2 + 2)
                        dve.tensor_tensor(ct[:, s, :], ct[:, s, :], cs[:, s, :], ALU.add).then_inc(sum_t, 1)
                        dve.tensor_tensor(cn[:, s], cn[:, s], cm[:, s], ALU.add).then_inc(sum_n, 1)
                        dve.wait_ge(high_n, n + 1)
                        if not first:
                            dve.wait_ge(out_n[s], i * 16)
                        halves = cn[:, s].rearrange("p b (c d) -> p (b c) d", d=D)
                        parts = vs[:, s].rearrange("p b c h d -> p (b c) h d")
                        dve.tensor_tensor(parts[:, :, 1, :], halves, parts[:, :, 0, :].bitcast(FP32),
                                          ALU.subtract).then_inc(low_n, 1)
                        dve.wait_ge(hi_done, n + 1)
                        if not first:
                            dve.wait_ge(out_t[s], i * 32)
                        dve.tensor_tensor(lo[:, s, :], ct[:, s, :], hi[:, s, :].bitcast(FP32),
                                          ALU.subtract).then_inc(lo_done, 1)

                from_first(dve, B // 4, step)
                dve.wait_ge(k0_in, 48)
                dve.tensor_copy(G["k0"][:, 0, :], k0[:, :]).then_inc(k0_done, 1)
                dve.wait_ge(k0_done, 1)
                dve.tensor_tensor(G["k0"][:, 1, :], k0[:, :], G["k0"][:, 0, :].bitcast(FP32),
                                  ALU.subtract).then_inc(k0_done, 1)

            @block.scalar
            def _(act):
                act.dma_start(k0[0:64, :], G["ctx0T"]).then_inc(k0_in, 16)
                act.dma_start(k0[64:128, :], G["ctx0T"]).then_inc(k0_in, 16)
                act.dma_start(G["v0"][:, :, :], G["ctx0N"]).then_inc(k0_in, 16)
                act.dma_start(G["x"][:, :, :], G["x_in"]).then_inc(gates_in, 16)
                act.dma_start(G["ident"][:, :], G["ident_in"]).then_inc(gates_in, 16)
                act.dma_start(G["gate"][:, 0:4], G["g_xattn"].broadcast_to([128, 4])).then_inc(gates_in, 16)
                act.dma_start(G["gate"][:, 4:8], G["g_ffn"].broadcast_to([128, 4])).then_inc(gates_in, 16)
                act.wait_ge(gates_in, 64)
                act.activation(G["tanh"][:, :], G["gate"][:, :], ACT.Tanh).then_inc(gates_done, 1)

                def step(i, first):
                    for s in range(2):
                        n = i * 2 + s
                        if not first:
                            act.wait_ge(out_t[s], i * 32)
                        act.wait_ge(sum_t, n + 1)
                        act.activation(hi[:, s, :], ct[:, s, :], ACT.Copy).then_inc(hi_done, 1)
                        act.wait_ge(sum_n, n + 1)
                        if not first:
                            act.wait_ge(out_n[s], i * 16)
                        act.activation(vs[:, s].rearrange("p b c h d -> p (b c) h d")[:, :, 0, :],
                                       cn[:, s].rearrange("p b (c d) -> p (b c) d", d=D), ACT.Copy).then_inc(high_n, 1)
                        act.wait_ge(low_n, n + 1)
                        act.dma_start(G["kvn"][bass.ds(i * 4 + 2 * s, 2)].rearrange("b p n -> p b n"),
                                      vs[:, s].rearrange("p b c h d -> p b (c h d)").bitcast(FP32)).then_inc(out_n[s], 16)
                        act.wait_ge(lo_done, n + 1)
                        rows = bass.ds(i * 256 + s * 128, 128)
                        act.dma_start(G["kvt_hi"][rows, :], hi[:, s, :].bitcast(FP32)).then_inc(out_t[s], 16)
                        act.dma_start(G["kvt_lo"][rows, :], lo[:, s, :].bitcast(FP32)).then_inc(out_t[s], 16)

                from_first(act, B // 4, step)
                for s in range(2):
                    act.wait_ge(out_t[s], B // 4 * 32)
                    act.wait_ge(out_n[s], B // 4 * 16)


def normalise(nc, G, name):
    x, xT, PS, ident = G["x"], G["xT"], G["PS"], G["ident"]
    with Stage(nc, name) as st:
        stats, mv = st.sb("stats", [128, NT, 6]), st.sb("mv", [128, NT, 2])
        ve, sd, r, t = (st.sb(n, [128, NT]) for n in ("ve", "sd", "r", "t"))
        xn = st.sb("xn", [128, NT, H])
        chain, var_ready, sqrt_done, xn_ready, tr_done, copied = (
            st.sem(n) for n in ("chain", "var_ready", "sqrt_done", "xn_ready", "tr_done", "copied"))
        with nc.Block() as block:

            @block.sync
            def _(sp):
                Stage.semaphores.clear_earlier(sp)

            @block.vector
            def _(dve):
                c = Count(dve, chain)
                for i in range(NT):
                    c.mark(dve.bn_stats(stats[:, i, :], x[:, i, :]))
                for i in range(NT):
                    dve.wait_ge(chain, i + 1)
                    c.mark(dve.bn_aggr(mv[:, i, :], stats[:, i, :]))
                dve.wait_ge(chain, c.n)
                dve.tensor_scalar(ve[:, :], mv[:, :, 1], EPS, None, ALU.add).then_inc(var_ready, 1)
                dve.wait_ge(sqrt_done, 1)
                c.link(dve.reciprocal(r[:, :], sd[:, :]))
                c.link(dve.tensor_tensor(t[:, :], r[:, :], r[:, :], ALU.mult))
                c.link(dve.tensor_tensor(t[:, :], t[:, :], ve[:, :], ALU.mult))
                c.link(dve.tensor_scalar(t[:, :], t[:, :], -0.5, 1.5, ALU.mult, ALU.add))
                c.link(dve.tensor_tensor(r[:, :], r[:, :], t[:, :], ALU.mult))
                for i in range(NT):
                    dve.tensor_scalar(xn[:, i, :], x[:, i, :], mv[:, i, 0:1], r[:, i:i + 1],
                                      ALU.subtract, ALU.mult).then_inc(xn_ready, 1)

            @block.scalar
            def _(act):
                act.wait_ge(var_ready, 1)
                act.activation(sd[:, :], ve[:, :], ACT.Sqrt).then_inc(sqrt_done, 1)
                for i in range(NT):
                    act.wait_ge(tr_done, i + 1)
                    act.activation(xT[:, :, 128 * i:128 * i + 128],
                                   PS[i][:, 0:256].rearrange("p (k n) -> p k n", k=KC), ACT.Copy).then_inc(copied, 1)

            @block.tensor
            def _(pe):
                for i in range(NT):
                    pe.wait_ge(xn_ready, i + 1)
                    for k in range(KC):
                        last = pe.transpose(PS[i][:, 128 * k:128 * k + 128], xn[:, i, 128 * k:128 * k + 128],
                                            ident[:, :])
                    last.then_inc(tr_done, 1)


def fold_small(nc, G, A, Bm):
    PS = G["PS"]
    HD = H // NH
    with Stage(nc, "fold0") as st:
        wq, wk = st.sb("wq", [HD, NH, H]), st.sb("wk", [HD, NH, D])
        wv, wo = st.sb("wv", [HD, NH, D]), st.sb("wo", [HD, NH, H])
        w_in, a_ready, b_ready, a_done, b_done = (
            st.sem(n) for n in ("w_in", "a_ready", "b_ready", "a_done", "b_done"))
        with nc.Block() as block:

            @block.sync
            def _(sp):
                Stage.semaphores.clear_earlier(sp)
                for dst, src in ((wq, "L0_wq"), (wk, "L0_wk"), (wv, "L0_wv"), (wo, "L0_wo")):
                    sp.dma_start(dst[:, :, :], G[src]).then_inc(w_in, 16)

            @block.tensor
            def _(pe):
                pe.wait_ge(w_in, 64)
                for g in range(4):
                    for h in range(4 * g, 4 * g + 4):
                        for k in range(KC):
                            o = (k * 4 + h % 4) * D
                            last = pe.matmul(PS[g][:, o:o + D], wq[:, h, 128 * k:128 * k + 128], wk[:, h, :],
                                             start=True, stop=True)
                    last.then_inc(a_ready, 1)
                for g in range(4):
                    for h in range(4 * g, 4 * g + 4):
                        o = h % 4 // 2 * H
                        last = pe.matmul(PS[4 + g][h % 2 * 64:h % 2 * 64 + 64, o:o + H], wv[:, h, :], wo[:, h, :],
                                         start=True, stop=True)
                    last.then_inc(b_ready, 1)

            @block.scalar
            def _(act):
                for g in range(4):
                    act.wait_ge(a_ready, g + 1)
                    act.activation(A[:, :, 4 * g:4 * g + 4, :],
                                   PS[g][:, :].rearrange("p (k h d) -> p k h d", k=KC, h=4),
                                   ACT.Copy).then_inc(a_done, 1)

            @block.vector
            def _(dve):
                for g in range(4):
                    dve.wait_ge(b_ready, g + 1)
                    dve.tensor_copy(Bm[:, 2 * g:2 * g + 2, :],
                                    PS[4 + g][:, :].rearrange("p (h n) -> p h n", h=2)).then_inc(b_done, 1)


def fold_latent(nc, G, l, A, Bm, Q=None, N=None):
    PS = G["PS"]
    rotated = Q is not None
    with Stage(nc, f"fold{l}") as st:
        wq = st.sb("wq", [K, NH, H])
        wqr, wkr = st.sb("wqr", [D, NH, CQ]), st.sb("wkr", [D, NH, D])
        wv, wo = st.sb("wv", [K, NH, D]), st.sb("wo", [K, NH, H])
        wc = st.sb("wc", [K, NH, CQ]) if rotated else st.sb("wc", [CQH, 2, NH, K])
        M = None if rotated else st.sb("M", [K, NH, D])
        Nn = N if rotated else st.sb("N", [CQH, 2, NH, D])
        in_n, in_b, in_q, n_ready, b_ready, m_ready, a_ready = (
            st.sem(n) for n in ("in_n", "in_b", "in_q", "n_ready", "b_ready", "m_ready", "a_ready"))
        n_done, b_done, m_done, a_done = (st.sem(n) for n in ("n_done", "b_done", "m_done", "a_done"))
        with nc.Block() as block:

            @block.sync
            def _(sp):
                Stage.semaphores.clear_earlier(sp)
                sp.dma_start(wqr[:, :, :], G[f"L{l}_wqr"]).then_inc(in_n, 16)
                sp.dma_start(wkr[:, :, :], G[f"L{l}_wkr"]).then_inc(in_n, 16)
                sp.dma_start(wc[:], G[f"L{l}_wc"]).then_inc(in_q, 16)
                sp.dma_start(wq[:, :, :], G[f"L{l}_wq"]).then_inc(in_q, 16)

            @block.tensor
            def _(pe):
                pe.wait_ge(in_n, 32)
                for g in range(4):
                    for h in range(4 * g, 4 * g + 4):
                        for c in range(2):
                            o = (c * 4 + h % 4) * D
                            last = pe.matmul(PS[g][0:CQH, o:o + D], wqr[:, h, CQH * c:CQH * c + CQH], wkr[:, h, :],
                                             start=True, stop=True)
                    last.then_inc(n_ready, 1)
                pe.wait_ge(in_b, 32)
                for g in range(4):
                    for h in range(4 * g, 4 * g + 4):
                        o = h % 4 // 2 * H
                        last = pe.matmul(PS[4 + g][h % 2 * 64:h % 2 * 64 + 64, o:o + H], wv[:, h, :], wo[:, h, :],
                                         start=True, stop=True)
                    last.then_inc(b_ready, 1)
                pe.wait_ge(in_q, 32)
                if rotated:
                    for h in range(NH):
                        if h < 4:
                            pe.wait_ge(n_done, h + 1)
                        else:
                            pe.wait_ge(a_done, h - 3)
                        for k in range(KC):
                            last = pe.matmul(PS[h % 4][:, k * CQ:k * CQ + CQ], wq[:, h, 128 * k:128 * k + 128],
                                             wc[:, h, :], start=True, stop=True)
                        last.then_inc(a_ready, 1)
                    return
                for g in range(2):
                    pe.wait_ge(n_done, 4)
                    for h in range(8 * g, 8 * g + 8):
                        for c in range(2):
                            last = pe.matmul(PS[g][:, h % 8 * D:h % 8 * D + D], wc[:, c, h, :], Nn[:, c, h, :],
                                             start=c == 0, stop=c == 1)
                    last.then_inc(m_ready, 1)
                for g in range(4):
                    pe.wait_ge(m_done, g // 2 + 1)
                    pe.wait_ge(b_done, g + 1)
                    for h in range(4 * g, 4 * g + 4):
                        for k in range(KC):
                            o = (k * 4 + h % 4) * D
                            last = pe.matmul(PS[4 + g][:, o:o + D], wq[:, h, 128 * k:128 * k + 128], M[:, h, :],
                                             start=True, stop=True)
                    last.then_inc(a_ready, 1)

            @block.scalar
            def _(act):
                act.dma_start(wv[:, :, :], G[f"L{l}_wv"]).then_inc(in_b, 16)
                act.dma_start(wo[:, :, :], G[f"L{l}_wo"]).then_inc(in_b, 16)
                for g in range(4):
                    act.wait_ge(n_ready, g + 1)
                    act.activation(Nn[:, :, 4 * g:4 * g + 4, :],
                                   PS[g][0:CQH, :].rearrange("p (c h d) -> p c h d", c=2, h=4),
                                   ACT.Copy).then_inc(n_done, 1)
                if rotated:
                    for h in range(NH):
                        act.wait_ge(a_ready, h + 1)
                        act.activation(Q[:, h, :, :], PS[h % 4][:, 0:KC * CQ].rearrange("p (k q) -> p k q", k=KC),
                                       ACT.Copy).then_inc(a_done, 1)
                    return
                for g in range(2):
                    act.wait_ge(m_ready, g + 1)
                    act.activation(M[:, 8 * g:8 * g + 8, :], PS[g][:, :].rearrange("p (h d) -> p h d", h=8),
                                   ACT.Copy).then_inc(m_done, 1)
                for g in range(4):
                    act.wait_ge(a_ready, g + 1)
                    act.activation(A[:, :, 4 * g:4 * g + 4, :],
                                   PS[4 + g][:, :].rearrange("p (k h d) -> p k h d", k=KC, h=4),
                                   ACT.Copy).then_inc(a_done, 1)

            @block.vector
            def _(dve):
                for g in range(4):
                    dve.wait_ge(b_ready, g + 1)
                    dve.tensor_copy(Bm[:, 2 * g:2 * g + 2, :],
                                    PS[4 + g][:, :].rearrange("p (h n) -> p h n", h=2)).then_inc(b_done, 1)


def queries(nc, G, l, A, q_all):
    PS, xT = G["PS"], G["xT"]
    with Stage(nc, f"q{l}") as st:
        q_ready, hi_done, lo_done = (st.sem(n) for n in ("q_ready", "hi_done", "lo_done"))
        groups = [(p, e) for p in range(NP) for e in range(2)]
        with nc.Block() as block:

            @block.tensor
            def _(pe):
                for n, (p, e) in enumerate(groups):
                    if n >= 4:
                        pe.wait_ge(lo_done, 2 * (n - 3))
                    for k in range(KC):
                        last = pe.matmul(PS[n % 4][:, 0:HALF],
                                         A[:, k, 2 * p:2 * p + 2, :].rearrange("p h d -> p (h d)"),
                                         xT[:, k, HALF * e:HALF * e + HALF], start=k == 0, stop=k == KC - 1)
                    last.then_inc(q_ready, 1)

            split_queries(block, PS, q_all, groups, q_ready, hi_done, lo_done)
            store_queries(block, G, q_all, groups, lo_done, st.sem("stored"))


def store_queries(block, G, q_all, groups, lo_done, stored):
    @block.sync
    def _(sp):
        Stage.semaphores.clear_earlier(sp)
        store_groups(sp, G, q_all, groups, lo_done, stored)


def store_groups(sp, G, q_all, groups, lo_done, stored):
    for n, (p, e) in enumerate(groups):
        sp.wait_ge(lo_done, 2 * n + 2)
        b0, c0 = B // 2 * e, 2 * p * S
        sp.dma_start(G["q"][b0:b0 + B // 2, :, c0:c0 + 2 * S].rearrange("b p n -> p b n"),
                     q_all[:, b0:b0 + B // 2, 2 * p:2 * p + 2, :].rearrange("p b h s -> p b (h s)").bitcast(FP32)
                     ).then_inc(stored, 16)
    sp.wait_ge(stored, 16 * len(groups))


def split_queries(block, PS, q_all, groups, q_ready, hi_done, lo_done):
    def places(n, p, e, odd):
        src = PS[n % 4][64 * odd:64 * odd + 64, 0:HALF].rearrange("p (b s) -> p b s", s=S)
        b0 = B // 2 * e
        return src, q_all[0:64, b0:b0 + B // 2, 2 * p + odd, :], q_all[64:128, b0:b0 + B // 2, 2 * p + odd, :]

    @block.scalar
    def _(act):
        for n, (p, e) in enumerate(groups):
            act.wait_ge(q_ready, n + 1)
            for odd in range(2):
                src, hi, _ = places(n, p, e, odd)
                act.activation(hi, src, ACT.Copy).then_inc(hi_done, 1)

    @block.vector
    def _(dve):
        for n, (p, e) in enumerate(groups):
            dve.wait_ge(hi_done, 2 * n + 2)
            for odd in range(2):
                src, hi, lo = places(n, p, e, odd)
                dve.tensor_tensor(lo, src, hi.bitcast(FP32), ALU.subtract).then_inc(lo_done, 1)


def rotated_queries(nc, G, Q, N, q_all):
    PS, xT = G["PS"], G["xT"]
    with Stage(nc, "q2") as st:
        cos, sin = st.sb("cos", [CQH, 2, S]), st.sb("sin", [CQH, 2, S])
        tc, ts = st.sb("tc", [CQH, 2, 2, HALF]), st.sb("ts", [CQH, 2, 2, HALF])
        tables, big_ready, mul_done, rot_done, q_ready, hi_done, lo_done = (
            st.sem(n) for n in ("tables", "big_ready", "mul_done", "rot_done", "q_ready", "hi_done", "lo_done"))
        stored = st.sem("stored")
        units = [(p, e, odd) for p in range(NP) for e in range(2) for odd in range(2)]
        with nc.Block() as block:

            @block.sync
            def _(sp):
                Stage.semaphores.clear_earlier(sp)
                sp.dma_start(cos[:, :, :], G["cosQ"]).then_inc(tables, 16)
                sp.dma_start(sin[:, :, :], G["sinQ"]).then_inc(tables, 16)
                store_groups(sp, G, q_all, [(p, e) for p, e, odd in units if not odd], lo_done, stored)

            @block.tensor
            def _(pe):
                def big(u):
                    p, e, odd = units[u]
                    if u >= 2:
                        pe.wait_ge(mul_done, 4 * (u - 1))
                    for c in range(2):
                        for k in range(KC):
                            last = pe.matmul(PS[4 + u % 2 * 2 + c][0:CQH, 0:HALF],
                                             Q[:, 2 * p + odd, k, CQH * c:CQH * c + CQH],
                                             xT[:, k, HALF * e:HALF * e + HALF], start=k == 0, stop=k == KC - 1)
                    last.then_inc(big_ready, 1)

                def small(u):
                    p, e, odd = units[u]
                    g = u // 2
                    if g >= 4 and not odd:
                        pe.wait_ge(lo_done, 2 * (g - 3))
                    pe.wait_ge(rot_done, u + 1)
                    for c in range(2):
                        last = pe.matmul(PS[g % 4][64 * odd:64 * odd + 64, 0:HALF], N[:, c, 2 * p + odd, :],
                                         tc[:, u % 2, c, :], start=c == 0, stop=c == 1)
                    last.then_inc(q_ready, 1)

                for u in range(len(units) + 1):
                    if u < len(units):
                        big(u)
                    if u:
                        small(u - 1)

            def places(g, odd):
                p, e, _ = units[2 * g + odd]
                src = PS[g % 4][64 * odd:64 * odd + 64, 0:HALF].rearrange("p (b s) -> p b s", s=S)
                b0 = B // 2 * e
                return src, q_all[0:64, b0:b0 + B // 2, 2 * p + odd, :], q_all[64:128, b0:b0 + B // 2, 2 * p + odd, :]

            @block.scalar
            def _(act):
                for g in range(len(units) // 2):
                    act.wait_ge(q_ready, 2 * g + 2)
                    for odd in range(2):
                        src, hi, _ = places(g, odd)
                        act.activation(hi, src, ACT.Copy).then_inc(hi_done, 1)

            @block.vector
            def _(dve):
                def lows(g):
                    dve.wait_ge(hi_done, 2 * g + 2)
                    for odd in range(2):
                        src, hi, lo = places(g, odd)
                        dve.tensor_tensor(lo, src, hi.bitcast(FP32), ALU.subtract).then_inc(lo_done, 1)

                dve.wait_ge(tables, 32)
                for u in range(len(units)):
                    dve.wait_ge(big_ready, u + 1)
                    if u >= 2:
                        dve.wait_ge(q_ready, u - 1)
                    for c in range(2):
                        src = PS[4 + u % 2 * 2 + c][0:CQH, 0:HALF].rearrange("p (b s) -> p b s", s=S)
                        for dst, tab in ((tc[:, u % 2, c, :], cos[:, c, :]), (ts[:, u % 2, 1 - c, :], sin[:, 1 - c, :])):
                            dve.tensor_tensor(dst.rearrange("p (b s) -> p b s", s=S), src,
                                              tab.unsqueeze(1).broadcast_to([CQH, B // 2, S]),
                                              ALU.mult).then_inc(mul_done, 1)
                    if u >= 3 and u % 2:
                        lows((u - 3) // 2)
                lows(len(units) // 2 - 1)

            @block.gpsimd
            def _(pool):
                for u in range(len(units)):
                    pool.wait_ge(mul_done, 4 * u + 4)
                    pool.tensor_tensor(tc[:, u % 2], tc[:, u % 2], ts[:, u % 2], ALU.add).then_inc(rot_done, 1)


def attend_short(nc, G, q_all, ctxT):
    PS, ident, k0, v0 = G["PS"], G["ident"], G["k0"], G["v0"]
    SCALE = float(H // NH) ** -0.5
    W0 = 4 * 128
    with Stage(nc, "att0") as st:
        mask = st.sb("mask", [128, NT, S])
        qst = st.sb("qst", [128, 2, NH * S], F32R)
        pw = st.sb("p", [128, 2, (NT - 1) * S + 128])
        pT = st.sb("pT", [S, 2, T])
        mx, rs = st.sb("mx", [128, 2, NT]), st.sb("rs", [128, 2, NT])
        p = [pw[:, s, 0:NT * S].rearrange("p (t k) -> p t k", t=NT) for s in range(2)]
        oc = st.sb("oc", [128, 2, NT + 1, D])
        cT = st.sb("cT", [D, 2, NH, S])
        pad_done = st.sem("pad_done")
        mask_in, s_ready, masked, maxed, centred, exp_done, summed, inverted = (
            st.sem(n) for n in ("mask_in", "s_ready", "masked", "maxed", "centred", "exp_done", "summed", "inverted"))
        q_in = [st.sem(f"q_in{s}") for s in range(2)]
        t_ready, t_copied, o_ready, o_scaled, c_ready, c_copied, placed = (
            st.sem(n) for n in ("t_ready", "t_copied", "o_ready", "o_scaled", "c_ready", "c_copied", "placed"))
        with nc.Block() as block:

            @block.sync
            def _(sp):
                Stage.semaphores.clear_earlier(sp)
                sp.dma_start(mask[:, :, :], G["mask0"]).then_inc(mask_in, 16)

                def step(i, first):
                    for s in range(2):
                        if not first:
                            sp.wait_ge(s_ready, 2 * i + s - 1)
                        sp.dma_start(qst[:, s, :].bitcast(FP32),
                                     q_all[bass.ds(2 * i + s, 1)].rearrange("b p n -> (b p) n")).then_inc(q_in[s], 16)

                from_first(sp, B // 2, step)

            @block.tensor
            def _(pe):
                pe.wait_ge(pad_done, 2)

                def step(i, first):
                    for s in range(2):
                        pe.wait_ge(q_in[s], i * 16 + 16)
                        if not first:
                            pe.wait_ge(masked, 2 * i + s - 1)
                        for t in range(NT):
                            for part in range(2):
                                last = pe.matmul(PS[s][:, t * S:t * S + S], qst[:, s, 128 * t:128 * t + 128],
                                                 k0[:, part, bass.ds((2 * i + s) * S, S)],
                                                 start=part == 0, stop=part == 1)
                        last.then_inc(s_ready, 1)
                    for s in range(2):
                        pe.wait_ge(exp_done, 2 * i + s + 1)
                        if not (first and s == 0):
                            pe.wait_ge(t_copied, 2 * (2 * i + s))
                        for t in range(NT):
                            last = pe.transpose(PS[2 + t // 4][:, t % 4 * 128:t % 4 * 128 + 128],
                                                pw[:, s, t * S:t * S + 128], ident[:, :])
                            if t in (3, NT - 1):
                                last.then_inc(t_ready, 1)
                    for s in range(2):
                        pe.wait_ge(t_copied, 2 * (2 * i + s) + 2)
                        if not (first and s == 0):
                            pe.wait_ge(o_scaled, 2 * i + s)
                        for t in range(NT):
                            last = pe.matmul(PS[4][:, t * D:t * D + D], pT[:, s, 128 * t:128 * t + 128],
                                             v0[:, bass.ds(2 * i + s, 1), :].rearrange("p b d -> p (b d)"),
                                             start=True, stop=True)
                        last.then_inc(o_ready, 1)
                    for s in range(2):
                        pe.wait_ge(o_scaled, 2 * i + s + 1)
                        if not (first and s == 0):
                            pe.wait_ge(c_copied, 2 * (2 * i + s))
                        for t in range(0, NT, 2):
                            last = pe.transpose(PS[5][:, 64 * t:64 * t + 128],
                                                oc[:, s, t:t + 2, :].rearrange("p t d -> p (t d)"), ident[:, :])
                        last.then_inc(c_ready, 1)

                from_first(pe, B // 2, step)

            @block.vector
            def _(dve):
                dve.wait_ge(mask_in, 16)
                with dve.Fori(0, B // 2) as i:
                    for s in range(2):
                        n = 2 * i + s + 1
                        dve.wait_ge(s_ready, n)
                        dve.tensor_tensor(p[s], PS[s][:, 0:NT * S].rearrange("p (t k) -> p t k", t=NT),
                                          mask[:, :, :], ALU.add).then_inc(masked, 1)
                        dve.wait_ge(masked, n)
                        dve.tensor_reduce(mx[:, s, :], p[s], AX.X, ALU.max).then_inc(maxed, 1)
                        dve.wait_ge(maxed, n)
                        dve.tensor_tensor(p[s], p[s], mx[:, s, :].unsqueeze(2).broadcast_to([128, NT, S]),
                                          ALU.subtract).then_inc(centred, 1)
                    for s in range(2):
                        n = 2 * i + s + 1
                        dve.wait_ge(exp_done, n)
                        dve.tensor_reduce(rs[:, s, :], p[s], AX.X, ALU.add).then_inc(summed, 1)
                        dve.wait_ge(summed, n)
                        dve.reciprocal(rs[:, s, :], rs[:, s, :]).then_inc(inverted, 1)
                    for s in range(2):
                        n = 2 * i + s + 1
                        dve.wait_ge(inverted, n)
                        dve.wait_ge(o_ready, n)
                        dve.tensor_tensor(oc[:, s, 0:NT, :], PS[4][:, 0:NT * D].rearrange("p (t d) -> p t d", t=NT),
                                          rs[:, s, :].unsqueeze(2).broadcast_to([128, NT, D]),
                                          ALU.mult).then_inc(o_scaled, 1)

            @block.scalar
            def _(act):

                def step(i, first):
                    for s in range(2):
                        act.wait_ge(centred, 2 * i + s + 1)
                        act.activation(p[s], p[s], ACT.Exp, scale=SCALE).then_inc(exp_done, 1)
                    for s in range(2):
                        for g, (a, z) in enumerate(((0, W0), (W0, T))):
                            act.wait_ge(t_ready, 2 * (2 * i + s) + g + 1)
                            act.activation(pT[:, s, a:z], PS[2 + g][0:S, 0:z - a], ACT.Copy).then_inc(t_copied, 1)
                    for s in range(2):
                        if not first:
                            act.wait_ge(placed, 4 * i)
                        act.wait_ge(c_ready, 2 * i + s + 1)
                        for odd in range(2):
                            copy_context(act, PS[5], cT[:, s], odd, c_copied)

                from_first(act, B // 2, step)

            @block.gpsimd
            def _(pool):
                pool.memset(oc[:, :, NT, :], 0.0).then_inc(pad_done, 1)
                pool.memset(pw[:, :, NT * S:], 0.0).then_inc(pad_done, 1)
                with pool.Fori(0, B // 2) as i:
                    for s in range(2):
                        pool.wait_ge(c_copied, 2 * (2 * i + s) + 2)
                        place_context(pool, ctxT, cT[:, s], (2 * i + s) * S, placed)


def copy_context(act, bank, cT, odd, c_copied):
    n = (NT + 1 - odd) // 2
    tiles = cT.rearrange("p h s -> p (h s)").rearrange("p (t r) -> p t r", r=128)
    act.activation(tiles[:, odd:NT:2, :], bank[64 * odd:64 * odd + D, 0:128 * n].rearrange("p (t r) -> p t r", r=128),
                   ACT.Copy).then_inc(c_copied, 1)


def place_context(pool, ctxT, cT, at, placed):
    for odd in range(2):
        pool.tensor_copy(ctxT[64 * odd:64 * odd + 64, :, bass.ds(at, S)],
                         cT.rearrange("p (h two) s -> p two h s", two=2)[:, odd]).then_inc(placed, 1)


def attend_long(nc, G, l, q_all, ctxT):
    PS, ident = G["PS"], G["ident"]
    PST, PSO = PS[6], PS[7]
    GROUPS = ((0, 2), (2, 4), (4, 7))
    SLOT = (0, 1, 2, 3, 0, 1, 2, 3, 4, 0, 1, 2, 3, 4)
    HC = NC // 2
    SUMS = {2: (0, 0), 3: (0, HC), 4: (1, 0), 5: (1, HC), 0: (2, 0), 1: (2, HC)}
    N = B * NT
    with Stage(nc, f"att{l}") as st:
        qst = st.sb("qst", [128, 2, NH * S], F32R)
        kst = st.sb("kst", [128, 2, 2, L], F32R)
        vst = st.sb("vst", [KP, 2, NC, 2 * D], F32R)
        p = st.sb("p", [128, 2, L])
        raw = st.sb("raw", [KP, NS, CG, 128])
        pT = st.sb("pT", [KP, 2, 5, NC, 128], F32R)
        nm = st.sb("nm", [128, 2])
        sums, rs = st.sb("sums", [128, 2, NT]), st.sb("rs", [128, NT])
        low = st.sb("low", [D, 384])
        cu, rsb = st.sb("cu", [D, 2, T]), st.sb("rsb", [D, 2, T])
        kv_in = [st.sem(f"kv_in{s}") for s in range(2)]
        s_ready, max_ready, exp_done, t_ready, raw_ready, mid_ready, act_high, dve_high, pool_low, dve_low = (
            st.sem(n) for n in ("s_ready", "max_ready", "exp_done", "t_ready", "raw_ready", "mid_ready", "act_high",
                                "dve_high", "pool_low", "dve_low"))
        o_ready, half_copied, o_added, inverted, spread, spread_copied, placed = (
            st.sem(n) for n in ("o_ready", "half_copied", "o_added", "inverted", "spread", "spread_copied", "placed"))

        def emit(eng, steps):
            steps(0, True, False)
            with eng.Fori(1, B // 2 - 1) as i:
                steps(i, False, False)
            steps(B // 2 - 1, False, True)

        with nc.Block() as block:

            @block.sync
            def _(sp):
                Stage.semaphores.clear_earlier(sp)

                def load(i, s):
                    b = 2 * i + s
                    sp.dma_start(qst[:, s, :].bitcast(FP32),
                                 q_all[bass.ds(b, 1)].rearrange("b p n -> (b p) n")).then_inc(kv_in[s], 16)
                    for half in range(2):
                        for part, src in enumerate(("kvt_hi", "kvt_lo")):
                            sp.dma_start(kst[64 * half:64 * half + 64, s, part, :].bitcast(FP32),
                                         G[src][bass.ds(b * D, D), :]).then_inc(kv_in[s], 16)
                    sp.dma_start(vst[:, s].rearrange("p c d -> p (c d)").bitcast(FP32),
                                 G["kvn"][bass.ds(b, 1)].rearrange("b p n -> (b p) n")).then_inc(kv_in[s], 16)

                load(0, 0)
                load(0, 1)
                with sp.Fori(1, B // 2) as i:
                    for s in range(2):
                        sp.wait_ge(o_ready, 3 * (2 * i + s - 1))
                        load(i, s)

            @block.tensor
            def _(pe):
                def scores(j, over):
                    s, t = j // NT % 2, j % NT
                    for c in over:
                        for part in range(2):
                            last = pe.matmul(PS[3 * (j % 2) + c][:, 0:SB], qst[:, s, 128 * t:128 * t + 128],
                                             kst[:, s, part, SB * c:SB * c + SB], start=part == 0, stop=part == 1)
                    if over[-1] == NS - 1:
                        last.then_inc(s_ready, 1)

                def weigh(i, j, which, over):
                    g, c0 = SUMS[which]
                    done = 2 * i + j // NT - (1 if g == 2 else 0)
                    s = (j // NT + (1 if g == 2 else 0)) % 2
                    t0, t1 = GROUPS[g]
                    first = SLOT[t0 + NT * s]
                    if c0 + over[0] == 0:
                        pe.wait_ge(pool_low, 2 * (done * NT + t1))
                        pe.wait_ge(dve_low, done * NT + t1)
                        if not (isinstance(done, int) and done == g == 0):
                            pe.wait_ge(o_added, 3 * done + g)
                        if g == 2:
                            pe.wait_ge(spread_copied, 2 * (done + 1))
                    for c in over:
                        c += c0
                        for part in range(2):
                            last = pe.matmul(PSO[:, 0:128 * (t1 - t0)], vst[:, s, c, :],
                                             pT[:, part, first:first + t1 - t0, c, :],
                                             start=c == part == 0, stop=c == NC - 1 and part == 1)
                    if c == NC - 1:
                        last.then_inc(o_ready, 1)

                def spread_sums(done, g):
                    if g == 0:
                        pe.wait_ge(inverted, done)
                        pe.wait_ge(o_added, 3 * done - 1)
                    else:
                        pe.wait_ge(spread_copied, 2 * done - 1)
                    for t in range(4 * g, min(4 * g + 4, NT)):
                        last = pe.matmul(PSO[:, t % 4 * 128:t % 4 * 128 + 128],
                                         rs[:, t:t + 1].broadcast_to([128, 128]), ident[:, :], start=True, stop=True)
                    last.then_inc(spread, 1)

                def steps(i, first, last_pair):
                    for j in range(2 * NT):
                        n = i * 2 * NT + j
                        t = j % NT
                        start = first and j < NT
                        ahead = not (last_pair and j >= 2 * NT - 2)
                        weighs = t in SUMS and not (start and t < 2)
                        for g in range(NS):
                            if g == 0:
                                pe.wait_ge(exp_done, n + 1)
                            if g == 2:
                                pe.wait_ge(mid_ready, n + 1)
                            elif not (first and j == g == 0):
                                pe.wait_ge(raw_ready, 2 * n + g)
                            for c in range(CG * g, CG * g + CG):
                                last = pe.transpose(PST[0:KP, c % CG * 128:c % CG * 128 + 128],
                                                    p[:, j % 2, KP * c:KP * c + KP], ident[:, :])
                            last.then_inc(t_ready, 1)
                            if g == 0 and ahead:
                                if (j + 2) % NT == 0:
                                    m = i + (j + 2) // (2 * NT)
                                    pe.wait_ge(kv_in[(j + 2) // NT % 2], m * 96 + 96)
                                scores(j + 2, (0, 1))
                            if g == 1:
                                if ahead:
                                    scores(j + 2, (2,))
                                if weighs:
                                    weigh(i, j, t, range(3))
                            if g == 2 and weighs:
                                weigh(i, j, t, range(3, HC))
                            if g > 0 and t == NT - 1:
                                spread_sums(2 * i + j // NT + 1, g - 1)

                pe.wait_ge(kv_in[0], 96)
                scores(0, (0, 1, 2))
                scores(1, (0, 1, 2))
                emit(pe, steps)
                for t in range(2):
                    weigh(B // 2, t, t, range(HC))

            @block.vector
            def _(dve):
                def row_max(j, n):
                    dve.wait_ge(s_ready, n + 1)
                    dve.tensor_reduce(nm[:, j % 2:j % 2 + 1], banks(PS, 3 * (j % 2)), AX.XY, ALU.max,
                                      negate=True).then_inc(max_ready, 1)

                def copy_middle(n, very_first):
                    if not very_first:
                        dve.wait_ge(dve_low, n)
                    dve.wait_ge(t_ready, 3 * n + 2)
                    dve.tensor_copy(raw[:, 1], PST[0:KP, :].rearrange("p (c r) -> p c r", c=CG)).then_inc(mid_ready, 1)

                def split(n, j, g):
                    o, sl = slice(CG * g, CG * g + CG), SLOT[j]
                    if g == 2:
                        dve.wait_ge(raw_ready, 2 * n + 2)
                    else:
                        dve.wait_ge(mid_ready, n + 1)
                    dve.tensor_copy(pT[:, 0, sl, o, :], raw[:, g]).then_inc(dve_high, 1)
                    if g == 1:
                        dve.wait_ge(dve_high, 2 * n + 2)
                        dve.tensor_tensor(pT[:, 1, sl, o, :], raw[:, g], pT[:, 0, sl, o, :].bitcast(FP32),
                                          ALU.subtract).then_inc(dve_low, 1)

                def add_halves(done, s, g):
                    t0, t1 = GROUPS[g]
                    if g == 0 and not (isinstance(done, int) and done < 2):
                        dve.wait_ge(placed, 2 * (done - 1))
                    dve.wait_ge(half_copied, 3 * done + g + 1)
                    dve.tensor_tensor(cu[:, s, 128 * t0:128 * t1], PSO[0:D, 0:128 * (t1 - t0)],
                                      low[:, 0:128 * (t1 - t0)], ALU.add).then_inc(o_added, 1)

                def steps(i, first, last_pair):
                    for j in range(2 * NT):
                        n = i * 2 * NT + j
                        t, s = j % NT, j // NT
                        if t == 2 and not (first and s == 0):
                            add_halves(2 * i + s - 1, 1 - s, 2)
                        if t in (4, 6):
                            add_halves(2 * i + s, s, t // 2 - 2)
                        if t == NT - 1:
                            if not (first and s == 0):
                                dve.wait_ge(spread, 2 * (2 * i + s))
                            dve.wait_ge(exp_done, n + 1)
                            dve.reciprocal(rs[:, :], sums[:, s, :]).then_inc(inverted, 1)
                        copy_middle(n, first and j == 0)
                        if not (last_pair and j >= 2 * NT - 2):
                            row_max(j, n + 2)
                        split(n, j, 2)
                        split(n, j, 1)

                row_max(0, 0)
                row_max(1, 1)
                emit(dve, steps)
                add_halves(B - 1, 1, 2)

            @block.scalar
            def _(act):
                def exps(j, n):
                    act.wait_ge(max_ready, n + 1)
                    act.activation(p[:, j % 2, :].rearrange("p (c k) -> p c k", c=NS), banks(PS, 3 * (j % 2)),
                                   ACT.Exp, bias=nm[:, j % 2:j % 2 + 1],
                                   accum_out=sums[:, j // NT % 2, j % NT:j % NT + 1]).then_inc(exp_done, 1)

                def copy(n, j, g, very_first):
                    if not very_first:
                        act.wait_ge(pool_low, 2 * n - 1 + g // 2)
                    act.wait_ge(t_ready, 3 * n + g + 1)
                    act.activation(raw[:, g], PST[0:KP, :].rearrange("p (c r) -> p c r", c=CG),
                                   ACT.Copy).then_inc(raw_ready, 1)

                def high(n, j):
                    act.wait_ge(raw_ready, 2 * n + 1)
                    act.activation(pT[:, 0, SLOT[j], 0:CG, :], raw[:, 0], ACT.Copy).then_inc(act_high, 1)

                def half(done, g):
                    t0, t1 = GROUPS[g]
                    if not (isinstance(done, int) and done == g == 0):
                        act.wait_ge(o_added, 3 * done + g)
                    act.wait_ge(o_ready, 3 * done + g + 1)
                    act.activation(low[:, 0:128 * (t1 - t0)], PSO[D:2 * D, 0:128 * (t1 - t0)],
                                   ACT.Copy).then_inc(half_copied, 1)

                def copy_spread(done, s, g):
                    a, z = 512 * g, min(512 * g + 512, T)
                    if g == 0 and not (isinstance(done, int) and done <= 2):
                        act.wait_ge(placed, 2 * (done - 2))
                    act.wait_ge(spread, 2 * (done - 1) + g + 1)
                    act.activation(rsb[:, s, a:z], PSO[0:D, 0:z - a], ACT.Copy).then_inc(spread_copied, 1)

                def steps(i, first, last_pair):
                    for j in range(2 * NT):
                        n = i * 2 * NT + j
                        t, s = j % NT, j // NT
                        if t == 2 and not (first and s == 0):
                            half(2 * i + s - 1, 2)
                        if t in (4, 6):
                            half(2 * i + s, t // 2 - 2)
                        copy(n, j, 0, first and j == 0)
                        if t == 0 and not (first and s == 0):
                            copy_spread(2 * i + s, 1 - s, 1)
                        if not (last_pair and j == 2 * NT - 1):
                            exps(j + 1, n + 1)
                        if t == NT - 1:
                            copy_spread(2 * i + s + 1, s, 0)
                        high(n, j)
                        copy(n, j, 2, first and j == 0)

                exps(0, 0)
                emit(act, steps)
                copy_spread(B, 1, 1)
                half(B - 1, 2)

            @block.gpsimd
            def _(pool):
                def steps(i, first, last_pair):
                    for j in range(2 * NT):
                        n = i * 2 * NT + j
                        for g in (0, 2):
                            o, sl = slice(CG * g, CG * g + CG), SLOT[j]
                            pool.wait_ge(*((act_high, n + 1) if g == 0 else (dve_high, 2 * n + 1)))
                            pool.tensor_tensor(pT[:, 1, sl, o, :], raw[:, g], pT[:, 0, sl, o, :].bitcast(FP32),
                                               ALU.subtract).then_inc(pool_low, 1)
                        if j % NT in (2, 3) and not (first and j < NT):
                            place(2 * i + j // NT, (j // NT + 1) % 2, 2 * (n + 1), j % NT - 2)

                def place(done, s, lows, odd):
                    pool.wait_ge(o_added, 3 * done)
                    pool.wait_ge(spread_copied, 2 * done)
                    pool.wait_ge(pool_low, lows)
                    a, r = (m[:, s, :].rearrange("p (h two s) -> p two h s", two=2, s=S)[:, odd] for m in (cu, rsb))
                    pool.tensor_tensor(ctxT[64 * odd:64 * odd + 64, :, bass.ds((done - 1) * S, S)], a, r,
                                       ALU.mult).then_inc(placed, 1)
                    pool.wait_ge(placed, 2 * (done - 1) + odd + 1)

                emit(pool, steps)
                place(B, 1, 2 * N, 0)
                place(B, 1, 2 * N, 1)


def banks(PS, first):
    return PS.all[:, first * 512:(first + NS) * 512].rearrange("p (c k) -> p c k", c=NS)[:, :, 0:SB]


def project_out(nc, G, l, Bm, ctxT):
    PS, x = G["PS"], G["x"]
    with Stage(nc, f"out{l}") as st:
        o_ready, x_done = st.sem("o_ready"), st.sem("x_done")
        with nc.Block() as block:

            @block.sync
            def _(sp):
                Stage.semaphores.clear_earlier(sp)

            @block.tensor
            def _(pe):
                for t in range(NT):
                    for h in range(NP):
                        last = pe.matmul(PS[t][:, 0:H], ctxT[:, h, 128 * t:128 * t + 128], Bm[:, h, :],
                                         start=h == 0, stop=h == NP - 1)
                    last.then_inc(o_ready, 1)

            @block.vector
            def _(dve):
                for t in range(NT):
                    dve.wait_ge(o_ready, t + 1)
                    dve.scalar_tensor_tensor(x[:, t, :], PS[t][:, 0:H], G["tanh"][:, l:l + 1], x[:, t, :],
                                             ALU.mult, ALU.add).then_inc(x_done, 1)


def route(nc, G, l, E, top, kind, rows, groups_per_expert):
    PS, xT, ident = G["PS"], G["xT"], G["ident"]
    with Stage(nc, f"route{l}") as st:
        wr, tie = st.sb("wr", [128, KC, E]), st.sb("tie", [128, E * E])
        bias = st.sb("bias", [128, E])
        lg, e, key = st.sb("lg", [128, NT, E]), st.sb("e", [128, NT, E]), st.sb("key", [128, NT, E])
        gt, eq = st.sb("gt", [128, NT, E * E]), st.sb("eq", [128, NT, E * E])
        rank, z = st.sb("rank", [128, NT, E]), st.sb("z", [128, NT])
        comb, combT = st.sb("comb", [128, NT, rows]), st.sb("combT", [rows, T])
        in_w, lg_ready, to_exp, exp_done, chain, comb_ready, tr_ready, tr_copied, stored = (
            st.sem(n) for n in ("in_w", "lg_ready", "to_exp", "exp_done", "chain", "comb_ready", "tr_ready",
                                "tr_copied", "stored"))
        loads = [(wr[:, :, :], G[f"L{l}_router"]), (tie[:, :], G[f"tie{E}"])]
        if kind == "renormalised":
            loads.append((bias[:, :], G["L3_bias"].broadcast_to([128, E])))
        with nc.Block() as block:

            @block.sync
            def _(sp):
                Stage.semaphores.clear_earlier(sp)
                for dst, src in loads:
                    sp.dma_start(dst, src).then_inc(in_w, 16)
                sp.wait_ge(tr_copied, 2)
                sp.dma_start(G["comb"][0:rows * groups_per_expert, :].rearrange("(e g) n -> e g n", e=rows),
                             combT[:, :].unsqueeze(1).broadcast_to([rows, groups_per_expert, T])).then_inc(stored, 16)
                sp.wait_ge(stored, 16)

            @block.tensor
            def _(pe):
                pe.wait_ge(in_w, 16 * len(loads))
                for t in range(NT):
                    for k in range(KC):
                        last = pe.matmul(PS[0][:, t * E:t * E + E], xT[:, k, 128 * t:128 * t + 128], wr[:, k, :],
                                         start=k == 0, stop=k == KC - 1)
                last.then_inc(lg_ready, 1)
                pe.wait_ge(comb_ready, 1)
                for t in range(NT):
                    last = pe.transpose(PS[1 + t // 4][0:rows, t % 4 * 128:t % 4 * 128 + 128], comb[:, t, :],
                                        ident[:, :])
                    if t in (3, NT - 1):
                        last.then_inc(tr_ready, 1)

            @block.scalar
            def _(act):
                act.wait_ge(to_exp, 1)
                act.activation(e[:, :, :], (lg if kind == "sigmoid" else e)[:, :, :], ACT.Exp,
                               scale=-1.0 if kind == "sigmoid" else 1.0).then_inc(exp_done, 1)
                for g, (a, b) in enumerate(((0, 512), (512, T))):
                    act.wait_ge(tr_ready, g + 1)
                    act.activation(combT[:, a:b], PS[1 + g][0:rows, 0:b - a], ACT.Copy).then_inc(tr_copied, 1)

            @block.vector
            def _(dve):
                c = Count(dve, chain)
                dve.wait_ge(lg_ready, 1)
                dve.wait_ge(in_w, 16 * len(loads))
                logits = PS[0][:, 0:NT * E].rearrange("p (t e) -> p t e", t=NT)
                wide = [128, NT, E]
                if kind == "renormalised":
                    c.link(dve.tensor_tensor(lg[:, :, :], logits, bias[:, :].unsqueeze(1).broadcast_to(wide), ALU.add))
                else:
                    c.link(dve.tensor_copy(lg[:, :, :], logits))
                if kind == "sigmoid":
                    dve.engine_nop().then_inc(to_exp, 1)
                    dve.wait_ge(exp_done, 1)
                    c.link(dve.tensor_scalar(e[:, :, :], e[:, :, :], 1.0, None, ALU.add))
                    c.link(dve.reciprocal(e[:, :, :], e[:, :, :]))
                    values = e
                else:
                    c.link(dve.tensor_reduce(z[:, :], lg[:, :, :], AX.X, ALU.max))
                    dve.tensor_tensor(e[:, :, :], lg[:, :, :], z[:, :].unsqueeze(2).broadcast_to(wide),
                                      ALU.subtract).then_inc(to_exp, 1)
                    values = lg
                for t in range(NT):
                    other = values[:, t, :].unsqueeze(1).broadcast_to([128, E, E])
                    own = values[:, t, :].unsqueeze(2).broadcast_to([128, E, E])
                    c.mark(dve.tensor_tensor(gt[:, t, :].rearrange("p (a b) -> p a b", a=E), other, own, ALU.is_gt))
                    c.mark(dve.tensor_tensor(eq[:, t, :].rearrange("p (a b) -> p a b", a=E), other, own, ALU.is_equal))
                dve.wait_ge(chain, c.n)
                c.link(dve.tensor_tensor(eq[:, :, :], eq[:, :, :], tie[:, :].unsqueeze(1).broadcast_to([128, NT, E * E]),
                                         ALU.mult))
                c.link(dve.tensor_tensor(gt[:, :, :], gt[:, :, :], eq[:, :, :], ALU.add))
                c.link(dve.tensor_reduce(rank[:, :, :], gt[:, :, :].rearrange("p t (a b) -> p t a b", a=E), AX.X,
                                         ALU.add))
                c.link(dve.tensor_scalar(rank[:, :, :], rank[:, :, :], float(top), None, ALU.is_lt))
                if rows > E:
                    c.link(dve.memset(comb[:, :, E:E + 2], 1.0))
                    c.link(dve.memset(comb[:, :, E + 2:rows], 0.0))
                if kind != "sigmoid":
                    dve.wait_ge(exp_done, 1)
                if kind == "sigmoid":
                    dve.tensor_tensor(comb[:, :, 0:E], e[:, :, :], rank[:, :, :], ALU.mult).then_inc(comb_ready, 1)
                    return
                c.link(dve.tensor_tensor(key[:, :, :], e[:, :, :], rank[:, :, :], ALU.mult))
                over = e if kind == "softmax" else key
                c.link(dve.tensor_reduce(z[:, :], over[:, :, :], AX.X, ALU.add))
                c.link(dve.reciprocal(z[:, :], z[:, :]))
                dve.tensor_tensor(comb[:, :, 0:E], key[:, :, :], z[:, :].unsqueeze(2).broadcast_to(wide),
                                  ALU.mult).then_inc(comb_ready, 1)


def experts(nc, G, l, chunks, group_rows):
    PS, xT, x, ident = G["PS"], G["xT"], G["x"], G["ident"]
    GU = 2 * KC * 128
    groups = 128 // group_rows
    with Stage(nc, f"moe{l}") as st:
        raw = st.sb("raw", [128, 2, GU + H])
        w = st.sb("w", [128, 2, 2, GU + H], F32R)
        xs = st.sb("xs", [128, 2, KC, T], F32R)
        cb = st.sb("cb", [128, 2, T])
        sg, sc, hf = st.sb("sg", [128, 2, HALF]), st.sb("sc", [128, 2, HALF]), st.sb("hf", [128, 2, HALF])
        h = st.sb("h", [128, 2, 2, 2, HALF], F32R)
        oT = st.sb("oT", [128, KC, T])
        w_in = [st.sem(f"w_in{s}") for s in range(2)]
        cb_in = [st.sem(f"cb_in{s}") for s in range(2)]
        x_high, x_split, gu_high, gu_split, d_high, d_split = (
            st.sem(n) for n in ("x_high", "x_split", "gu_high", "gu_split", "d_high", "d_split"))
        gu_ready, silu_done, comb_done, h_made, h_high, h_split, d_done = (
            st.sem(n) for n in ("gu_ready", "silu_done", "comb_done", "h_made", "h_high", "h_split", "d_done"))
        o_copied, tr_ready, x_done = (st.sem(n) for n in ("o_copied", "tr_ready", "x_done"))
        w_dram = G[f"L{l}_experts"]

        def emit(eng, chunk):
            chunk(0, 0, True, True)
            chunk(0, 1, False, True)
            done = (chunks - 1) // 2
            with eng.Fori(1, done) as i:
                for s in range(2):
                    chunk(i, s, False, True)
            for c in range(2 * done, chunks):
                chunk(done, c % 2, False, c < chunks - 1)

        def following(i, s):
            return (i, 1) if s == 0 else (i + 1, 0)

        with nc.Block() as block:

            @block.sync
            def _(sp):
                Stage.semaphores.clear_earlier(sp)

                def chunk(i, s, first, more):
                    c = 2 * i + s
                    if not isinstance(i, int) or i:
                        sp.wait_ge(d_split, c - 1)
                    sp.dma_start(raw[:, s, :], w_dram[bass.ds(c * 128, 128), :]).then_inc(w_in[s], 16)
                    if not isinstance(i, int) or i:
                        sp.wait_ge(comb_done, 2 * c - 2)
                    sp.dma_start(cb[:, s, :], G["comb"][bass.ds(c * groups, groups), :].unsqueeze(1)
                                 .broadcast_to([groups, group_rows, T])).then_inc(cb_in[s], 16)

                emit(sp, chunk)

            @block.tensor
            def _(pe):
                PARTS = ((0, 0), (0, 1), (1, 0))

                def up(c, s, e):
                    for m in range(2):
                        n = 0
                        for k in range(KC):
                            o = (m * KC + k) * 128
                            for pw, px in PARTS:
                                last = pe.matmul(PS[2 * e + m][:, 0:HALF], w[:, s, pw, o:o + 128],
                                                 xs[:, px, k, HALF * e:HALF * e + HALF],
                                                 start=n == 0, stop=n == 3 * KC - 1)
                                n += 1
                    last.then_inc(gu_ready, 1)

                def down(c, s, e, start, stop):
                    if e == 0:
                        pe.wait_ge(d_split, c + 1)
                    pe.wait_ge(h_split, 2 * c + e + 1)
                    for d in range(KC):
                        o = GU + 128 * d
                        for n, (pw, ph) in enumerate(PARTS):
                            last = pe.matmul(PS[4 + 2 * d + e][:, 0:HALF], w[:, s, pw, o:o + 128], h[:, s, ph, e, :],
                                             start=start and n == 0, stop=stop and n == 2)
                    if e == 1:
                        last.then_inc(d_done, 1)

                def chunk(i, s, first, more):
                    c = 2 * i + s
                    pe.wait_ge(gu_split, c + 1)
                    for e in range(2):
                        if not first:
                            pe.wait_ge(h_made, 2 * (c - 1) + e + 1)
                        up(c, s, e)
                        if not first:
                            down(c - 1, 1 - s, e, isinstance(i, int) and c == 1, False)

                pe.wait_ge(x_split, 1)
                emit(pe, chunk)
                for e in range(2):
                    down(chunks - 1, (chunks - 1) % 2, e, False, True)
                for t in range(NT):
                    if t == 0:
                        pe.wait_ge(o_copied, 2 * KC)
                    if t >= 4:
                        pe.wait_ge(x_done, t - 3)
                    for d in range(KC):
                        last = pe.transpose(PS[t % 4][:, 128 * d:128 * d + 128], oT[:, d, 128 * t:128 * t + 128],
                                            ident[:, :])
                    last.then_inc(tr_ready, 1)

            @block.scalar
            def _(act):
                def gu_part(i, s):
                    act.wait_ge(w_in[s], i * 16 + 16)
                    act.activation(w[:, s, 0, 0:GU], raw[:, s, 0:GU], ACT.Copy).then_inc(gu_high, 1)

                def d_part(i, s):
                    act.activation(w[:, s, 0, GU:], raw[:, s, GU:], ACT.Copy).then_inc(d_high, 1)

                def chunk(i, s, first, more):
                    c = 2 * i + s
                    for e in range(2):
                        n = 2 * c + e
                        act.wait_ge(gu_ready, n + 1)
                        act.activation(sg[:, e, :], PS[2 * e][:, 0:HALF], ACT.Silu).then_inc(silu_done, 1)
                        if more and e == 0:
                            gu_part(*following(i, s))
                        if more and e == 1:
                            if not first:
                                act.wait_ge(d_done, c)
                            d_part(*following(i, s))
                        act.wait_ge(h_made, n + 1)
                        act.activation(h[:, s, 0, e, :], hf[:, e, :], ACT.Copy).then_inc(h_high, 1)

                gu_part(0, 0)
                act.activation(xs[:, 0], xT[:, :, :], ACT.Copy).then_inc(x_high, 1)
                d_part(0, 0)
                emit(act, chunk)
                act.wait_ge(d_done, chunks)
                for e in range(2):
                    act.activation(oT[:, 0, HALF * e:HALF * e + HALF], PS[4 + e][:, 0:HALF],
                                   ACT.Copy).then_inc(o_copied, 1)

            @block.gpsimd
            def _(pool):
                def chunk(i, s, first, more):
                    pool.wait_ge(cb_in[s], i * 16 + 16)
                    for e in range(2):
                        n = 2 * (2 * i + s) + e
                        pool.wait_ge(silu_done, n + 1)
                        pool.tensor_tensor(sc[:, e, :], sg[:, e, :], cb[:, s, HALF * e:HALF * e + HALF],
                                           ALU.mult).then_inc(comb_done, 1)

                emit(pool, chunk)

            @block.vector
            def _(dve):
                def gu_part(c, s):
                    dve.wait_ge(gu_high, c + 1)
                    dve.tensor_tensor(w[:, s, 1, 0:GU], raw[:, s, 0:GU], w[:, s, 0, 0:GU].bitcast(FP32),
                                      ALU.subtract).then_inc(gu_split, 1)

                def d_part(c, s):
                    dve.wait_ge(d_high, c + 1)
                    dve.tensor_tensor(w[:, s, 1, GU:], raw[:, s, GU:], w[:, s, 0, GU:].bitcast(FP32),
                                      ALU.subtract).then_inc(d_split, 1)

                def chunk(i, s, first, more):
                    c = 2 * i + s
                    for e in range(2):
                        n = 2 * c + e
                        dve.wait_ge(comb_done, n + 1)
                        dve.tensor_tensor(hf[:, e, :], PS[2 * e + 1][:, 0:HALF], sc[:, e, :],
                                          ALU.mult).then_inc(h_made, 1)
                        if more:
                            (gu_part if e == 0 else d_part)(c + 1, 1 - s)
                        dve.wait_ge(h_high, n + 1)
                        dve.tensor_tensor(h[:, s, 1, e, :], hf[:, e, :], h[:, s, 0, e, :].bitcast(FP32),
                                          ALU.subtract).then_inc(h_split, 1)

                gu_part(0, 0)
                dve.wait_ge(x_high, 1)
                dve.tensor_tensor(xs[:, 1], xT[:, :, :], xs[:, 0].bitcast(FP32), ALU.subtract).then_inc(x_split, 1)
                d_part(0, 0)
                emit(dve, chunk)
                dve.wait_ge(d_done, chunks)
                for e in range(2):
                    dve.tensor_copy(oT[:, 1, HALF * e:HALF * e + HALF], PS[6 + e][:, 0:HALF]).then_inc(o_copied, 1)
                for t in range(NT):
                    dve.wait_ge(tr_ready, t + 1)
                    dve.scalar_tensor_tensor(x[:, t, :], PS[t % 4][:, 0:H], G["tanh"][:, 4 + l:5 + l], x[:, t, :],
                                             ALU.mult, ALU.add).then_inc(x_done, 1)


def quantised_linear(nc, G):
    PS, xT, x = G["PS"], G["xT"], G["x"]
    with Stage(nc, "fp8") as st:
        w8, wi, wm = st.sb("w8", [128, KC, H], U8), st.sb("wi", [128, KC, H], I32), st.sb("wm", [128, KC, H], I32)
        wv, w2, wb = st.sb("wv", [128, KC, H]), st.sb("w2", [128, KC, H]), st.sb("wb", [128, KC, H], BF16)
        s16, sf, ws = st.sb("s16", [128, 1], BF16), st.sb("sf", [128, 1]), st.sb("ws", [128, 1])
        rs, sw = st.sb("rs", [128, 1]), st.sb("sw", [128, 1])
        y, step, q = st.sb("y", [128, KC, T]), st.sb("step", [128, KC, T]), st.sb("q", [128, KC, T], BF16)
        in_w, chain, w_ready, q_ready, o_ready, x_done = (
            st.sem(n) for n in ("in_w", "chain", "w_ready", "q_ready", "o_ready", "x_done"))
        with nc.Block() as block:

            @block.sync
            def _(sp):
                Stage.semaphores.clear_earlier(sp)
                sp.dma_start(w8[:, :, :], G["L1_w8"]).then_inc(in_w, 16)
                sp.dma_start(s16[:, :], G["L1_in_scale"].broadcast_to([128, 1])).then_inc(in_w, 16)
                sp.dma_start(ws[:, :], G["L1_w_scale"].broadcast_to([128, 1])).then_inc(in_w, 16)

            @block.vector
            def _(dve):
                c = Count(dve, chain)
                dve.wait_ge(in_w, 48)
                c.link(dve.tensor_copy(sf[:, :], s16[:, :]))
                c.link(dve.reciprocal(rs[:, :], sf[:, :]))
                c.link(dve.tensor_tensor(sw[:, :], sf[:, :], ws[:, :], ALU.mult))
                c.link(dve.tensor_tensor(sw[:, :], sw[:, :], G["tanh"][:, 5:6], ALU.mult))
                c.link(dve.tensor_scalar(y[:, :, :], xT[:, :, :], rs[:, :], FP8_MAX, ALU.mult, ALU.min))
                c.link(dve.tensor_scalar(y[:, :, :], y[:, :, :], -FP8_MAX, None, ALU.max))
                c.link(dve.tensor_scalar(step[:, :, :].bitcast(I32), y[:, :, :].bitcast(I32), 0x7F800000, None,
                                         ALU.bitwise_and))
                c.link(dve.tensor_scalar(step[:, :, :], step[:, :, :], 2.0 ** -6, 1.5 * 2.0 ** 20, ALU.max, ALU.mult))
                c.link(dve.tensor_tensor(y[:, :, :], y[:, :, :], step[:, :, :], ALU.add))
                dve.tensor_tensor(q[:, :, :], y[:, :, :], step[:, :, :], ALU.subtract).then_inc(q_ready, 1)
                c.link(dve.tensor_copy(wi[:, :, :], w8[:, :, :]))
                c.link(dve.tensor_scalar(wm[:, :, :], wi[:, :, :], 0x7F, 20, ALU.bitwise_and, ALU.logical_shift_left))
                c.link(dve.tensor_scalar(wm[:, :, :], wm[:, :, :], 0x40000000, None, ALU.bitwise_or))
                c.link(dve.tensor_scalar(wv[:, :, :], wm[:, :, :].bitcast(FP32), 2.0 ** -8, None, ALU.mult))
                c.link(dve.tensor_scalar(w2[:, :, :], wv[:, :, :], 2.0, -2.0 ** -6, ALU.mult, ALU.add))
                c.link(dve.tensor_tensor(wv[:, :, :], wv[:, :, :], w2[:, :, :], ALU.min))
                c.link(dve.tensor_scalar(wi[:, :, :], wi[:, :, :], 0x80, None, ALU.bitwise_and))
                c.link(dve.tensor_scalar(w2[:, :, :], wi[:, :, :], -1.0 / 64, 1.0, ALU.mult, ALU.add))
                dve.tensor_tensor(wb[:, :, :], wv[:, :, :], w2[:, :, :], ALU.mult).then_inc(w_ready, 1)
                for t in range(NT):
                    dve.wait_ge(o_ready, t + 1)
                    dve.scalar_tensor_tensor(x[:, t, :], PS[t][:, 0:H], sw[:, :], x[:, t, :],
                                             ALU.mult, ALU.add).then_inc(x_done, 1)

            @block.tensor
            def _(pe):
                pe.wait_ge(q_ready, 1)
                pe.wait_ge(w_ready, 1)
                for t in range(NT):
                    for k in range(KC):
                        last = pe.matmul(PS[t][:, 0:H], q[:, k, 128 * t:128 * t + 128], wb[:, k, :],
                                         start=k == 0, stop=k == KC - 1)
                    last.then_inc(o_ready, 1)


class Banks:

    def __init__(self, tensor):
        self.all = tensor[:, :]

    def __getitem__(self, i):
        return self.all[:, 512 * i:512 * i + 512]


MOE = {
    0: (16, 4, "softmax", 19, 176),
    2: (8, 1, "sigmoid", 8, 512),
    3: (16, 4, "renormalised", 16, 224),
}
CHUNKS = {0: 25, 2: 32, 3: 28}


def program(nc, G, out):
    with ExitStack() as stack:
        def sb(name, shape, dt=FP32):
            return stack.enter_context(nc.sbuf_tensor(name, shape, dt))

        G["comb"] = nc.dram_tensor("comb_rows", [19 * 11, T], FP32, kind="Internal").ap()
        G["kvt_hi"] = nc.dram_tensor("kvt_hi", [B * D, L], FP32, kind="Internal").ap()
        G["kvt_lo"] = nc.dram_tensor("kvt_lo", [B * D, L], FP32, kind="Internal").ap()
        G["kvn"] = nc.dram_tensor("kvn", [B, KP, NC * 2 * D], FP32, kind="Internal").ap()
        G["q"] = nc.dram_tensor("q_rows", [B, 128, NH * S], FP32, kind="Internal").ap()
        G["x"], G["xT"] = sb("x", [128, NT, H]), sb("xT", [128, KC, T])
        G["ident"], G["gate"], G["tanh"] = sb("ident", [128, 128]), sb("gate", [128, 8]), sb("tanh", [128, 8])
        G["PS"] = Banks(stack.enter_context(nc.psum_tensor("banks", [128, 8 * 512], FP32)))

        Stage.semaphores = Semaphores(nc, stack)
        with Stage(nc, "layer0") as st:
            G["k0"], G["v0"] = st.sb("k0", [128, 2, T], F32R), st.sb("v0", [S, B, D])
            rotate_context(nc, G)
            attention(nc, G, 0)
        for l in range(4):
            if l:
                attention(nc, G, l)
            normalise(nc, G, f"normf{l}")
            if l == 1:
                quantised_linear(nc, G)
            else:
                E, top, kind, rows, width = MOE[l]
                group_rows = np.gcd(width, 128).item()
                route(nc, G, l, E, top, kind, rows, width // group_rows)
                experts(nc, G, l, CHUNKS[l], group_rows)
        with Stage(nc, "store") as st:
            stored = st.sem("stored")
            with nc.Block() as block:

                @block.sync
                def _(sp):
                    Stage.semaphores.clear_earlier(sp)
                    sp.dma_start(out, G["x"][:, :, :]).then_inc(stored, 16)
                    sp.wait_ge(stored, 16)


def attention(nc, G, l):
    normalise(nc, G, f"norma{l}")
    with Stage(nc, f"keep{l}") as keep:
        Bm = keep.sb("B", [128, NP, H])
        with Stage(nc, f"mats{l}") as st:
            q_all = st.sb("q", [128, B, NH, S], F32R)
            if l == 2:
                Q, N = st.sb("Q", [128, NH, KC, CQ]), st.sb("N", [CQH, 2, NH, D])
                fold_latent(nc, G, l, None, Bm, Q, N)
                rotated_queries(nc, G, Q, N, q_all)
            else:
                A = st.sb("A", [128, KC, NH, D])
                if l:
                    fold_latent(nc, G, l, A, Bm)
                else:
                    fold_small(nc, G, A, Bm)
                queries(nc, G, l, A, q_all)
        with Stage(nc, f"ctx{l}") as st:
            ctxT = st.sb("ctxT", [128, NP, T])
            if l:
                attend_long(nc, G, l, G["q"], ctxT)
            else:
                attend_short(nc, G, G["q"], ctxT)
            project_out(nc, G, l, Bm, ctxT)


def rope_tables(length, dim):
    inv = (1.0 / np.float32(10000.0) ** (np.arange(0, dim, 2, dtype=np.float32) / np.float32(dim))).astype(np.float32)
    f = np.arange(length, dtype=np.float32)[:, None] * inv[None, :]
    cos, sin = np.repeat(np.cos(f), 2, axis=-1), np.repeat(np.sin(f), 2, axis=-1)
    sign = np.where(np.arange(dim) < dim // 2, -1.0, 1.0).astype(np.float32)
    return cos, sin * sign


def laid_out(i):
    c = np.ascontiguousarray
    ctx = i["ctx_512"]
    swapped = np.concatenate([ctx[..., D // 2:], ctx[..., :D // 2]], axis=-1)

    def by_width(a):
        return c(a.transpose(0, 2, 1).reshape(B * D, L))

    def by_key(a):
        return c(a.reshape(B, NC, KP, D).transpose(0, 2, 1, 3).reshape(B, KP, NC * D))

    cos, sin = rope_tables(L, D)
    cosq, sinq = rope_tables(S, CQ)
    a = {
        "x_in": c(i["x"].reshape(NT, 128, H).transpose(1, 0, 2)),
        "ctxT": by_width(ctx), "ctxTs": by_width(swapped), "ctxN": by_key(ctx), "ctxNs": by_key(swapped),
        "cosT": c(np.tile(cos.T, (2, 1))), "sinT": c(np.tile(sin.T, (2, 1))),
        "cosN": by_key(np.broadcast_to(cos, (B, L, D)))[0], "sinN": by_key(np.broadcast_to(sin, (B, L, D)))[0],
        "cosQ": c(cosq.T.reshape(2, CQH, S).transpose(1, 0, 2)), "sinQ": c(sinq.T.reshape(2, CQH, S).transpose(1, 0, 2)),
        "ctx0T": c(ctx[:, :S].transpose(2, 0, 1).reshape(D, T)), "ctx0N": c(ctx[:, :S].transpose(1, 0, 2)),
        "ident_in": np.eye(128, dtype=np.float32),
        "g_xattn": c(i["g_xattn"].reshape(1, 4)), "g_ffn": c(i["g_ffn"].reshape(1, 4)),
    }
    row = np.arange(NH * S).reshape(NT, 128).T % S
    a["mask0"] = np.where(np.arange(S) <= row[:, :, None], 0.0, np.finfo(np.float32).min).astype(np.float32)
    for E in (8, 16):
        a[f"tie{E}"] = c(np.broadcast_to((np.arange(E)[None, :] < np.arange(E)[:, None]).astype(np.float32)
                                         .reshape(1, E * E), (128, E * E)))
    HD = H // NH
    wkv = i["L0_xattn_Wkv_expand"]
    a["L0_wq"] = c(i["L0_xattn_Wq"].reshape(NH, HD, H).transpose(1, 0, 2))
    a["L0_wk"] = c(wkv[:H].reshape(NH, HD, D).transpose(1, 0, 2))
    a["L0_wv"] = c(wkv[H:].reshape(NH, HD, D).transpose(1, 0, 2))
    a["L0_wo"] = c(i["L0_xattn_Wout"].T.reshape(NH, HD, H).transpose(1, 0, 2))
    for l in (1, 2, 3):
        w = {n: i[f"L{l}_xattn_{n}"] for n in ("Wq", "w_kc_q", "w_kc_kv", "W_qr", "W_kr", "Wo")}
        a[f"L{l}_wq"] = c(w["Wq"].reshape(NH, K, H).transpose(1, 0, 2))
        a[f"L{l}_wqr"] = c(w["W_qr"].transpose(2, 0, 1))
        a[f"L{l}_wkr"] = c(w["W_kr"].transpose(2, 0, 1))
        a[f"L{l}_wv"] = c(w["w_kc_kv"].transpose(1, 0, 2))
        a[f"L{l}_wo"] = c(w["Wo"].T.reshape(NH, K, H).transpose(1, 0, 2))
        if l == 2:
            a["L2_wc"] = c(w["w_kc_q"].transpose(1, 0, 2))
        else:
            a[f"L{l}_wc"] = c(w["w_kc_q"].reshape(NH, K, 2, CQH).transpose(3, 2, 0, 1))

    def expert_chunks(gate, up, down, chunks):
        pad = [(0, chunks * 128 - gate.shape[0]), (0, 0)]
        gate, up, down = (np.pad(m, pad) for m in (gate, up, down))
        def stationary(m):
            return m.reshape(chunks, 128, KC, 128).transpose(0, 3, 2, 1).reshape(chunks * 128, KC * 128)
        return c(np.concatenate([stationary(gate), stationary(up), down], axis=1))

    a["L0_experts"] = expert_chunks(
        np.concatenate([i["L0_ffn_W1"].reshape(-1, H), i["L0_ffn_W1s"]]),
        np.concatenate([i["L0_ffn_W3"].reshape(-1, H), i["L0_ffn_W3s"]]),
        np.concatenate([i["L0_ffn_W2"].transpose(0, 2, 1).reshape(-1, H), i["L0_ffn_W2s"].T]), CHUNKS[0])
    for l, (g, u, d) in {2: ("gate_w", "up_w", "down_w"), 3: ("gate_proj", "up_proj", "down_proj")}.items():
        a[f"L{l}_experts"] = expert_chunks(i[f"L{l}_ffn_{g}"].transpose(0, 2, 1).reshape(-1, H),
                                           i[f"L{l}_ffn_{u}"].transpose(0, 2, 1).reshape(-1, H),
                                           i[f"L{l}_ffn_{d}"].reshape(-1, H), CHUNKS[l])

    def router(w):
        return c(w.reshape(KC, 128, -1).transpose(1, 0, 2))

    a["L0_router"], a["L2_router"] = router(i["L0_ffn_Wg"].T), router(i["L2_ffn_router_w"])
    a["L3_router"], a["L3_bias"] = router(i["L3_ffn_router_w"].T), c(i["L3_ffn_expert_bias"].reshape(1, -1))
    a["L1_w8"] = c(i["L1_ffn_weight"].view(np.uint8).T.reshape(KC, 128, H).transpose(1, 0, 2))
    a["L1_in_scale"] = c(i["L1_ffn_input_scale"].reshape(1, 1))
    a["L1_w_scale"] = c(i["L1_ffn_weight_scale"].reshape(1, 1))
    return a


def kernel(**inputs):
    import concourse.bacc as bacc
    from concourse.bass_utils import run_bass_kernel_spmd

    nc = bacc.Bacc("TRN2", target_bir_lowering=False, num_devices=1)
    arrays, G = {}, {}
    for name, a in laid_out({k: np.asarray(v) for k, v in inputs.items()}).items():
        arrays[f"{name}_dram"] = a
        G[name] = nc.dram_tensor(f"{name}_dram", a.shape, mybir.dt.from_np(a.dtype), kind="ExternalInput").ap()
    out = nc.dram_tensor("out_dram", (128, NT, H), FP32, kind="ExternalOutput").ap()
    program(nc, G, out)
    r = run_bass_kernel_spmd(nc, [arrays], core_ids=[0])
    return np.ascontiguousarray(r.results[0]["out_dram"].transpose(1, 0, 2)).reshape(B, S, H)
```

```python
from contextlib import ExitStack

import numpy as np
import concourse.bass as bass
from concourse import mybir

FP32 = mybir.dt.float32
F32R = mybir.dt.float32r
BF16 = mybir.dt.bfloat16
U8 = mybir.dt.uint8
I32 = mybir.dt.int32
ALU = mybir.AluOpType
ACT = mybir.ActivationFunctionType
AX = mybir.AxisListType

B, S, H, L, D = 16, 56, 256, 1500, 64
NH, K, CQ = 16, 128, 192
T = B * S
NT = T // 128
KC = H // 128
HALF = T // 2
NP = NH // 2
KP = 125
NC = L // KP
SB = 500
NS = L // SB
CG = NC // NS
CQH = CQ // 2
EPS = 1e-5
FP8_MAX = 448.0


PARTS = ((0, 0), (0, 1), (1, 0))


class Count:

    def __init__(self, eng, sem):
        self.eng, self.sem, self.n = eng, sem, 0

    def mark(self, ins):
        self.n += 1
        ins.then_inc(self.sem, 1)

    def link(self, ins):
        self.mark(ins)
        self.eng.wait_ge(self.sem, self.n)


class Semaphores:

    EACH = 40

    def __init__(self, nc, stack):
        self.sets = [[stack.enter_context(nc.semaphore(f"set{i}_{n}")) for n in range(self.EACH)] for i in range(2)]
        self.used, self.turn = [0, 0], 0

    def start(self):
        self.turn = 1 - self.turn
        self.used[self.turn] = 0

    def take(self):
        n = self.used[self.turn]
        self.used[self.turn] = n + 1
        return self.sets[self.turn][n]

    def clear_earlier(self, sp):
        for sem in self.sets[1 - self.turn][:self.used[1 - self.turn]]:
            sp.sem_clear(sem)


class Stage:

    semaphores = None

    def __init__(self, nc, name):
        self.nc, self.name, self.stack, self.started = nc, name, ExitStack(), False

    def __enter__(self):
        self.stack.__enter__()
        return self

    def __exit__(self, *a):
        return self.stack.__exit__(*a)

    def sb(self, name, shape, dt=FP32):
        return self.stack.enter_context(self.nc.sbuf_tensor(f"{self.name}_{name}", shape, dt))

    def sem(self, name):
        if not self.started:
            self.started = True
            self.semaphores.start()
        return self.semaphores.take()


def from_first(eng, steps, step):
    step(0, True)
    with eng.Fori(1, steps) as i:
        step(i, False)


def load_inputs(nc, G):
    with Stage(nc, "load") as st:
        loaded, k0_done, tanh_done = st.sem("loaded"), st.sem("k0_done"), st.sem("tanh_done")
        k0 = st.sb("k0", [128, T])
        with nc.Block() as block:

            @block.sync
            def _(sp):
                Stage.semaphores.clear_earlier(sp)
                for dst, src in ((G["x"][:, :, :], G["x_in"]), (G["ident"][:, :], G["ident_in"]),
                                 (G["v0"][:, :, :], G["ctx0N"]), (k0[0:64, :], G["ctx0T"]), (k0[64:128, :], G["ctx0T"]),
                                 (G["gate"][:, 0:4], G["g_xattn"].broadcast_to([128, 4])),
                                 (G["gate"][:, 4:8], G["g_ffn"].broadcast_to([128, 4]))):
                    sp.dma_start(dst, src).then_inc(loaded, 16)

            @block.scalar
            def _(act):
                act.wait_ge(loaded, 112)
                act.activation(G["tanh"][:, :], G["gate"][:, :], ACT.Tanh).then_inc(tanh_done, 1)

            @block.vector
            def _(dve):
                dve.wait_ge(loaded, 112)
                dve.tensor_copy(G["k0"][:, 0, :], k0[:, :]).then_inc(k0_done, 1)
                dve.wait_ge(k0_done, 1)
                dve.tensor_tensor(G["k0"][:, 1, :], k0[:, :], G["k0"][:, 0, :].bitcast(FP32),
                                  ALU.subtract).then_inc(k0_done, 1)


class Rotation:

    def __init__(self, G, st):
        self.G = G
        self.cosT, self.sinT = st.sb("cosT", [128, L]), st.sb("sinT", [128, L])
        self.cosN, self.sinN = st.sb("cosN", [KP, NC * D]), st.sb("sinN", [KP, NC * D])
        self.ct, self.cs = st.sb("ct", [128, 2, L]), st.sb("cs", [128, 2, L])
        self.hi, self.lo = st.sb("hi", [128, 2, L], F32R), st.sb("lo", [128, 2, L], F32R)
        self.cn, self.cm = st.sb("cn", [KP, 2, 2, NC * D]), st.sb("cm", [KP, 2, 2, NC * D])
        self.vs = st.sb("vs", [KP, 2, 2, NC, 2, D], F32R)
        self.tables = st.sem("tables")
        self.in_t, self.in_n = ([st.sem(f"{n}{u}") for u in range(2)] for n in ("in_t", "in_n"))
        self.out_t, self.out_n = ([st.sem(f"{n}{u}") for u in range(2)] for n in ("out_t", "out_n"))
        (self.sin_n, self.sin_t, self.cos_n, self.cos_t, self.sum_t, self.sum_n, self.hi_t, self.hi_n, self.lo_t,
         self.lo_n) = (st.sem(n) for n in ("sin_n", "sin_t", "cos_n", "cos_t", "sum_t", "sum_n", "hi_t", "hi_n",
                                           "lo_t", "lo_n"))

    def load_tables(self, sp):
        for dst, src in ((self.cosT, "cosT"), (self.sinT, "sinT"), (self.cosN, "cosN"), (self.sinN, "sinN")):
            sp.dma_start(dst[:, :], self.G[src]).then_inc(self.tables, 16)

    def load(self, sp, m, u, fresh):
        if not fresh:
            sp.wait_ge(self.lo_t, m - 1)
            sp.wait_ge(self.lo_n, m - 1)
        rows = bass.ds(m * 128, 128)
        sp.dma_start(self.cn[:, u], self.G["ctxN"][bass.ds(m * 2, 2)].rearrange("b p n -> p b n")
                     ).then_inc(self.in_n[u], 16)
        sp.dma_start(self.ct[:, u, :], self.G["ctxT"][rows, :]).then_inc(self.in_t[u], 16)
        sp.dma_start(self.cs[:, u, :], self.G["ctxTs"][rows, :]).then_inc(self.in_t[u], 16)

    def store(self, sp, m, u):
        sp.wait_ge(self.lo_n, m + 1)
        sp.dma_start(self.G["kvn"][bass.ds(m * 2, 2)].rearrange("b p n -> p b n"),
                     self.vs[:, u].rearrange("p b c h d -> p b (c h d)").bitcast(FP32)).then_inc(self.out_n[u], 16)
        sp.wait_ge(self.lo_t, m + 1)
        rows = bass.ds(m * 128, 128)
        sp.dma_start(self.G["kvt_hi"][rows, :], self.hi[:, u, :].bitcast(FP32)).then_inc(self.out_t[u], 16)
        sp.dma_start(self.G["kvt_lo"][rows, :], self.lo[:, u, :].bitcast(FP32)).then_inc(self.out_t[u], 16)

    def wait_stored(self, sp):
        for u in range(2):
            sp.wait_ge(self.out_t[u], B // 4 * 32)
            sp.wait_ge(self.out_n[u], B // 4 * 16)

    def sines(self, pool, i, m, u):
        pool.wait_ge(self.in_n[u], i * 16 + 16)
        pool.tensor_tensor(self.cm[:, u], self.cn[:, u], self.sinN[:, :].unsqueeze(1).broadcast_to([KP, 2, NC * D]),
                           ALU.mult).then_inc(self.sin_n, 1)
        pool.wait_ge(self.in_t[u], i * 32 + 32)
        pool.tensor_tensor(self.cs[:, u, :], self.cs[:, u, :], self.sinT[:, :], ALU.mult).then_inc(self.sin_t, 1)

    def cosines(self, dve, i, m, u):
        dve.wait_ge(self.in_t[u], i * 32 + 32)
        dve.tensor_tensor(self.ct[:, u, :], self.ct[:, u, :], self.cosT[:, :], ALU.mult).then_inc(self.cos_t, 1)
        dve.wait_ge(self.sin_n, m + 1)
        dve.tensor_tensor(self.cn[:, u], self.cn[:, u], self.cosN[:, :].unsqueeze(1).broadcast_to([KP, 2, NC * D]),
                          ALU.mult).then_inc(self.cos_n, 1)

    def sums(self, dve, m, u):
        dve.wait_ge(self.cos_t, m + 1)
        dve.wait_ge(self.sin_t, m + 1)
        dve.tensor_tensor(self.ct[:, u, :], self.ct[:, u, :], self.cs[:, u, :], ALU.add).then_inc(self.sum_t, 1)
        dve.wait_ge(self.cos_n, m + 1)
        cn, cm = (v[:, u].rearrange("p b (c e d) -> p (b c) e d", e=2, d=D // 2) for v in (self.cn, self.cm))
        for e in range(2):
            dve.tensor_tensor(cn[:, :, e], cn[:, :, e], cm[:, :, 1 - e], ALU.add).then_inc(self.sum_n, 1)

    def highs(self, act, i, m, u, fresh):
        if not fresh:
            act.wait_ge(self.out_t[u], i * 32)
            act.wait_ge(self.out_n[u], i * 16)
        act.wait_ge(self.sum_t, m + 1)
        act.activation(self.hi[:, u, :], self.ct[:, u, :], ACT.Copy).then_inc(self.hi_t, 1)
        act.wait_ge(self.sum_n, m * 2 + 2)
        act.activation(self.vs[:, u].rearrange("p b c h d -> p (b c) h d")[:, :, 0, :],
                       self.cn[:, u].rearrange("p b (c d) -> p (b c) d", d=D), ACT.Copy).then_inc(self.hi_n, 1)

    def lows(self, dve, m, u):
        dve.wait_ge(self.hi_t, m + 1)
        dve.tensor_tensor(self.lo[:, u, :], self.ct[:, u, :], self.hi[:, u, :].bitcast(FP32),
                          ALU.subtract).then_inc(self.lo_t, 1)
        dve.wait_ge(self.hi_n, m + 1)
        parts = self.vs[:, u].rearrange("p b c h d -> p (b c) h d")
        dve.tensor_tensor(parts[:, :, 1, :], self.cn[:, u].rearrange("p b (c d) -> p (b c) d", d=D),
                          parts[:, :, 0, :].bitcast(FP32), ALU.subtract).then_inc(self.lo_n, 1)


class FoldWeights:

    def __init__(self, G, st, l):
        HD = H // NH
        if l == 0:
            shapes = {"wq": [HD, NH, H], "wk": [HD, NH, D], "wv": [HD, NH, D], "wo": [HD, NH, H]}
        else:
            shapes = {"wqr": [D, NH, CQ], "wkr": [D, NH, D], "wc": [K, NH, CQ] if l == 2 else [CQH, 2, NH, K],
                      "wq": [K, NH, H], "wv": [K, NH, D], "wo": [K, NH, H]}
        self.tiles = {n: st.sb(n, shape) for n, shape in shapes.items()}
        self.sources = {n: G[f"L{l}_{n}"] for n in shapes}

    def __getitem__(self, n):
        return self.tiles[n]

    def load(self, sp, loaded):
        for n, tile in self.tiles.items():
            sp.dma_start(tile[:], self.sources[n]).then_inc(loaded, 16)

    def wait(self, sp, loaded):
        sp.wait_ge(loaded, 16 * len(self.tiles))


def normalise(nc, G, name, W=None):
    x, xT, PS, ident = G["x"], G["xT"], G["PS"], G["ident"]
    with Stage(nc, name) as st:
        stats, mv = st.sb("stats", [128, NT, 6]), st.sb("mv", [128, NT, 2])
        ve, sd, r, t = (st.sb(n, [128, NT]) for n in ("ve", "sd", "r", "t"))
        xn = st.sb("xn", [128, NT, H])
        chain, var_ready, sqrt_done, xn_ready, tr_done, copied = (
            st.sem(n) for n in ("chain", "var_ready", "sqrt_done", "xn_ready", "tr_done", "copied"))
        weights_in = st.sem("weights_in")
        with nc.Block() as block:

            @block.sync
            def _(sp):
                Stage.semaphores.clear_earlier(sp)
                if W:
                    W.load(sp, weights_in)
                    W.wait(sp, weights_in)

            @block.vector
            def _(dve):
                c = Count(dve, chain)
                for i in range(NT):
                    c.mark(dve.bn_stats(stats[:, i, :], x[:, i, :]))
                for i in range(NT):
                    dve.wait_ge(chain, i + 1)
                    c.mark(dve.bn_aggr(mv[:, i, :], stats[:, i, :]))
                dve.wait_ge(chain, c.n)
                dve.tensor_scalar(ve[:, :], mv[:, :, 1], EPS, None, ALU.add).then_inc(var_ready, 1)
                dve.wait_ge(sqrt_done, 1)
                c.link(dve.reciprocal(r[:, :], sd[:, :]))
                c.link(dve.tensor_tensor(t[:, :], r[:, :], r[:, :], ALU.mult))
                c.link(dve.tensor_tensor(t[:, :], t[:, :], ve[:, :], ALU.mult))
                c.link(dve.tensor_scalar(t[:, :], t[:, :], -0.5, 1.5, ALU.mult, ALU.add))
                c.link(dve.tensor_tensor(r[:, :], r[:, :], t[:, :], ALU.mult))
                for i in range(NT):
                    dve.tensor_scalar(xn[:, i, :], x[:, i, :], mv[:, i, 0:1], r[:, i:i + 1],
                                      ALU.subtract, ALU.mult).then_inc(xn_ready, 1)

            @block.scalar
            def _(act):
                act.wait_ge(var_ready, 1)
                act.activation(sd[:, :], ve[:, :], ACT.Sqrt).then_inc(sqrt_done, 1)
                for i in range(NT):
                    act.wait_ge(tr_done, i + 1)
                    act.activation(xT[:, :, 128 * i:128 * i + 128],
                                   PS[i][:, 0:256].rearrange("p (k n) -> p k n", k=KC), ACT.Copy).then_inc(copied, 1)

            @block.tensor
            def _(pe):
                for i in range(NT):
                    pe.wait_ge(xn_ready, i + 1)
                    for k in range(KC):
                        last = pe.transpose(PS[i][:, 128 * k:128 * k + 128], xn[:, i, 128 * k:128 * k + 128],
                                            ident[:, :])
                    last.then_inc(tr_done, 1)


def fold_small(nc, G, W, A, Bm):
    PS = G["PS"]
    wq, wk, wv, wo = (W[n] for n in ("wq", "wk", "wv", "wo"))
    with Stage(nc, "fold0") as st:
        a_ready, b_ready, a_done, b_done = (st.sem(n) for n in ("a_ready", "b_ready", "a_done", "b_done"))
        with nc.Block() as block:

            @block.sync
            def _(sp):
                Stage.semaphores.clear_earlier(sp)

            @block.tensor
            def _(pe):
                for g in range(4):
                    for h in range(4 * g, 4 * g + 4):
                        for k in range(KC):
                            o = (k * 4 + h % 4) * D
                            last = pe.matmul(PS[g][:, o:o + D], wq[:, h, 128 * k:128 * k + 128], wk[:, h, :],
                                             start=True, stop=True)
                    last.then_inc(a_ready, 1)
                for g in range(4):
                    for h in range(4 * g, 4 * g + 4):
                        o = h % 4 // 2 * H
                        last = pe.matmul(PS[4 + g][h % 2 * 64:h % 2 * 64 + 64, o:o + H], wv[:, h, :], wo[:, h, :],
                                         start=True, stop=True)
                    last.then_inc(b_ready, 1)

            @block.scalar
            def _(act):
                for g in range(4):
                    act.wait_ge(a_ready, g + 1)
                    act.activation(A[:, :, 4 * g:4 * g + 4, :],
                                   PS[g][:, :].rearrange("p (k h d) -> p k h d", k=KC, h=4),
                                   ACT.Copy).then_inc(a_done, 1)

            @block.vector
            def _(dve):
                for g in range(4):
                    dve.wait_ge(b_ready, g + 1)
                    dve.tensor_copy(Bm[:, 2 * g:2 * g + 2, :],
                                    PS[4 + g][:, :].rearrange("p (h n) -> p h n", h=2)).then_inc(b_done, 1)


def fold_latent(nc, G, l, W, A, Bm, Q=None, N=None):
    PS = G["PS"]
    rotated = Q is not None
    wq, wqr, wkr, wv, wo, wc = (W[n] for n in ("wq", "wqr", "wkr", "wv", "wo", "wc"))
    with Stage(nc, f"fold{l}") as st:
        M = None if rotated else st.sb("M", [K, NH, D])
        Nn = N if rotated else st.sb("N", [CQH, 2, NH, D])
        n_ready, b_ready, m_ready, a_ready = (st.sem(n) for n in ("n_ready", "b_ready", "m_ready", "a_ready"))
        n_done, b_done, m_done, a_high, a_done = (
            st.sem(n) for n in ("n_done", "b_done", "m_done", "a_high", "a_done"))
        with nc.Block() as block:

            @block.sync
            def _(sp):
                Stage.semaphores.clear_earlier(sp)

            @block.tensor
            def _(pe):
                for g in range(4):
                    for h in range(4 * g, 4 * g + 4):
                        for c in range(2):
                            o = (c * 4 + h % 4) * D
                            last = pe.matmul(PS[g][0:CQH, o:o + D], wqr[:, h, CQH * c:CQH * c + CQH], wkr[:, h, :],
                                             start=True, stop=True)
                    last.then_inc(n_ready, 1)
                for g in range(4):
                    for h in range(4 * g, 4 * g + 4):
                        o = h % 4 // 2 * H
                        last = pe.matmul(PS[4 + g][h % 2 * 64:h % 2 * 64 + 64, o:o + H], wv[:, h, :], wo[:, h, :],
                                         start=True, stop=True)
                    last.then_inc(b_ready, 1)
                if rotated:
                    for h in range(NH):
                        if h < 4:
                            pe.wait_ge(n_done, h + 1)
                        else:
                            pe.wait_ge(a_done, h - 3)
                        for k in range(KC):
                            last = pe.matmul(PS[h % 4][:, k * CQ:k * CQ + CQ], wq[:, h, 128 * k:128 * k + 128],
                                             wc[:, h, :], start=True, stop=True)
                        last.then_inc(a_ready, 1)
                    return
                for g in range(2):
                    pe.wait_ge(n_done, 4)
                    for h in range(8 * g, 8 * g + 8):
                        for c in range(2):
                            last = pe.matmul(PS[g][:, h % 8 * D:h % 8 * D + D], wc[:, c, h, :], Nn[:, c, h, :],
                                             start=c == 0, stop=c == 1)
                    last.then_inc(m_ready, 1)
                for g in range(4):
                    pe.wait_ge(m_done, g // 2 + 1)
                    pe.wait_ge(b_done, g + 1)
                    for h in range(4 * g, 4 * g + 4):
                        for k in range(KC):
                            o = (k * 4 + h % 4) * D
                            last = pe.matmul(PS[4 + g][:, o:o + D], wq[:, h, 128 * k:128 * k + 128], M[:, h, :],
                                             start=True, stop=True)
                    last.then_inc(a_ready, 1)

            @block.scalar
            def _(act):
                for g in range(4):
                    act.wait_ge(n_ready, g + 1)
                    act.activation(Nn[:, :, 4 * g:4 * g + 4, :],
                                   PS[g][0:CQH, :].rearrange("p (c h d) -> p c h d", c=2, h=4),
                                   ACT.Copy).then_inc(n_done, 1)
                if rotated:
                    for h in range(NH):
                        act.wait_ge(a_ready, h + 1)
                        act.activation(Q[:, 0, h, :, :], PS[h % 4][:, 0:KC * CQ].rearrange("p (k q) -> p k q", k=KC),
                                       ACT.Copy).then_inc(a_high, 1)
                    return
                for g in range(2):
                    act.wait_ge(m_ready, g + 1)
                    act.activation(M[:, 8 * g:8 * g + 8, :], PS[g][:, :].rearrange("p (h d) -> p h d", h=8),
                                   ACT.Copy).then_inc(m_done, 1)
                for g in range(4):
                    act.wait_ge(a_ready, g + 1)
                    act.activation(A[:, :, 4 * g:4 * g + 4, :],
                                   PS[4 + g][:, :].rearrange("p (k h d) -> p k h d", k=KC, h=4),
                                   ACT.Copy).then_inc(a_done, 1)

            @block.vector
            def _(dve):
                for g in range(4):
                    dve.wait_ge(b_ready, g + 1)
                    dve.tensor_copy(Bm[:, 2 * g:2 * g + 2, :],
                                    PS[4 + g][:, :].rearrange("p (h n) -> p h n", h=2)).then_inc(b_done, 1)
                if rotated:
                    for h in range(NH):
                        dve.wait_ge(a_high, h + 1)
                        dve.tensor_tensor(Q[:, 1, h, :, :],
                                          PS[h % 4][:, 0:KC * CQ].rearrange("p (k q) -> p k q", k=KC),
                                          Q[:, 0, h, :, :].bitcast(FP32), ALU.subtract).then_inc(a_done, 1)


QUERY_GROUPS = [(2 * m + o, e) for m in range(NP // 2) for e in range(2) for o in range(2)]


def queries(nc, G, l, A, q_all):
    PS, xT = G["PS"], G["xT"]
    with Stage(nc, f"q{l}") as st:
        q_ready, hi_done, lo_done = (st.sem(n) for n in ("q_ready", "hi_done", "lo_done"))
        groups = QUERY_GROUPS
        with nc.Block() as block:

            @block.tensor
            def _(pe):
                for n, (p, e) in enumerate(groups):
                    if n >= 4:
                        pe.wait_ge(lo_done, 2 * (n - 3))
                    for k in range(KC):
                        last = pe.matmul(PS[n % 4][:, 0:HALF],
                                         A[:, k, 2 * p:2 * p + 2, :].rearrange("p h d -> p (h d)"),
                                         xT[:, k, HALF * e:HALF * e + HALF], start=k == 0, stop=k == KC - 1)
                    last.then_inc(q_ready, 1)

            split_queries(block, PS, q_all, groups, q_ready, hi_done, lo_done)
            store_queries(block, G, q_all, groups, lo_done, st.sem("stored"))


def store_queries(block, G, q_all, groups, lo_done, stored):
    @block.sync
    def _(sp):
        Stage.semaphores.clear_earlier(sp)
        store_groups(sp, G, q_all, groups, lo_done, stored)


def store_groups(sp, G, q_all, groups, lo_done, stored):
    for n in range(1, len(groups), 2):
        p, e = groups[n]
        sp.wait_ge(lo_done, 2 * n + 2)
        b0, c0 = B // 2 * e, 2 * (p - 1) * S
        sp.dma_start(G["q"][b0:b0 + B // 2, :, c0:c0 + 4 * S].rearrange("b p n -> p b n"),
                     q_all[:, b0:b0 + B // 2, 2 * (p - 1):2 * (p + 1), :].rearrange("p b h s -> p b (h s)").bitcast(FP32)
                     ).then_inc(stored, 16)
    sp.wait_ge(stored, 16 * (len(groups) // 2))


def split_queries(block, PS, q_all, groups, q_ready, hi_done, lo_done):
    def places(n, p, e, odd):
        src = PS[n % 4][64 * odd:64 * odd + 64, 0:HALF].rearrange("p (b s) -> p b s", s=S)
        b0 = B // 2 * e
        return src, q_all[0:64, b0:b0 + B // 2, 2 * p + odd, :], q_all[64:128, b0:b0 + B // 2, 2 * p + odd, :]

    @block.scalar
    def _(act):
        for n, (p, e) in enumerate(groups):
            act.wait_ge(q_ready, n + 1)
            for odd in range(2):
                src, hi, _ = places(n, p, e, odd)
                act.activation(hi, src, ACT.Copy).then_inc(hi_done, 1)

    @block.vector
    def _(dve):
        for n, (p, e) in enumerate(groups):
            dve.wait_ge(hi_done, 2 * n + 2)
            for odd in range(2):
                src, hi, lo = places(n, p, e, odd)
                dve.tensor_tensor(lo, src, hi.bitcast(FP32), ALU.subtract).then_inc(lo_done, 1)


def rotated_queries(nc, G, Q, N, q_all):
    PS, xT = G["PS"], G["xT"]
    with Stage(nc, "q2") as st:
        cos, sin = st.sb("cos", [CQH, 2, S]), st.sb("sin", [CQH, 2, S])
        tc, ts = st.sb("tc", [CQH, 3, 2, HALF]), st.sb("ts", [CQH, 3, 2, HALF])
        xs = st.sb("xs", [128, 2, KC, T], F32R)
        x_high, x_split = st.sem("x_high"), st.sem("x_split")
        tables, big_ready, mul_done, rot_done, q_ready, hi_done, lo_done = (
            st.sem(n) for n in ("tables", "big_ready", "mul_done", "rot_done", "q_ready", "hi_done", "lo_done"))
        stored = st.sem("stored")
        units = [(p, e, odd) for p, e in QUERY_GROUPS for odd in range(2)]
        with nc.Block() as block:

            @block.sync
            def _(sp):
                Stage.semaphores.clear_earlier(sp)
                sp.dma_start(cos[:, :, :], G["cosQ"]).then_inc(tables, 16)
                sp.dma_start(sin[:, :, :], G["sinQ"]).then_inc(tables, 16)
                store_groups(sp, G, q_all, [(p, e) for p, e, odd in units if not odd], lo_done, stored)

            @block.tensor
            def _(pe):
                def big(u):
                    p, e, odd = units[u]
                    if u >= 2:
                        pe.wait_ge(mul_done, 4 * (u - 1))
                    for c in range(2):
                        for n in range(3 * KC):
                            k, (pq, px) = n // 3, PARTS[n % 3]
                            last = pe.matmul(PS[4 + u % 2 * 2 + c][0:CQH, 0:HALF],
                                             Q[:, pq, 2 * p + odd, k, CQH * c:CQH * c + CQH],
                                             xs[:, px, k, HALF * e:HALF * e + HALF],
                                             start=n == 0, stop=n == 3 * KC - 1)
                    last.then_inc(big_ready, 1)

                def small(u):
                    p, e, odd = units[u]
                    g = u // 2
                    if g >= 4 and not odd:
                        pe.wait_ge(lo_done, 2 * (g - 3))
                    pe.wait_ge(rot_done, u + 1)
                    for c in range(2):
                        last = pe.matmul(PS[g % 4][64 * odd:64 * odd + 64, 0:HALF], N[:, c, 2 * p + odd, :],
                                         tc[:, u % 3, c, :], start=c == 0, stop=c == 1)
                    last.then_inc(q_ready, 1)

                pe.wait_ge(x_split, 1)
                for u in range(len(units) + 2):
                    if u < len(units):
                        big(u)
                    if u >= 2:
                        small(u - 2)

            def places(g, odd):
                p, e, _ = units[2 * g + odd]
                src = PS[g % 4][64 * odd:64 * odd + 64, 0:HALF].rearrange("p (b s) -> p b s", s=S)
                b0 = B // 2 * e
                return src, q_all[0:64, b0:b0 + B // 2, 2 * p + odd, :], q_all[64:128, b0:b0 + B // 2, 2 * p + odd, :]

            @block.scalar
            def _(act):
                act.activation(xs[:, 0], xT[:, :, :], ACT.Copy).then_inc(x_high, 1)
                for g in range(len(units) // 2):
                    act.wait_ge(q_ready, 2 * g + 2)
                    for odd in range(2):
                        src, hi, _ = places(g, odd)
                        act.activation(hi, src, ACT.Copy).then_inc(hi_done, 1)

            @block.vector
            def _(dve):
                def lows(g):
                    dve.wait_ge(hi_done, 2 * g + 2)
                    for odd in range(2):
                        src, hi, lo = places(g, odd)
                        dve.tensor_tensor(lo, src, hi.bitcast(FP32), ALU.subtract).then_inc(lo_done, 1)

                dve.wait_ge(x_high, 1)
                dve.tensor_tensor(xs[:, 1], xT[:, :, :], xs[:, 0].bitcast(FP32), ALU.subtract).then_inc(x_split, 1)
                dve.wait_ge(tables, 32)
                for u in range(len(units)):
                    dve.wait_ge(big_ready, u + 1)
                    if u >= 3:
                        dve.wait_ge(q_ready, u - 2)
                    for c in range(2):
                        src = PS[4 + u % 2 * 2 + c][0:CQH, 0:HALF].rearrange("p (b s) -> p b s", s=S)
                        for dst, tab in ((tc[:, u % 3, c, :], cos[:, c, :]), (ts[:, u % 3, 1 - c, :], sin[:, 1 - c, :])):
                            dve.tensor_tensor(dst.rearrange("p (b s) -> p b s", s=S), src,
                                              tab.unsqueeze(1).broadcast_to([CQH, B // 2, S]),
                                              ALU.mult).then_inc(mul_done, 1)
                    if u >= 5 and u % 2:
                        lows((u - 5) // 2)
                for g in (2, 1):
                    lows(len(units) // 2 - g)

            @block.gpsimd
            def _(pool):
                for u in range(len(units)):
                    pool.wait_ge(mul_done, 4 * u + 4)
                    pool.tensor_tensor(tc[:, u % 3], tc[:, u % 3], ts[:, u % 3], ALU.add).then_inc(rot_done, 1)


def attend_short(nc, G, q_all, ctxT):
    PS, ident, k0, v0 = G["PS"], G["ident"], G["k0"], G["v0"]
    SCALE = float(H // NH) ** -0.5
    W0 = 4 * 128
    with Stage(nc, "att0") as st:
        mask = st.sb("mask", [128, NT, S])
        qst = st.sb("qst", [128, 2, NH * S], F32R)
        pw = st.sb("p", [128, 2, (NT - 1) * S + 128])
        pT = st.sb("pT", [S, 2, T])
        mx, rs = st.sb("mx", [128, 2, NT]), st.sb("rs", [128, 2, NT])
        p = [pw[:, s, 0:NT * S].rearrange("p (t k) -> p t k", t=NT) for s in range(2)]
        oc = st.sb("oc", [128, 2, NT + 1, D])
        cT = st.sb("cT", [D, 2, NH, S])
        pad_done = st.sem("pad_done")
        mask_in, s_ready, masked, maxed, centred, exp_done, summed, inverted = (
            st.sem(n) for n in ("mask_in", "s_ready", "masked", "maxed", "centred", "exp_done", "summed", "inverted"))
        q_in = [st.sem(f"q_in{s}") for s in range(2)]
        t_ready, t_copied, o_ready, o_scaled, c_ready, c_copied, placed = (
            st.sem(n) for n in ("t_ready", "t_copied", "o_ready", "o_scaled", "c_ready", "c_copied", "placed"))
        rot = Rotation(G, st)

        def pairs(eng, step):
            def two(i, first):
                for u in range(2):
                    step(i, 2 * i + u, u, first and u == 0, first)

            from_first(eng, B // 4, two)

        with nc.Block() as block:

            @block.sync
            def _(sp):
                Stage.semaphores.clear_earlier(sp)
                sp.dma_start(mask[:, :, :], G["mask0"]).then_inc(mask_in, 16)

                def step(i, m, u, first, fresh):
                    for s in range(2):
                        if not first:
                            sp.wait_ge(s_ready, 2 * m + s - 1)
                        sp.dma_start(qst[:, s, :].bitcast(FP32),
                                     q_all[bass.ds(2 * m + s, 1)].rearrange("b p n -> (b p) n")).then_inc(q_in[s], 16)
                    if first:
                        rot.load_tables(sp)
                    rot.load(sp, m, u, fresh)
                    if not fresh:
                        rot.store(sp, m - 2, u)

                pairs(sp, step)
                for u in range(2):
                    rot.store(sp, B // 2 - 2 + u, u)
                rot.wait_stored(sp)

            @block.tensor
            def _(pe):
                def scores(m, first):
                    for s in range(2):
                        pe.wait_ge(q_in[s], m * 16 + 16)
                        if not first:
                            pe.wait_ge(masked, 2 * m + s - 1)
                        for t in range(NT):
                            for part in range(2):
                                last = pe.matmul(PS[s][:, t * S:t * S + S], qst[:, s, 128 * t:128 * t + 128],
                                                 k0[:, part, bass.ds((2 * m + s) * S, S)],
                                                 start=part == 0, stop=part == 1)
                        last.then_inc(s_ready, 1)

                def step(m, first, last_step):
                    for s in range(2):
                        pe.wait_ge(exp_done, 2 * m + s + 1)
                        if not (first and s == 0):
                            pe.wait_ge(t_copied, 2 * (2 * m + s))
                        for t in range(NT):
                            last = pe.transpose(PS[2 + t // 4][:, t % 4 * 128:t % 4 * 128 + 128],
                                                pw[:, s, t * S:t * S + 128], ident[:, :])
                            if t in (3, NT - 1):
                                last.then_inc(t_ready, 1)
                    for s in range(2):
                        pe.wait_ge(t_copied, 2 * (2 * m + s) + 2)
                        if not first:
                            pe.wait_ge(o_scaled, 2 * m + s - 1)
                        for t in range(NT):
                            last = pe.matmul(PS[4 + s][:, t * D:t * D + D], pT[:, s, 128 * t:128 * t + 128],
                                             v0[:, bass.ds(2 * m + s, 1), :].rearrange("p b d -> p (b d)"),
                                             start=True, stop=True)
                        last.then_inc(o_ready, 1)
                    if not last_step:
                        scores(m + 1, False)
                    for s in range(2):
                        pe.wait_ge(o_scaled, 2 * m + s + 1)
                        if not first:
                            pe.wait_ge(c_copied, 4 * m + 2 * s - 2)
                        for t in range(0, NT, 2):
                            last = pe.transpose(PS[6 + s][:, 64 * t:64 * t + 128],
                                                oc[:, s, t:t + 2, :].rearrange("p t d -> p (t d)"), ident[:, :])
                        last.then_inc(c_ready, 1)

                pe.wait_ge(pad_done, 2)
                scores(0, True)
                step(0, True, False)
                with pe.Fori(1, B // 2 - 1) as m:
                    step(m, False, False)
                step(B // 2 - 1, False, True)

            @block.vector
            def _(dve):
                dve.wait_ge(mask_in, 16)
                dve.wait_ge(rot.tables, 64)

                def step(i, m, u, first, fresh):
                    for s in range(2):
                        n = 2 * m + s + 1
                        dve.wait_ge(s_ready, n)
                        dve.tensor_tensor(p[s], PS[s][:, 0:NT * S].rearrange("p (t k) -> p t k", t=NT),
                                          mask[:, :, :], ALU.add).then_inc(masked, 1)
                        dve.wait_ge(masked, n)
                        dve.tensor_reduce(mx[:, s, :], p[s], AX.X, ALU.max).then_inc(maxed, 1)
                        dve.wait_ge(maxed, n)
                        dve.tensor_tensor(p[s], p[s], mx[:, s, :].unsqueeze(2).broadcast_to([128, NT, S]),
                                          ALU.subtract).then_inc(centred, 1)
                    rot.cosines(dve, i, m, u)
                    if not first:
                        rot.lows(dve, m - 1, 1 - u)
                    for s in range(2):
                        n = 2 * m + s + 1
                        dve.wait_ge(exp_done, n)
                        dve.tensor_reduce(rs[:, s, :], p[s], AX.X, ALU.add).then_inc(summed, 1)
                        dve.wait_ge(summed, n)
                        dve.reciprocal(rs[:, s, :], rs[:, s, :]).then_inc(inverted, 1)
                    for s in range(2):
                        n = 2 * m + s + 1
                        dve.wait_ge(inverted, n)
                        dve.wait_ge(o_ready, n)
                        dve.tensor_tensor(oc[:, s, 0:NT, :], PS[4 + s][:, 0:NT * D].rearrange("p (t d) -> p t d", t=NT),
                                          rs[:, s, :].unsqueeze(2).broadcast_to([128, NT, D]),
                                          ALU.mult).then_inc(o_scaled, 1)
                    rot.sums(dve, m, u)

                pairs(dve, step)
                rot.lows(dve, B // 2 - 1, 1)

            @block.scalar
            def _(act):
                def step(i, m, u, first, fresh):
                    for s in range(2):
                        act.wait_ge(centred, 2 * m + s + 1)
                        act.activation(p[s], p[s], ACT.Exp, scale=SCALE).then_inc(exp_done, 1)
                    for s in range(2):
                        for g, (a, z) in enumerate(((0, W0), (W0, T))):
                            act.wait_ge(t_ready, 2 * (2 * m + s) + g + 1)
                            act.activation(pT[:, s, a:z], PS[2 + g][0:S, 0:z - a], ACT.Copy).then_inc(t_copied, 1)
                    for s in range(2):
                        if not first:
                            act.wait_ge(placed, 4 * m)
                        act.wait_ge(c_ready, 2 * m + s + 1)
                        for odd in range(2):
                            copy_context(act, PS[6 + s], cT[:, s], odd, c_copied)
                    rot.highs(act, i, m, u, fresh)

                pairs(act, step)

            @block.gpsimd
            def _(pool):
                pool.memset(oc[:, :, NT, :], 0.0).then_inc(pad_done, 1)
                pool.memset(pw[:, :, NT * S:], 0.0).then_inc(pad_done, 1)
                pool.wait_ge(rot.tables, 64)

                def place(m):
                    for s in range(2):
                        pool.wait_ge(c_copied, 2 * (2 * m + s) + 2)
                        for odd in range(2):
                            place_context(pool, ctxT, cT[:, s], (2 * m + s) * S, odd, placed)
                            pool.wait_ge(placed, 2 * (2 * m + s) + odd + 1)

                def step(i, m, u, first, fresh):
                    rot.sines(pool, i, m, u)
                    if not first:
                        pool.wait_ge(rot.sin_t, m + 1)
                        place(m - 1)

                pairs(pool, step)
                pool.wait_ge(rot.sin_t, B // 2)
                place(B // 2 - 1)


def copy_context(act, bank, cT, odd, c_copied):
    n = (NT + 1 - odd) // 2
    tiles = cT.rearrange("p h s -> p (h s)").rearrange("p (t r) -> p t r", r=128)
    act.activation(tiles[:, odd:NT:2, :], bank[64 * odd:64 * odd + D, 0:128 * n].rearrange("p (t r) -> p t r", r=128),
                   ACT.Copy).then_inc(c_copied, 1)


def place_context(pool, ctxT, cT, at, odd, placed):
    pool.tensor_copy(ctxT[64 * odd:64 * odd + 64, :, bass.ds(at, S)],
                     cT.rearrange("p (h two) s -> p two h s", two=2)[:, odd]).then_inc(placed, 1)


def attend_long(nc, G, l, q_all, ctxT):
    PS, ident = G["PS"], G["ident"]
    PST, PSO = PS[6], PS[7]
    GROUPS = ((0, 2), (2, 4), (4, 7))
    SLOT = (0, 1, 2, 3, 0, 1, 2, 3, 4, 0, 1, 2, 3, 4)
    HC = NC // 2
    SUMS = {2: (0, 0), 3: (0, HC), 4: (1, 0), 5: (1, HC), 0: (2, 0), 1: (2, HC)}
    N = B * NT
    with Stage(nc, f"att{l}") as st:
        qst = st.sb("qst", [128, 2, NH * S], F32R)
        kst = st.sb("kst", [128, 2, 2, L], F32R)
        vst = st.sb("vst", [KP, 2, NC, 2 * D], F32R)
        p = st.sb("p", [128, 2, L])
        raw = st.sb("raw", [KP, NS, CG, 128])
        pT = st.sb("pT", [KP, 2, 5, NC, 128], F32R)
        nm = st.sb("nm", [128, 2])
        sums, rs = st.sb("sums", [128, 2, NT]), st.sb("rs", [128, NT])
        low = st.sb("low", [D, 384])
        cu, rsb = st.sb("cu", [D, 2, T]), st.sb("rsb", [D, 2, T])
        qk_in, v_in = ([st.sem(f"{n}{s}") for s in range(2)] for n in ("qk_in", "v_in"))
        s_ready, max_ready, exp_done, t_ready, raw_ready, mid_ready, act_high, dve_high, pool_low, dve_low = (
            st.sem(n) for n in ("s_ready", "max_ready", "exp_done", "t_ready", "raw_ready", "mid_ready", "act_high",
                                "dve_high", "pool_low", "dve_low"))
        o_ready, half_copied, o_added, inverted, spread, spread_copied, placed = (
            st.sem(n) for n in ("o_ready", "half_copied", "o_added", "inverted", "spread", "spread_copied", "placed"))

        def emit(eng, steps):
            steps(0, True, False)
            with eng.Fori(1, B // 2 - 1) as i:
                steps(i, False, False)
            steps(B // 2 - 1, False, True)

        with nc.Block() as block:

            @block.sync
            def _(sp):
                Stage.semaphores.clear_earlier(sp)

                def load(i, s):
                    b = 2 * i + s
                    sp.dma_start(qst[:, s, :].bitcast(FP32),
                                 q_all[bass.ds(b, 1)].rearrange("b p n -> (b p) n")).then_inc(qk_in[s], 16)
                    for half in range(2):
                        for part, src in enumerate(("kvt_hi", "kvt_lo")):
                            sp.dma_start(kst[64 * half:64 * half + 64, s, part, :].bitcast(FP32),
                                         G[src][bass.ds(b * D, D), :]).then_inc(qk_in[s], 16)
                    sp.dma_start(vst[:, s].rearrange("p c d -> p (c d)").bitcast(FP32),
                                 G["kvn"][bass.ds(b, 1)].rearrange("b p n -> (b p) n")).then_inc(v_in[s], 16)

                load(0, 0)
                load(0, 1)
                with sp.Fori(1, B // 2) as i:
                    for s in range(2):
                        sp.wait_ge(o_ready, 3 * (2 * i + s - 1))
                        load(i, s)

            @block.tensor
            def _(pe):
                def scores(j, over):
                    s, t = j // NT % 2, j % NT
                    for c in over:
                        for part in range(2):
                            last = pe.matmul(PS[3 * (j % 2) + c][:, 0:SB], qst[:, s, 128 * t:128 * t + 128],
                                             kst[:, s, part, SB * c:SB * c + SB], start=part == 0, stop=part == 1)
                    if over[-1] == NS - 1:
                        last.then_inc(s_ready, 1)

                def weigh(i, j, which, over):
                    g, c0 = SUMS[which]
                    done = 2 * i + j // NT - (1 if g == 2 else 0)
                    s = (j // NT + (1 if g == 2 else 0)) % 2
                    t0, t1 = GROUPS[g]
                    first = SLOT[t0 + NT * s]
                    if c0 + over[0] == 0:
                        if g == 0:
                            pe.wait_ge(v_in[s], 16 * (i + 1))
                        pe.wait_ge(pool_low, 2 * (done * NT + t1))
                        pe.wait_ge(dve_low, done * NT + t1)
                        if not (isinstance(done, int) and done == g == 0):
                            pe.wait_ge(o_added, 3 * done + g)
                        if g == 2:
                            pe.wait_ge(spread_copied, 2 * (done + 1))
                    for c in over:
                        c += c0
                        for part in range(2):
                            last = pe.matmul(PSO[:, 0:128 * (t1 - t0)], vst[:, s, c, :],
                                             pT[:, part, first:first + t1 - t0, c, :],
                                             start=c == part == 0, stop=c == NC - 1 and part == 1)
                    if c == NC - 1:
                        last.then_inc(o_ready, 1)

                def spread_sums(done, g):
                    if g == 0:
                        pe.wait_ge(inverted, done)
                        pe.wait_ge(o_added, 3 * done - 1)
                    else:
                        pe.wait_ge(spread_copied, 2 * done - 1)
                    for t in range(4 * g, min(4 * g + 4, NT)):
                        last = pe.matmul(PSO[:, t % 4 * 128:t % 4 * 128 + 128],
                                         rs[:, t:t + 1].broadcast_to([128, 128]), ident[:, :], start=True, stop=True)
                    last.then_inc(spread, 1)

                def steps(i, first, last_pair):
                    for j in range(2 * NT):
                        n = i * 2 * NT + j
                        t = j % NT
                        start = first and j < NT
                        ahead = not (last_pair and j >= 2 * NT - 2)
                        weighs = t in SUMS and not (start and t < 2)
                        for g in range(NS):
                            if g == 0:
                                pe.wait_ge(exp_done, n + 1)
                            if g == 2:
                                pe.wait_ge(mid_ready, n + 1)
                            elif not (first and j == g == 0):
                                pe.wait_ge(raw_ready, 2 * n + g)
                            for c in range(CG * g, CG * g + CG):
                                last = pe.transpose(PST[0:KP, c % CG * 128:c % CG * 128 + 128],
                                                    p[:, j % 2, KP * c:KP * c + KP], ident[:, :])
                            last.then_inc(t_ready, 1)
                            if g == 0 and ahead:
                                if (j + 2) % NT == 0:
                                    m = i + (j + 2) // (2 * NT)
                                    pe.wait_ge(qk_in[(j + 2) // NT % 2], m * 80 + 80)
                                scores(j + 2, (0, 1))
                            if g == 1:
                                if ahead:
                                    scores(j + 2, (2,))
                                if weighs:
                                    weigh(i, j, t, range(2))
                            if g == 2 and weighs:
                                weigh(i, j, t, range(2, HC))
                            if g > 0 and t == NT - 1:
                                spread_sums(2 * i + j // NT + 1, g - 1)

                pe.wait_ge(qk_in[0], 80)
                scores(0, (0, 1, 2))
                scores(1, (0, 1, 2))
                emit(pe, steps)
                for t in range(2):
                    weigh(B // 2, t, t, range(HC))

            @block.vector
            def _(dve):
                def row_max(j, n):
                    dve.wait_ge(s_ready, n + 1)
                    dve.tensor_reduce(nm[:, j % 2:j % 2 + 1], banks(PS, 3 * (j % 2)), AX.XY, ALU.max,
                                      negate=True).then_inc(max_ready, 1)

                def copy_middle(n, very_first):
                    if not very_first:
                        dve.wait_ge(dve_low, n)
                    dve.wait_ge(t_ready, 3 * n + 2)
                    dve.tensor_copy(raw[:, 1], PST[0:KP, :].rearrange("p (c r) -> p c r", c=CG)).then_inc(mid_ready, 1)

                def split(n, j, g):
                    o, sl = slice(CG * g, CG * g + CG), SLOT[j]
                    if g == 2:
                        dve.wait_ge(raw_ready, 2 * n + 2)
                    else:
                        dve.wait_ge(mid_ready, n + 1)
                    dve.tensor_copy(pT[:, 0, sl, o, :], raw[:, g]).then_inc(dve_high, 1)
                    if g == 1:
                        dve.wait_ge(dve_high, 2 * n + 2)
                        dve.tensor_tensor(pT[:, 1, sl, o, :], raw[:, g], pT[:, 0, sl, o, :].bitcast(FP32),
                                          ALU.subtract).then_inc(dve_low, 1)

                def add_halves(done, s, g):
                    t0, t1 = GROUPS[g]
                    if g == 0 and not (isinstance(done, int) and done < 2):
                        dve.wait_ge(placed, 2 * (done - 1))
                    dve.wait_ge(half_copied, 3 * done + g + 1)
                    dve.tensor_tensor(cu[:, s, 128 * t0:128 * t1], PSO[0:D, 0:128 * (t1 - t0)],
                                      low[:, 0:128 * (t1 - t0)], ALU.add).then_inc(o_added, 1)

                def steps(i, first, last_pair):
                    for j in range(2 * NT):
                        n = i * 2 * NT + j
                        t, s = j % NT, j // NT
                        if t == 2 and not (first and s == 0):
                            add_halves(2 * i + s - 1, 1 - s, 2)
                        if t in (4, 6):
                            add_halves(2 * i + s, s, t // 2 - 2)
                        if t == NT - 1:
                            if not (first and s == 0):
                                dve.wait_ge(spread, 2 * (2 * i + s))
                            dve.wait_ge(exp_done, n + 1)
                            dve.reciprocal(rs[:, :], sums[:, s, :]).then_inc(inverted, 1)
                        copy_middle(n, first and j == 0)
                        if not (last_pair and j >= 2 * NT - 2):
                            row_max(j, n + 2)
                        split(n, j, 2)
                        split(n, j, 1)

                row_max(0, 0)
                row_max(1, 1)
                emit(dve, steps)
                add_halves(B - 1, 1, 2)

            @block.scalar
            def _(act):
                def exps(j, n):
                    act.wait_ge(max_ready, n + 1)
                    act.activation(p[:, j % 2, :].rearrange("p (c k) -> p c k", c=NS), banks(PS, 3 * (j % 2)),
                                   ACT.Exp, bias=nm[:, j % 2:j % 2 + 1],
                                   accum_out=sums[:, j // NT % 2, j % NT:j % NT + 1]).then_inc(exp_done, 1)

                def copy(n, j, g, very_first):
                    if not very_first:
                        act.wait_ge(pool_low, 2 * n - 1 + g // 2)
                    act.wait_ge(t_ready, 3 * n + g + 1)
                    act.activation(raw[:, g], PST[0:KP, :].rearrange("p (c r) -> p c r", c=CG),
                                   ACT.Copy).then_inc(raw_ready, 1)

                def high(n, j):
                    act.wait_ge(raw_ready, 2 * n + 1)
                    act.activation(pT[:, 0, SLOT[j], 0:CG, :], raw[:, 0], ACT.Copy).then_inc(act_high, 1)

                def half(done, g):
                    t0, t1 = GROUPS[g]
                    if not (isinstance(done, int) and done == g == 0):
                        act.wait_ge(o_added, 3 * done + g)
                    act.wait_ge(o_ready, 3 * done + g + 1)
                    act.activation(low[:, 0:128 * (t1 - t0)], PSO[D:2 * D, 0:128 * (t1 - t0)],
                                   ACT.Copy).then_inc(half_copied, 1)

                def copy_spread(done, s, g):
                    a, z = 512 * g, min(512 * g + 512, T)
                    if g == 0 and not (isinstance(done, int) and done <= 2):
                        act.wait_ge(placed, 2 * (done - 2))
                    act.wait_ge(spread, 2 * (done - 1) + g + 1)
                    act.activation(rsb[:, s, a:z], PSO[0:D, 0:z - a], ACT.Copy).then_inc(spread_copied, 1)

                def steps(i, first, last_pair):
                    for j in range(2 * NT):
                        n = i * 2 * NT + j
                        t, s = j % NT, j // NT
                        if t == 2 and not (first and s == 0):
                            half(2 * i + s - 1, 2)
                        if t in (4, 6):
                            half(2 * i + s, t // 2 - 2)
                        copy(n, j, 0, first and j == 0)
                        if t == 0 and not (first and s == 0):
                            copy_spread(2 * i + s, 1 - s, 1)
                        if not (last_pair and j == 2 * NT - 1):
                            exps(j + 1, n + 1)
                        if t == NT - 1:
                            copy_spread(2 * i + s + 1, s, 0)
                        high(n, j)
                        copy(n, j, 2, first and j == 0)

                exps(0, 0)
                emit(act, steps)
                copy_spread(B, 1, 1)
                half(B - 1, 2)

            @block.gpsimd
            def _(pool):
                def steps(i, first, last_pair):
                    for j in range(2 * NT):
                        n = i * 2 * NT + j
                        for g in (0, 2):
                            o, sl = slice(CG * g, CG * g + CG), SLOT[j]
                            pool.wait_ge(*((act_high, n + 1) if g == 0 else (dve_high, 2 * n + 1)))
                            pool.tensor_tensor(pT[:, 1, sl, o, :], raw[:, g], pT[:, 0, sl, o, :].bitcast(FP32),
                                               ALU.subtract).then_inc(pool_low, 1)
                        if j % NT in (2, 3) and not (first and j < NT):
                            place(2 * i + j // NT, (j // NT + 1) % 2, 2 * (n + 1), j % NT - 2)

                def place(done, s, lows, odd):
                    pool.wait_ge(o_added, 3 * done)
                    pool.wait_ge(spread_copied, 2 * done)
                    pool.wait_ge(pool_low, lows)
                    a, r = (m[:, s, :].rearrange("p (h two s) -> p two h s", two=2, s=S)[:, odd] for m in (cu, rsb))
                    pool.tensor_tensor(ctxT[64 * odd:64 * odd + 64, :, bass.ds((done - 1) * S, S)], a, r,
                                       ALU.mult).then_inc(placed, 1)
                    pool.wait_ge(placed, 2 * (done - 1) + odd + 1)

                emit(pool, steps)
                place(B, 1, 2 * N, 0)
                place(B, 1, 2 * N, 1)


def banks(PS, first):
    return PS.all[:, first * 512:(first + NS) * 512].rearrange("p (c k) -> p c k", c=NS)[:, :, 0:SB]


def project_out(nc, G, l, Bm, ctxT):
    PS, x = G["PS"], G["x"]
    with Stage(nc, f"out{l}") as st:
        o_ready, x_done = st.sem("o_ready"), st.sem("x_done")
        with nc.Block() as block:

            @block.sync
            def _(sp):
                Stage.semaphores.clear_earlier(sp)

            @block.tensor
            def _(pe):
                for t in range(NT):
                    for h in range(NP):
                        last = pe.matmul(PS[t][:, 0:H], ctxT[:, h, 128 * t:128 * t + 128], Bm[:, h, :],
                                         start=h == 0, stop=h == NP - 1)
                    last.then_inc(o_ready, 1)

            @block.vector
            def _(dve):
                for t in range(NT):
                    dve.wait_ge(o_ready, t + 1)
                    dve.scalar_tensor_tensor(x[:, t, :], PS[t][:, 0:H], G["tanh"][:, l:l + 1], x[:, t, :],
                                             ALU.mult, ALU.add).then_inc(x_done, 1)


def route(nc, G, l, E, top, kind, rows, groups_per_expert):
    PS, xT, ident = G["PS"], G["xT"], G["ident"]
    with Stage(nc, f"route{l}") as st:
        wr, tie = st.sb("wr", [128, KC, E]), st.sb("tie", [128, E * E])
        bias = st.sb("bias", [128, E])
        lg, e, key = st.sb("lg", [128, NT, E]), st.sb("e", [128, NT, E]), st.sb("key", [128, NT, E])
        gt, eq = st.sb("gt", [128, NT, E * E]), st.sb("eq", [128, NT, E * E])
        rank, z = st.sb("rank", [128, NT, E]), st.sb("z", [128, NT])
        comb, combT = st.sb("comb", [128, NT, rows]), st.sb("combT", [rows, T])
        in_w, lg_ready, to_exp, exp_done, chain, comb_ready, tr_ready, tr_copied, stored = (
            st.sem(n) for n in ("in_w", "lg_ready", "to_exp", "exp_done", "chain", "comb_ready", "tr_ready",
                                "tr_copied", "stored"))
        loads = [(wr[:, :, :], G[f"L{l}_router"]), (tie[:, :], G[f"tie{E}"])]
        if kind == "renormalised":
            loads.append((bias[:, :], G["L3_bias"].broadcast_to([128, E])))
        with nc.Block() as block:

            @block.sync
            def _(sp):
                Stage.semaphores.clear_earlier(sp)
                for dst, src in loads:
                    sp.dma_start(dst, src).then_inc(in_w, 16)
                sp.wait_ge(tr_copied, 2)
                sp.dma_start(G["comb"][0:rows * groups_per_expert, :].rearrange("(e g) n -> e g n", e=rows),
                             combT[:, :].unsqueeze(1).broadcast_to([rows, groups_per_expert, T])).then_inc(stored, 16)
                sp.wait_ge(stored, 16)

            @block.tensor
            def _(pe):
                pe.wait_ge(in_w, 16 * len(loads))
                for t in range(NT):
                    for k in range(KC):
                        last = pe.matmul(PS[0][:, t * E:t * E + E], xT[:, k, 128 * t:128 * t + 128], wr[:, k, :],
                                         start=k == 0, stop=k == KC - 1)
                last.then_inc(lg_ready, 1)
                pe.wait_ge(comb_ready, 1)
                for t in range(NT):
                    last = pe.transpose(PS[1 + t // 4][0:rows, t % 4 * 128:t % 4 * 128 + 128], comb[:, t, :],
                                        ident[:, :])
                    if t in (3, NT - 1):
                        last.then_inc(tr_ready, 1)

            @block.scalar
            def _(act):
                act.wait_ge(to_exp, 1)
                act.activation(e[:, :, :], (lg if kind == "sigmoid" else e)[:, :, :], ACT.Exp,
                               scale=-1.0 if kind == "sigmoid" else 1.0).then_inc(exp_done, 1)
                for g, (a, b) in enumerate(((0, 512), (512, T))):
                    act.wait_ge(tr_ready, g + 1)
                    act.activation(combT[:, a:b], PS[1 + g][0:rows, 0:b - a], ACT.Copy).then_inc(tr_copied, 1)

            @block.vector
            def _(dve):
                c = Count(dve, chain)
                dve.wait_ge(lg_ready, 1)
                dve.wait_ge(in_w, 16 * len(loads))
                logits = PS[0][:, 0:NT * E].rearrange("p (t e) -> p t e", t=NT)
                wide = [128, NT, E]
                if kind == "renormalised":
                    c.link(dve.tensor_tensor(lg[:, :, :], logits, bias[:, :].unsqueeze(1).broadcast_to(wide), ALU.add))
                else:
                    c.link(dve.tensor_copy(lg[:, :, :], logits))
                if kind == "sigmoid":
                    dve.engine_nop().then_inc(to_exp, 1)
                    dve.wait_ge(exp_done, 1)
                    c.link(dve.tensor_scalar(e[:, :, :], e[:, :, :], 1.0, None, ALU.add))
                    c.link(dve.reciprocal(e[:, :, :], e[:, :, :]))
                    values = e
                else:
                    c.link(dve.tensor_reduce(z[:, :], lg[:, :, :], AX.X, ALU.max))
                    dve.tensor_tensor(e[:, :, :], lg[:, :, :], z[:, :].unsqueeze(2).broadcast_to(wide),
                                      ALU.subtract).then_inc(to_exp, 1)
                    values = lg
                for t in range(NT):
                    other = values[:, t, :].unsqueeze(1).broadcast_to([128, E, E])
                    own = values[:, t, :].unsqueeze(2).broadcast_to([128, E, E])
                    c.mark(dve.tensor_tensor(gt[:, t, :].rearrange("p (a b) -> p a b", a=E), other, own, ALU.is_gt))
                    c.mark(dve.tensor_tensor(eq[:, t, :].rearrange("p (a b) -> p a b", a=E), other, own, ALU.is_equal))
                dve.wait_ge(chain, c.n)
                c.link(dve.tensor_tensor(eq[:, :, :], eq[:, :, :], tie[:, :].unsqueeze(1).broadcast_to([128, NT, E * E]),
                                         ALU.mult))
                c.link(dve.tensor_tensor(gt[:, :, :], gt[:, :, :], eq[:, :, :], ALU.add))
                c.link(dve.tensor_reduce(rank[:, :, :], gt[:, :, :].rearrange("p t (a b) -> p t a b", a=E), AX.X,
                                         ALU.add))
                c.link(dve.tensor_scalar(rank[:, :, :], rank[:, :, :], float(top), None, ALU.is_lt))
                if rows > E:
                    c.link(dve.memset(comb[:, :, E:E + 2], 1.0))
                    c.link(dve.memset(comb[:, :, E + 2:rows], 0.0))
                if kind != "sigmoid":
                    dve.wait_ge(exp_done, 1)
                if kind == "sigmoid":
                    dve.tensor_tensor(comb[:, :, 0:E], e[:, :, :], rank[:, :, :], ALU.mult).then_inc(comb_ready, 1)
                    return
                c.link(dve.tensor_tensor(key[:, :, :], e[:, :, :], rank[:, :, :], ALU.mult))
                over = e if kind == "softmax" else key
                c.link(dve.tensor_reduce(z[:, :], over[:, :, :], AX.X, ALU.add))
                c.link(dve.reciprocal(z[:, :], z[:, :]))
                dve.tensor_tensor(comb[:, :, 0:E], key[:, :, :], z[:, :].unsqueeze(2).broadcast_to(wide),
                                  ALU.mult).then_inc(comb_ready, 1)


def experts(nc, G, l, chunks, group_rows, W):
    PS, xT, x, ident = G["PS"], G["xT"], G["x"], G["ident"]
    GU = 2 * KC * 128
    groups = 128 // group_rows
    with Stage(nc, f"moe{l}") as st:
        raw = st.sb("raw", [128, 2, GU + H])
        w = st.sb("w", [128, 2, 2, GU + H], F32R)
        xs = st.sb("xs", [128, 2, KC, T], F32R)
        cb = st.sb("cb", [128, 2, T])
        sg, sc, hf = st.sb("sg", [128, 2, HALF]), st.sb("sc", [128, 2, HALF]), st.sb("hf", [128, 2, HALF])
        h = st.sb("h", [128, 2, 2, 2, HALF], F32R)
        oT = st.sb("oT", [128, KC, T])
        w_in = [st.sem(f"w_in{s}") for s in range(2)]
        cb_in = [st.sem(f"cb_in{s}") for s in range(2)]
        x_high, x_split, gu_high, gu_split, d_high, d_split = (
            st.sem(n) for n in ("x_high", "x_split", "gu_high", "gu_split", "d_high", "d_split"))
        gu_ready, silu_done, comb_done, h_made, h_high, h_split, d_done = (
            st.sem(n) for n in ("gu_ready", "silu_done", "comb_done", "h_made", "h_high", "h_split", "d_done"))
        o_copied, tr_ready, x_done = (st.sem(n) for n in ("o_copied", "tr_ready", "x_done"))
        weights_in = st.sem("weights_in")
        w_dram = G[f"L{l}_experts"]

        def emit(eng, chunk):
            chunk(0, 0, True, True)
            chunk(0, 1, False, True)
            done = (chunks - 1) // 2
            with eng.Fori(1, done) as i:
                for s in range(2):
                    chunk(i, s, False, True)
            for c in range(2 * done, chunks):
                chunk(done, c % 2, False, c < chunks - 1)

        def following(i, s):
            return (i, 1) if s == 0 else (i + 1, 0)

        with nc.Block() as block:

            @block.sync
            def _(sp):
                Stage.semaphores.clear_earlier(sp)

                def chunk(i, s, first, more):
                    c = 2 * i + s
                    if not isinstance(i, int) or i:
                        sp.wait_ge(d_split, c - 1)
                    sp.dma_start(raw[:, s, :], w_dram[bass.ds(c * 128, 128), :]).then_inc(w_in[s], 16)
                    if not isinstance(i, int) or i:
                        sp.wait_ge(comb_done, 2 * c - 2)
                    sp.dma_start(cb[:, s, :], G["comb"][bass.ds(c * groups, groups), :].unsqueeze(1)
                                 .broadcast_to([groups, group_rows, T])).then_inc(cb_in[s], 16)

                emit(sp, chunk)
                if W:
                    W.load(sp, weights_in)
                    W.wait(sp, weights_in)

            @block.tensor
            def _(pe):
                def up(c, s, e):
                    for m in range(2):
                        n = 0
                        for k in range(KC):
                            o = (m * KC + k) * 128
                            for pw, px in PARTS:
                                last = pe.matmul(PS[2 * e + m][:, 0:HALF], w[:, s, pw, o:o + 128],
                                                 xs[:, px, k, HALF * e:HALF * e + HALF],
                                                 start=n == 0, stop=n == 3 * KC - 1)
                                n += 1
                    last.then_inc(gu_ready, 1)

                def down(c, s, e, start, stop):
                    if e == 0:
                        pe.wait_ge(d_split, c + 1)
                    pe.wait_ge(h_split, 2 * c + e + 1)
                    for d in range(KC):
                        o = GU + 128 * d
                        for n, (pw, ph) in enumerate(PARTS):
                            last = pe.matmul(PS[4 + 2 * d + e][:, 0:HALF], w[:, s, pw, o:o + 128], h[:, s, ph, e, :],
                                             start=start and n == 0, stop=stop and n == 2)
                    if e == 1:
                        last.then_inc(d_done, 1)

                def chunk(i, s, first, more):
                    c = 2 * i + s
                    pe.wait_ge(gu_split, c + 1)
                    for e in range(2):
                        if not first:
                            pe.wait_ge(h_made, 2 * (c - 1) + e + 1)
                        up(c, s, e)
                        if not first:
                            down(c - 1, 1 - s, e, isinstance(i, int) and c == 1, False)

                pe.wait_ge(x_split, 1)
                emit(pe, chunk)
                for e in range(2):
                    down(chunks - 1, (chunks - 1) % 2, e, False, True)
                for t in range(NT):
                    if t == 0:
                        pe.wait_ge(o_copied, 2 * KC)
                    if t >= 4:
                        pe.wait_ge(x_done, t - 3)
                    for d in range(KC):
                        last = pe.transpose(PS[t % 4][:, 128 * d:128 * d + 128], oT[:, d, 128 * t:128 * t + 128],
                                            ident[:, :])
                    last.then_inc(tr_ready, 1)

            @block.scalar
            def _(act):
                def gu_part(i, s):
                    act.wait_ge(w_in[s], i * 16 + 16)
                    act.activation(w[:, s, 0, 0:GU], raw[:, s, 0:GU], ACT.Copy).then_inc(gu_high, 1)

                def d_part(i, s):
                    act.activation(w[:, s, 0, GU:], raw[:, s, GU:], ACT.Copy).then_inc(d_high, 1)

                def chunk(i, s, first, more):
                    c = 2 * i + s
                    for e in range(2):
                        n = 2 * c + e
                        act.wait_ge(gu_ready, n + 1)
                        act.activation(sg[:, e, :], PS[2 * e][:, 0:HALF], ACT.Silu).then_inc(silu_done, 1)
                        if more and e == 0:
                            gu_part(*following(i, s))
                        if more and e == 1:
                            if not first:
                                act.wait_ge(d_done, c)
                            d_part(*following(i, s))
                        act.wait_ge(h_made, n + 1)
                        act.activation(h[:, s, 0, e, :], hf[:, e, :], ACT.Copy).then_inc(h_high, 1)

                gu_part(0, 0)
                act.activation(xs[:, 0], xT[:, :, :], ACT.Copy).then_inc(x_high, 1)
                d_part(0, 0)
                emit(act, chunk)
                act.wait_ge(d_done, chunks)
                for e in range(2):
                    act.activation(oT[:, 0, HALF * e:HALF * e + HALF], PS[4 + e][:, 0:HALF],
                                   ACT.Copy).then_inc(o_copied, 1)

            @block.gpsimd
            def _(pool):
                def chunk(i, s, first, more):
                    pool.wait_ge(cb_in[s], i * 16 + 16)
                    for e in range(2):
                        n = 2 * (2 * i + s) + e
                        pool.wait_ge(silu_done, n + 1)
                        pool.tensor_tensor(sc[:, e, :], sg[:, e, :], cb[:, s, HALF * e:HALF * e + HALF],
                                           ALU.mult).then_inc(comb_done, 1)

                emit(pool, chunk)

            @block.vector
            def _(dve):
                def gu_part(c, s):
                    dve.wait_ge(gu_high, c + 1)
                    dve.tensor_tensor(w[:, s, 1, 0:GU], raw[:, s, 0:GU], w[:, s, 0, 0:GU].bitcast(FP32),
                                      ALU.subtract).then_inc(gu_split, 1)

                def d_part(c, s):
                    dve.wait_ge(d_high, c + 1)
                    dve.tensor_tensor(w[:, s, 1, GU:], raw[:, s, GU:], w[:, s, 0, GU:].bitcast(FP32),
                                      ALU.subtract).then_inc(d_split, 1)

                def chunk(i, s, first, more):
                    c = 2 * i + s
                    for e in range(2):
                        n = 2 * c + e
                        dve.wait_ge(comb_done, n + 1)
                        dve.tensor_tensor(hf[:, e, :], PS[2 * e + 1][:, 0:HALF], sc[:, e, :],
                                          ALU.mult).then_inc(h_made, 1)
                        if more:
                            (gu_part if e == 0 else d_part)(c + 1, 1 - s)
                        dve.wait_ge(h_high, n + 1)
                        dve.tensor_tensor(h[:, s, 1, e, :], hf[:, e, :], h[:, s, 0, e, :].bitcast(FP32),
                                          ALU.subtract).then_inc(h_split, 1)

                gu_part(0, 0)
                dve.wait_ge(x_high, 1)
                dve.tensor_tensor(xs[:, 1], xT[:, :, :], xs[:, 0].bitcast(FP32), ALU.subtract).then_inc(x_split, 1)
                d_part(0, 0)
                emit(dve, chunk)
                dve.wait_ge(d_done, chunks)
                for e in range(2):
                    dve.tensor_copy(oT[:, 1, HALF * e:HALF * e + HALF], PS[6 + e][:, 0:HALF]).then_inc(o_copied, 1)
                for t in range(NT):
                    dve.wait_ge(tr_ready, t + 1)
                    dve.scalar_tensor_tensor(x[:, t, :], PS[t % 4][:, 0:H], G["tanh"][:, 4 + l:5 + l], x[:, t, :],
                                             ALU.mult, ALU.add).then_inc(x_done, 1)


def quantised_linear(nc, G, W):
    PS, xT, x = G["PS"], G["xT"], G["x"]
    with Stage(nc, "fp8") as st:
        w8, wi, wm = st.sb("w8", [128, KC, H], U8), st.sb("wi", [128, KC, H], I32), st.sb("wm", [128, KC, H], I32)
        wv, w2, wb = st.sb("wv", [128, KC, H]), st.sb("w2", [128, KC, H]), st.sb("wb", [128, KC, H], BF16)
        s16, sf, ws = st.sb("s16", [128, 1], BF16), st.sb("sf", [128, 1]), st.sb("ws", [128, 1])
        rs, sw = st.sb("rs", [128, 1]), st.sb("sw", [128, 1])
        y, step, q = st.sb("y", [128, KC, T]), st.sb("step", [128, KC, T]), st.sb("q", [128, KC, T], BF16)
        weights_in, in_w, chain, w_ready, q_ready, o_ready, x_done = (
            st.sem(n) for n in ("weights_in", "in_w", "chain", "w_ready", "q_ready", "o_ready", "x_done"))
        with nc.Block() as block:

            @block.sync
            def _(sp):
                Stage.semaphores.clear_earlier(sp)
                sp.dma_start(w8[:, :, :], G["L1_w8"]).then_inc(in_w, 16)
                sp.dma_start(s16[:, :], G["L1_in_scale"].broadcast_to([128, 1])).then_inc(in_w, 16)
                sp.dma_start(ws[:, :], G["L1_w_scale"].broadcast_to([128, 1])).then_inc(in_w, 16)
                W.load(sp, weights_in)
                W.wait(sp, weights_in)

            @block.vector
            def _(dve):
                c = Count(dve, chain)
                dve.wait_ge(in_w, 48)
                c.link(dve.tensor_copy(sf[:, :], s16[:, :]))
                c.link(dve.reciprocal(rs[:, :], sf[:, :]))
                c.link(dve.tensor_tensor(sw[:, :], sf[:, :], ws[:, :], ALU.mult))
                c.link(dve.tensor_tensor(sw[:, :], sw[:, :], G["tanh"][:, 5:6], ALU.mult))
                c.link(dve.tensor_scalar(y[:, :, :], xT[:, :, :], rs[:, :], FP8_MAX, ALU.mult, ALU.min))
                c.link(dve.tensor_scalar(y[:, :, :], y[:, :, :], -FP8_MAX, None, ALU.max))
                c.link(dve.tensor_scalar(step[:, :, :].bitcast(I32), y[:, :, :].bitcast(I32), 0x7F800000, None,
                                         ALU.bitwise_and))
                c.link(dve.tensor_scalar(step[:, :, :], step[:, :, :], 2.0 ** -6, 1.5 * 2.0 ** 20, ALU.max, ALU.mult))
                c.link(dve.tensor_tensor(y[:, :, :], y[:, :, :], step[:, :, :], ALU.add))
                dve.tensor_tensor(q[:, :, :], y[:, :, :], step[:, :, :], ALU.subtract).then_inc(q_ready, 1)
                c.link(dve.tensor_copy(wi[:, :, :], w8[:, :, :]))
                c.link(dve.tensor_scalar(wm[:, :, :], wi[:, :, :], 0x7F, 20, ALU.bitwise_and, ALU.logical_shift_left))
                c.link(dve.tensor_scalar(wm[:, :, :], wm[:, :, :], 0x40000000, None, ALU.bitwise_or))
                c.link(dve.tensor_scalar(wv[:, :, :], wm[:, :, :].bitcast(FP32), 2.0 ** -8, None, ALU.mult))
                c.link(dve.tensor_scalar(w2[:, :, :], wv[:, :, :], 2.0, -2.0 ** -6, ALU.mult, ALU.add))
                c.link(dve.tensor_tensor(wv[:, :, :], wv[:, :, :], w2[:, :, :], ALU.min))
                c.link(dve.tensor_scalar(wi[:, :, :], wi[:, :, :], 0x80, None, ALU.bitwise_and))
                c.link(dve.tensor_scalar(w2[:, :, :], wi[:, :, :], -1.0 / 64, 1.0, ALU.mult, ALU.add))
                dve.tensor_tensor(wb[:, :, :], wv[:, :, :], w2[:, :, :], ALU.mult).then_inc(w_ready, 1)
                for t in range(NT):
                    dve.wait_ge(o_ready, t + 1)
                    dve.scalar_tensor_tensor(x[:, t, :], PS[t][:, 0:H], sw[:, :], x[:, t, :],
                                             ALU.mult, ALU.add).then_inc(x_done, 1)

            @block.tensor
            def _(pe):
                pe.wait_ge(q_ready, 1)
                pe.wait_ge(w_ready, 1)
                for t in range(NT):
                    for k in range(KC):
                        last = pe.matmul(PS[t][:, 0:H], q[:, k, 128 * t:128 * t + 128], wb[:, k, :],
                                         start=k == 0, stop=k == KC - 1)
                    last.then_inc(o_ready, 1)


class Banks:

    def __init__(self, tensor):
        self.all = tensor[:, :]

    def __getitem__(self, i):
        return self.all[:, 512 * i:512 * i + 512]


MOE = {
    0: (16, 4, "softmax", 19, 176),
    2: (8, 1, "sigmoid", 8, 512),
    3: (16, 4, "renormalised", 16, 224),
}
CHUNKS = {0: 25, 2: 32, 3: 28}


def program(nc, G, out):
    with ExitStack() as stack:
        def sb(name, shape, dt=FP32):
            return stack.enter_context(nc.sbuf_tensor(name, shape, dt))

        G["comb"] = nc.dram_tensor("comb_rows", [19 * 11, T], FP32, kind="Internal").ap()
        G["kvt_hi"] = nc.dram_tensor("kvt_hi", [B * D, L], FP32, kind="Internal").ap()
        G["kvt_lo"] = nc.dram_tensor("kvt_lo", [B * D, L], FP32, kind="Internal").ap()
        G["kvn"] = nc.dram_tensor("kvn", [B, KP, NC * 2 * D], FP32, kind="Internal").ap()
        G["q"] = nc.dram_tensor("q_rows", [B, 128, NH * S], FP32, kind="Internal").ap()
        G["x"], G["xT"] = sb("x", [128, NT, H]), sb("xT", [128, KC, T])
        G["ident"], G["gate"], G["tanh"] = sb("ident", [128, 128]), sb("gate", [128, 8]), sb("tanh", [128, 8])
        G["PS"] = Banks(stack.enter_context(nc.psum_tensor("banks", [128, 8 * 512], FP32)))

        Stage.semaphores = Semaphores(nc, stack)
        for l in range(4):
            attention(nc, G, l)
        feed_forward(nc, G, 3, None)
        with Stage(nc, "store") as st:
            stored = st.sem("stored")
            with nc.Block() as block:

                @block.sync
                def _(sp):
                    Stage.semaphores.clear_earlier(sp)
                    sp.dma_start(out, G["x"][:, :, :]).then_inc(stored, 16)
                    sp.wait_ge(stored, 16)


def feed_forward(nc, G, l, W):
    normalise(nc, G, f"normf{l}")
    if l == 1:
        quantised_linear(nc, G, W)
    else:
        E, top, kind, rows, width = MOE[l]
        group_rows = np.gcd(width, 128).item()
        route(nc, G, l, E, top, kind, rows, width // group_rows)
        experts(nc, G, l, CHUNKS[l], group_rows, W)


def attention(nc, G, l):
    with Stage(nc, f"keep{l}") as keep:
        Bm = keep.sb("B", [128, NP, H])
        if l == 0:
            G["k0"], G["v0"] = keep.sb("k0", [128, 2, T], F32R), keep.sb("v0", [S, B, D])
            load_inputs(nc, G)
        with Stage(nc, f"mats{l}") as st:
            if l == 2:
                Q, N = st.sb("Q", [128, 2, NH, KC, CQ], F32R), st.sb("N", [CQH, 2, NH, D])
            else:
                A = st.sb("A", [128, KC, NH, D])
            with Stage(nc, f"weights{l}") as weights:
                W = FoldWeights(G, weights, l)
                if l:
                    feed_forward(nc, G, l - 1, W)
                normalise(nc, G, f"norma{l}", None if l else W)
                if l == 0:
                    fold_small(nc, G, W, A, Bm)
                elif l == 2:
                    fold_latent(nc, G, l, W, None, Bm, Q, N)
                else:
                    fold_latent(nc, G, l, W, A, Bm)
            q_all = st.sb("q", [128, B, NH, S], F32R)
            if l == 2:
                rotated_queries(nc, G, Q, N, q_all)
            else:
                queries(nc, G, l, A, q_all)
        with Stage(nc, f"ctx{l}") as st:
            ctxT = st.sb("ctxT", [128, NP, T])
            if l:
                attend_long(nc, G, l, G["q"], ctxT)
            else:
                attend_short(nc, G, G["q"], ctxT)
            project_out(nc, G, l, Bm, ctxT)


def rope_tables(length, dim):
    inv = (1.0 / np.float32(10000.0) ** (np.arange(0, dim, 2, dtype=np.float32) / np.float32(dim))).astype(np.float32)
    f = np.arange(length, dtype=np.float32)[:, None] * inv[None, :]
    cos, sin = np.repeat(np.cos(f), 2, axis=-1), np.repeat(np.sin(f), 2, axis=-1)
    sign = np.where(np.arange(dim) < dim // 2, -1.0, 1.0).astype(np.float32)
    return cos, sin * sign


def laid_out(i):
    c = np.ascontiguousarray
    ctx = i["ctx_512"]
    swapped = np.concatenate([ctx[..., D // 2:], ctx[..., :D // 2]], axis=-1)

    def by_width(a):
        return c(a.transpose(0, 2, 1).reshape(B * D, L))

    def by_key(a):
        return c(a.reshape(B, NC, KP, D).transpose(0, 2, 1, 3).reshape(B, KP, NC * D))

    cos, sin = rope_tables(L, D)
    cosq, sinq = rope_tables(S, CQ)
    a = {
        "x_in": c(i["x"].reshape(NT, 128, H).transpose(1, 0, 2)),
        "ctxT": by_width(ctx), "ctxTs": by_width(swapped), "ctxN": by_key(ctx),
        "cosT": c(np.tile(cos.T, (2, 1))), "sinT": c(np.tile(sin.T, (2, 1))),
        "cosN": by_key(np.broadcast_to(cos, (B, L, D)))[0], "sinN": by_key(np.broadcast_to(np.roll(sin, D // 2, axis=1), (B, L, D)))[0],
        "cosQ": c(cosq.T.reshape(2, CQH, S).transpose(1, 0, 2)), "sinQ": c(sinq.T.reshape(2, CQH, S).transpose(1, 0, 2)),
        "ctx0T": c(ctx[:, :S].transpose(2, 0, 1).reshape(D, T)), "ctx0N": c(ctx[:, :S].transpose(1, 0, 2)),
        "ident_in": np.eye(128, dtype=np.float32),
        "g_xattn": c(i["g_xattn"].reshape(1, 4)), "g_ffn": c(i["g_ffn"].reshape(1, 4)),
    }
    row = np.arange(NH * S).reshape(NT, 128).T % S
    a["mask0"] = np.where(np.arange(S) <= row[:, :, None], 0.0, np.finfo(np.float32).min).astype(np.float32)
    for E in (8, 16):
        a[f"tie{E}"] = c(np.broadcast_to((np.arange(E)[None, :] < np.arange(E)[:, None]).astype(np.float32)
                                         .reshape(1, E * E), (128, E * E)))
    HD = H // NH
    wkv = i["L0_xattn_Wkv_expand"]
    a["L0_wq"] = c(i["L0_xattn_Wq"].reshape(NH, HD, H).transpose(1, 0, 2))
    a["L0_wk"] = c(wkv[:H].reshape(NH, HD, D).transpose(1, 0, 2))
    a["L0_wv"] = c(wkv[H:].reshape(NH, HD, D).transpose(1, 0, 2))
    a["L0_wo"] = c(i["L0_xattn_Wout"].T.reshape(NH, HD, H).transpose(1, 0, 2))
    for l in (1, 2, 3):
        w = {n: i[f"L{l}_xattn_{n}"] for n in ("Wq", "w_kc_q", "w_kc_kv", "W_qr", "W_kr", "Wo")}
        a[f"L{l}_wq"] = c(w["Wq"].reshape(NH, K, H).transpose(1, 0, 2))
        a[f"L{l}_wqr"] = c(w["W_qr"].transpose(2, 0, 1))
        a[f"L{l}_wkr"] = c(w["W_kr"].transpose(2, 0, 1))
        a[f"L{l}_wv"] = c(w["w_kc_kv"].transpose(1, 0, 2))
        a[f"L{l}_wo"] = c(w["Wo"].T.reshape(NH, K, H).transpose(1, 0, 2))
        if l == 2:
            a["L2_wc"] = c(w["w_kc_q"].transpose(1, 0, 2))
        else:
            a[f"L{l}_wc"] = c(w["w_kc_q"].reshape(NH, K, 2, CQH).transpose(3, 2, 0, 1))

    def expert_chunks(gate, up, down, chunks):
        pad = [(0, chunks * 128 - gate.shape[0]), (0, 0)]
        gate, up, down = (np.pad(m, pad) for m in (gate, up, down))
        def stationary(m):
            return m.reshape(chunks, 128, KC, 128).transpose(0, 3, 2, 1).reshape(chunks * 128, KC * 128)
        return c(np.concatenate([stationary(gate), stationary(up), down], axis=1))

    a["L0_experts"] = expert_chunks(
        np.concatenate([i["L0_ffn_W1"].reshape(-1, H), i["L0_ffn_W1s"]]),
        np.concatenate([i["L0_ffn_W3"].reshape(-1, H), i["L0_ffn_W3s"]]),
        np.concatenate([i["L0_ffn_W2"].transpose(0, 2, 1).reshape(-1, H), i["L0_ffn_W2s"].T]), CHUNKS[0])
    for l, (g, u, d) in {2: ("gate_w", "up_w", "down_w"), 3: ("gate_proj", "up_proj", "down_proj")}.items():
        a[f"L{l}_experts"] = expert_chunks(i[f"L{l}_ffn_{g}"].transpose(0, 2, 1).reshape(-1, H),
                                           i[f"L{l}_ffn_{u}"].transpose(0, 2, 1).reshape(-1, H),
                                           i[f"L{l}_ffn_{d}"].reshape(-1, H), CHUNKS[l])

    def router(w):
        return c(w.reshape(KC, 128, -1).transpose(1, 0, 2))

    a["L0_router"], a["L2_router"] = router(i["L0_ffn_Wg"].T), router(i["L2_ffn_router_w"])
    a["L3_router"], a["L3_bias"] = router(i["L3_ffn_router_w"].T), c(i["L3_ffn_expert_bias"].reshape(1, -1))
    a["L1_w8"] = c(i["L1_ffn_weight"].view(np.uint8).T.reshape(KC, 128, H).transpose(1, 0, 2))
    a["L1_in_scale"] = c(i["L1_ffn_input_scale"].reshape(1, 1))
    a["L1_w_scale"] = c(i["L1_ffn_weight_scale"].reshape(1, 1))
    return a


def kernel(**inputs):
    import concourse.bacc as bacc
    from concourse.bass_utils import run_bass_kernel_spmd

    nc = bacc.Bacc("TRN2", target_bir_lowering=False, num_devices=1)
    arrays, G = {}, {}
    for name, a in laid_out({k: np.asarray(v) for k, v in inputs.items()}).items():
        arrays[f"{name}_dram"] = a
        G[name] = nc.dram_tensor(f"{name}_dram", a.shape, mybir.dt.from_np(a.dtype), kind="ExternalInput").ap()
    out = nc.dram_tensor("out_dram", (128, NT, H), FP32, kind="ExternalOutput").ap()
    program(nc, G, out)
    r = run_bass_kernel_spmd(nc, [arrays], core_ids=[0])
    return np.ascontiguousarray(r.results[0]["out_dram"].transpose(1, 0, 2)).reshape(B, S, H)
```
